# Optimizing a Trainium2 kernel written in Bass

```python
import numpy as np
import jax
import jax.numpy as jnp

def _softmax(x, axis=-1):
    return jax.nn.softmax(x, axis=axis)

def _gelu(x):
    return jax.nn.gelu(x, approximate=True)

def _silu(x):
    return jax.nn.silu(x)

def _sigmoid(x):
    return jax.nn.sigmoid(x)

def _layernorm(x, axis=-1, eps=1e-05):
    m = jnp.mean(x, axis=axis, keepdims=True)
    v = jnp.var(x, axis=axis, keepdims=True)
    return (x - m) / jnp.sqrt(v + eps)

def _scatter_add(tgt, idx, src, axis=0):
    return tgt.at[idx].add(src)

def _segment_sum(src, seg, n):
    return jax.ops.segment_sum(src, seg, n)
kernel_name = 'mk_gps_d4_gnn_r16_d9aa47'

def setup_inputs(seed: int=0):
    np.random.seed(seed)
    _w = jnp.asarray

    def _rec_inputs():
        import jax
        import jax.numpy as jnp
        _gk = jax.random.key(seed)
        x = -0.0003713 + 1 * jax.random.normal(jax.random.fold_in(_gk, 1), (3125, 256), jnp.float32)
        src = jax.random.randint(jax.random.fold_in(_gk, 2), (100000,), 0, 3125, jnp.int32)
        dst = jnp.minimum((3125 * jax.random.uniform(jax.random.fold_in(_gk, 3), (100000,)) ** 2.0).astype(jnp.int32), 49999)
        _o = jnp.argsort(dst, stable=True)
        src = src[_o]
        dst = dst[_o]
        edge_attr_2 = jax.random.uniform(jax.random.fold_in(_gk, 12), (100000, 2), jnp.float32, 0.0, 1)
        return (x, src, dst, edge_attr_2)
    x, src, dst, edge_attr_2 = _rec_inputs()

    def _L0_gnn_setup():
        import jax, jax.numpy as jnp
        import numpy as np
        N, E = (3125, 50000)
        IN_DIM = 256
        OUT_DIM = 256
        H = 8
        D = OUT_DIM // H
        SCALE = D ** (-0.5)
        LN_EPS = 1e-05

        def _layernorm(x, g, b):
            mu = jnp.mean(x, axis=-1, keepdims=True)
            var = jnp.mean((x - mu) ** 2, axis=-1, keepdims=True)
            return (x - mu) * jax.lax.rsqrt(var + LN_EPS) * g + b
        key = jax.random.key(seed)
        ks = jax.random.split(key, 12)
        s = 1.0 / np.sqrt(IN_DIM)
        inp = {'x': jax.random.normal(ks[0], (N, IN_DIM), jnp.float32), 'edge_index': jax.random.randint(ks[1], (2, E), 0, N, jnp.int64), 'batch': jnp.zeros((N,), jnp.int64), 'Wq': jax.random.uniform(ks[2], (IN_DIM, OUT_DIM), jnp.float32, -s, s), 'Wk': jax.random.uniform(ks[3], (IN_DIM, OUT_DIM), jnp.float32, -s, s), 'Wv': jax.random.uniform(ks[4], (IN_DIM, OUT_DIM), jnp.float32, -s, s), 'Wo_w': jax.random.uniform(ks[5], (OUT_DIM, OUT_DIM), jnp.float32, -s, s), 'Wo_b': jnp.zeros((OUT_DIM,), jnp.float32), 'ln1_g': jnp.ones((OUT_DIM,), jnp.float32), 'ln1_b': jnp.zeros((OUT_DIM,), jnp.float32), 'ln2_g': jnp.ones((OUT_DIM,), jnp.float32), 'ln2_b': jnp.zeros((OUT_DIM,), jnp.float32), 'ffn_w1': jax.random.uniform(ks[6], (OUT_DIM, 2 * OUT_DIM), jnp.float32, -s, s), 'ffn_b1': jnp.zeros((2 * OUT_DIM,), jnp.float32), 'ffn_w2': jax.random.uniform(ks[7], (2 * OUT_DIM, OUT_DIM), jnp.float32, -s, s), 'ffn_b2': jnp.zeros((OUT_DIM,), jnp.float32)}
        return inp
    _L0_gnn_all = _L0_gnn_setup()
    _L0_gnn_in = {k: v for k, v in _L0_gnn_all.items() if k in ('Wq', 'Wk', 'Wv', 'Wo_w', 'Wo_b', 'ln1_g', 'ln1_b', 'ln2_g', 'ln2_b', 'ffn_w1', 'ffn_b1', 'ffn_w2', 'ffn_b2')}
    del _L0_gnn_all

    def _L0_mix_setup():
        import jax, jax.numpy as jnp
        import numpy as np
        import math
        EMBED = 256
        HEADS = 4
        HEAD_DIM = EMBED // HEADS
        OUT_DIM = 256
        LN_EPS = 1e-05

        def _qkv_init(key):
            spread = math.sqrt(3.0 / EMBED)
            gain, delta = (0.01, 0.01)
            w = jax.random.uniform(key, (EMBED, EMBED), minval=-spread, maxval=spread) * gain
            return w + delta * jnp.eye(EMBED, dtype=w.dtype)

        def _layer_norm(x, g, b):
            mu = jnp.mean(x, axis=-1, keepdims=True)
            var = jnp.mean(jnp.square(x - mu), axis=-1, keepdims=True)
            return (x - mu) * jax.lax.rsqrt(var + LN_EPS) * g + b

        def _split_heads(x, B, S):
            return x.reshape(B, S, HEADS, HEAD_DIM).transpose(0, 2, 1, 3)
        key = jax.random.key(seed)
        ks = jax.random.split(key, 6)
        seq = jax.random.normal(ks[0], (4, 512, EMBED), dtype=jnp.float32)
        wq = _qkv_init(ks[1])
        wk = _qkv_init(ks[2])
        wv = _qkv_init(ks[3])
        bound = 1.0 / math.sqrt(EMBED)
        wo = jax.random.uniform(ks[4], (OUT_DIM, EMBED), minval=-bound, maxval=bound)
        bo = jax.random.uniform(ks[5], (OUT_DIM,), minval=-bound, maxval=bound)
        ln_k_g = jnp.ones((HEAD_DIM,), jnp.float32)
        ln_k_b = jnp.zeros((HEAD_DIM,), jnp.float32)
        ln_v_g = jnp.ones((HEAD_DIM,), jnp.float32)
        ln_v_b = jnp.zeros((HEAD_DIM,), jnp.float32)
        return {'seq': seq, 'wq': wq, 'wk': wk, 'wv': wv, 'wo': wo, 'bo': bo, 'ln_k_g': ln_k_g, 'ln_k_b': ln_k_b, 'ln_v_g': ln_v_g, 'ln_v_b': ln_v_b}
    _L0_mix_all = _L0_mix_setup()
    _L0_mix_in = {k: v for k, v in _L0_mix_all.items() if k in ('wq', 'wk', 'wv', 'wo', 'bo', 'ln_k_g', 'ln_k_b', 'ln_v_g', 'ln_v_b')}
    del _L0_mix_all

    def _L0_ffn_setup():
        import jax, jax.numpy as jnp
        import numpy as np
        B, N, D = (16, 256, 256)
        NUM_EXPERTS, TOP_K, HEADS = (4, 2, 4)
        N_EDGES = 65536
        LN_EPS = 1e-05

        def _layernorm(x, g, b):
            mu = x.mean(-1, keepdims=True)
            var = ((x - mu) ** 2).mean(-1, keepdims=True)
            return (x - mu) * jax.lax.rsqrt(var + LN_EPS) * g + b

        def _forward(x, edge_index, W_gat, att_src, att_dst, b_gat, ln_gamma, ln_beta, W1, b1, W2, b2):
            Bc, Nc, Dc = x.shape
            M = Bc * Nc
            x_flat = x.reshape(M, Dc)
            h = (x_flat @ W_gat).reshape(M, HEADS, NUM_EXPERTS)
            loops = jnp.arange(M, dtype=edge_index.dtype)
            src = jnp.concatenate([edge_index[0], loops])
            dst = jnp.concatenate([edge_index[1], loops])
            a_src = (h * att_src).sum(-1)
            a_dst = (h * att_dst).sum(-1)
            e = jax.nn.leaky_relu(a_src[src] + a_dst[dst], negative_slope=0.2)
            e_max = jax.ops.segment_max(e, dst, num_segments=M)
            ee = jnp.exp(e - e_max[dst])
            denom = jax.ops.segment_sum(ee, dst, num_segments=M)
            alpha = ee / (denom[dst] + 1e-16)
            msg = h[src] * alpha[:, :, None]
            agg = jax.ops.segment_sum(msg, dst, num_segments=M).reshape(M, HEADS * NUM_EXPERTS) + b_gat
            scores = _layernorm(agg, ln_gamma, ln_beta).reshape(M, HEADS, NUM_EXPERTS).mean(1)
            scores = scores.reshape(Bc, Nc, NUM_EXPERTS)
            topk_s, topk_i = jax.lax.top_k(scores, TOP_K)
            w = jax.nn.softmax(topk_s, axis=-1)
            out = jnp.zeros_like(x)
            for ei in range(NUM_EXPERTS):
                g = jnp.where(topk_i == ei, w, 0.0).sum(-1)
                hh = jax.nn.gelu(x @ W1[ei] + b1[ei], approximate=False)
                out = out + g[..., None] * (hh @ W2[ei] + b2[ei])
            return out
        key = jax.random.key(seed)
        ks = jax.random.split(key, 8)
        s = 0.05
        return {'x': jax.random.normal(ks[0], (B, N, D), jnp.float32), 'W_gat': jax.random.normal(ks[1], (D, HEADS * NUM_EXPERTS), jnp.float32) * s, 'att_src': jax.random.normal(ks[2], (HEADS, NUM_EXPERTS), jnp.float32) * s, 'att_dst': jax.random.normal(ks[3], (HEADS, NUM_EXPERTS), jnp.float32) * s, 'b_gat': jnp.zeros((HEADS * NUM_EXPERTS,), jnp.float32), 'ln_gamma': jnp.ones((HEADS * NUM_EXPERTS,), jnp.float32), 'ln_beta': jnp.zeros((HEADS * NUM_EXPERTS,), jnp.float32), 'W1': jax.random.normal(ks[4], (NUM_EXPERTS, D, 2 * D), jnp.float32) * s, 'b1': jnp.zeros((NUM_EXPERTS, 2 * D), jnp.float32), 'W2': jax.random.normal(ks[5], (NUM_EXPERTS, 2 * D, D), jnp.float32) * s, 'b2': jnp.zeros((NUM_EXPERTS, D), jnp.float32), 'edge_index': jax.random.randint(ks[6], (2, N_EDGES), 0, B * N, jnp.int32)}
    _L0_ffn_all = _L0_ffn_setup()
    _L0_ffn_in = {k: v for k, v in _L0_ffn_all.items() if k in ('W_gat', 'att_src', 'att_dst', 'b_gat', 'ln_gamma', 'ln_beta', 'W1', 'b1', 'W2', 'b2', 'edge_index')}
    del _L0_ffn_all

    def _L1_gnn_setup():
        import jax, jax.numpy as jnp
        import numpy as np
        N_NODES = 3125
        N_EDGES = 50000
        D_IN = 256
        D_OUT = 256
        key = jax.random.key(seed)
        k1, k2, k3, k4 = jax.random.split(key, 4)
        x = jax.random.normal(k1, (N_NODES, D_IN), dtype=jnp.float32)
        edge_index = jax.random.randint(k2, (2, N_EDGES), 0, N_NODES, dtype=jnp.int64)
        glorot = (6.0 / (D_IN + D_OUT)) ** 0.5
        W = jax.random.uniform(k3, (D_OUT, D_IN), minval=-glorot, maxval=glorot, dtype=jnp.float32)
        b = jnp.zeros((D_OUT,), dtype=jnp.float32)
        return {'x': x, 'edge_index': edge_index, 'W': W, 'b': b}
    _L1_gnn_all = _L1_gnn_setup()
    _L1_gnn_in = {k: v for k, v in _L1_gnn_all.items() if k in ('W', 'b')}
    del _L1_gnn_all

    def _L1_mix_setup():
        import jax, jax.numpy as jnp
        import numpy as np
        NHEAD = 8
        ATT_EPS = 1e-06
        LN_EPS = 1e-05

        def _layernorm(x, g, b):
            mu = jnp.mean(x, axis=-1, keepdims=True)
            var = jnp.mean(jnp.square(x - mu), axis=-1, keepdims=True)
            return (x - mu) * jax.lax.rsqrt(var + LN_EPS) * g + b
        key = jax.random.key(seed)
        ks = jax.random.split(key, 7)
        N, L, C = (4, 1024, 256)
        s = 1.0 / np.sqrt(C)
        return {'x': jax.random.normal(ks[0], (N, L, C), jnp.float32), 'Wq': jax.random.normal(ks[1], (C, C), jnp.float32) * s, 'Wk': jax.random.normal(ks[2], (C, C), jnp.float32) * s, 'Wv': jax.random.normal(ks[3], (C, C), jnp.float32) * s, 'Wm': jax.random.normal(ks[4], (C, C), jnp.float32) * s, 'W1': jax.random.normal(ks[5], (2 * C, 2 * C), jnp.float32) * (1.0 / np.sqrt(2 * C)), 'W2': jax.random.normal(ks[6], (2 * C, C), jnp.float32) * (1.0 / np.sqrt(2 * C)), 'g1': jnp.ones((C,), jnp.float32), 'b1': jnp.zeros((C,), jnp.float32), 'g2': jnp.ones((C,), jnp.float32), 'b2': jnp.zeros((C,), jnp.float32)}
    _L1_mix_all = _L1_mix_setup()
    _L1_mix_in = {k: v for k, v in _L1_mix_all.items() if k in ('Wq', 'Wk', 'Wv', 'Wm', 'W1', 'W2', 'g1', 'b1', 'g2', 'b2')}
    del _L1_mix_all

    def _L1_ffn_setup():
        import jax, jax.numpy as jnp
        import numpy as np
        B, A = (256, 8)
        IN, OUT = (256, 256)
        SH1, SH2 = (256, 128)
        EH1, EH2 = (128, 64)
        E, TOPK = (4, 2)

        def _shared_mlp(x, W1, b1, W2, b2, W3, b3):
            h = jax.nn.relu(x @ W1 + b1)
            h = jax.nn.relu(h @ W2 + b2)
            return h @ W3 + b3

        def _experts_mlp(x, eW1, eb1, eW2, eb2, eW3, eb3):
            h = jax.nn.relu(jnp.einsum('baf,efh->ebah', x, eW1) + eb1[:, None, None, :])
            h = jax.nn.relu(jnp.einsum('ebah,ehg->ebag', h, eW2) + eb2[:, None, None, :])
            o = jnp.einsum('ebag,ego->ebao', h, eW3) + eb3[:, None, None, :]
            return jnp.moveaxis(o, 0, -1)
        key = jax.random.key(seed)
        ks = jax.random.split(key, 16)
        s = 0.05
        return {'x': jax.random.normal(ks[0], (B, A, IN), jnp.float32), 'sW1': jax.random.normal(ks[1], (IN, SH1), jnp.float32) * s, 'sb1': jnp.zeros((SH1,), jnp.float32), 'sW2': jax.random.normal(ks[2], (SH1, SH2), jnp.float32) * s, 'sb2': jnp.zeros((SH2,), jnp.float32), 'sW3': jax.random.normal(ks[3], (SH2, OUT), jnp.float32) * s, 'sb3': jnp.zeros((OUT,), jnp.float32), 'eW1': jax.random.normal(ks[4], (E, IN, EH1), jnp.float32) * s, 'eb1': jnp.zeros((E, EH1), jnp.float32), 'eW2': jax.random.normal(ks[5], (E, EH1, EH2), jnp.float32) * s, 'eb2': jnp.zeros((E, EH2), jnp.float32), 'eW3': jax.random.normal(ks[6], (E, EH2, OUT), jnp.float32) * s, 'eb3': jnp.zeros((E, OUT), jnp.float32), 'gW': jax.random.normal(ks[7], (IN, E), jnp.float32) * s, 'gb': jnp.zeros((E,), jnp.float32)}
    _L1_ffn_all = _L1_ffn_setup()
    _L1_ffn_in = {k: v for k, v in _L1_ffn_all.items() if k in ('sW1', 'sb1', 'sW2', 'sb2', 'sW3', 'sb3', 'eW1', 'eb1', 'eW2', 'eb2', 'eW3', 'eb3', 'gW', 'gb')}
    del _L1_ffn_all

    def _L2_gnn_setup():
        import jax, jax.numpy as jnp
        import numpy as np
        N_NODES = 6250
        N_EDGES = 100000
        IN_FEATS = 256
        OUT_FEATS = 64
        NUM_HEADS = 4
        key = jax.random.key(seed)
        k_h, k_adj, k_dir, k_wf, k_wr, k_af = jax.random.split(key, 6)
        h = jax.random.normal(k_h, (N_NODES, IN_FEATS), dtype=jnp.float32)
        adj = jax.random.randint(k_adj, (2, N_EDGES), 0, N_NODES, dtype=jnp.int64)
        bit = jax.random.randint(k_dir, (N_EDGES,), 0, 2).astype(jnp.float32)
        direction = jnp.stack([bit, 1.0 - bit], axis=1)
        s_w = float(np.sqrt(6.0 / (IN_FEATS + OUT_FEATS)))
        s_a = float(np.sqrt(6.0 / (NUM_HEADS + OUT_FEATS)))
        W_forward = jax.random.uniform(k_wf, (OUT_FEATS, IN_FEATS), jnp.float32, -s_w, s_w)
        W_reverse = jax.random.uniform(k_wr, (OUT_FEATS, IN_FEATS), jnp.float32, -s_w, s_w)
        attn_forward = jax.random.uniform(k_af, (1, NUM_HEADS, OUT_FEATS), jnp.float32, -s_a, s_a)
        return {'h': h, 'adj': adj, 'direction': direction, 'W_forward': W_forward, 'W_reverse': W_reverse, 'attn_forward': attn_forward}
    _L2_gnn_all = _L2_gnn_setup()
    _L2_gnn_in = {k: v for k, v in _L2_gnn_all.items() if k in ('W_forward', 'W_reverse', 'attn_forward')}
    del _L2_gnn_all

    def _L2_mix_setup():
        import jax, jax.numpy as jnp
        import numpy as np
        DIM = 256
        HEADS = 4
        HEAD_DIM = DIM // HEADS
        MLP_HIDDEN = DIM * 3
        B, N = (8, 256)
        EPS = 1e-05

        def _layernorm(x, g, b):
            mu = jnp.mean(x, axis=-1, keepdims=True)
            var = jnp.mean(jnp.square(x - mu), axis=-1, keepdims=True)
            return (x - mu) * jax.lax.rsqrt(var + EPS) * g + b
        key = jax.random.key(seed)
        ks = jax.random.split(key, 8)
        s = 0.02
        return {'x': jax.random.normal(ks[0], (B, N, DIM), dtype=jnp.float32), 'w_qkv': jax.random.normal(ks[1], (DIM, 3 * DIM), dtype=jnp.float32) * s, 'b_qkv': jnp.zeros((3 * DIM,), dtype=jnp.float32), 'norm_g': jnp.ones((DIM,), dtype=jnp.float32), 'norm_b': jnp.zeros((DIM,), dtype=jnp.float32), 'w_fc1': jax.random.normal(ks[2], (DIM, MLP_HIDDEN), dtype=jnp.float32) * s, 'b_fc1': jnp.zeros((MLP_HIDDEN,), dtype=jnp.float32), 'w_fc2': jax.random.normal(ks[3], (MLP_HIDDEN, DIM), dtype=jnp.float32) * s, 'b_fc2': jnp.zeros((DIM,), dtype=jnp.float32)}
    _L2_mix_all = _L2_mix_setup()
    _L2_mix_in = {k: v for k, v in _L2_mix_all.items() if k in ('w_qkv', 'b_qkv', 'norm_g', 'norm_b', 'w_fc1', 'b_fc1', 'w_fc2', 'b_fc2')}
    del _L2_mix_all

    def _L2_ffn_setup():
        import jax, jax.numpy as jnp
        import numpy as np
        TOP_K = 2
        LN_EPS = 1e-05
        key = jax.random.key(seed)
        ks = jax.random.split(key, 8)
        B, S, D, E, H = (16, 1024, 256, 8, 1024)
        x = jax.random.normal(ks[0], (B, S, D), dtype=jnp.float32)
        Wr = jax.random.normal(ks[1], (D, E), dtype=jnp.float32) * 0.1
        br = jnp.zeros((E,), dtype=jnp.float32)
        ln_g = jnp.ones((E, D), dtype=jnp.float32)
        ln_b = jnp.zeros((E, D), dtype=jnp.float32)
        W1 = jax.random.normal(ks[2], (E, D, H), dtype=jnp.float32) * (1.0 / np.sqrt(D))
        b1 = jnp.zeros((E, H), dtype=jnp.float32)
        W2 = jax.random.normal(ks[3], (E, H, D), dtype=jnp.float32) * (1.0 / np.sqrt(H))
        b2 = jnp.zeros((E, D), dtype=jnp.float32)
        return {'x': x, 'Wr': Wr, 'br': br, 'ln_g': ln_g, 'ln_b': ln_b, 'W1': W1, 'b1': b1, 'W2': W2, 'b2': b2}
    _L2_ffn_all = _L2_ffn_setup()
    _L2_ffn_in = {k: v for k, v in _L2_ffn_all.items() if k in ('Wr', 'br', 'ln_g', 'ln_b', 'W1', 'b1', 'W2', 'b2')}
    del _L2_ffn_all

    def _L3_gnn_setup():
        import jax, jax.numpy as jnp
        import numpy as np
        N_NODES = 3125
        N_EDGES = 50000
        D_MODEL = 256
        NUM_HEADS = 8
        HEAD_DIM = D_MODEL // NUM_HEADS
        D_FF = 2 * D_MODEL
        NEG_SLOPE = 0.2
        BN_EPS = 1e-05

        def _batch_norm(h, g, b):
            mean = jnp.mean(h, axis=0)
            var = jnp.mean((h - mean) ** 2, axis=0)
            return (h - mean) * jax.lax.rsqrt(var + BN_EPS) * g + b
        key = jax.random.key(seed)
        ks = jax.random.split(key, 16)
        x = jax.random.normal(ks[0], (N_NODES, D_MODEL), dtype=jnp.float32)
        src = jax.random.randint(ks[1], (N_EDGES,), 0, N_NODES)
        off = jax.random.randint(ks[2], (N_EDGES,), 1, N_NODES)
        dst = (src + off) % N_NODES
        edge_index = jnp.stack([src, dst]).astype(jnp.int64)

        def lin(k, fi, fo):
            s = 1.0 / np.sqrt(fi)
            return jax.random.uniform(k, (fi, fo), jnp.float32, -s, s)
        inp = {'x': x, 'edge_index': edge_index, 'Wq': lin(ks[3], D_MODEL, D_MODEL), 'bq': jnp.zeros((D_MODEL,), jnp.float32), 'Wk': lin(ks[4], D_MODEL, D_MODEL), 'bk': jnp.zeros((D_MODEL,), jnp.float32), 'Wv': lin(ks[5], D_MODEL, D_MODEL), 'bv': jnp.zeros((D_MODEL,), jnp.float32), 'Wo': lin(ks[6], D_MODEL, D_MODEL), 'bo': jnp.zeros((D_MODEL,), jnp.float32), 'W1': lin(ks[7], D_MODEL, D_FF), 'b1': jnp.zeros((D_FF,), jnp.float32), 'W2': lin(ks[8], D_FF, D_MODEL), 'b2': jnp.zeros((D_MODEL,), jnp.float32), 'bn1_g': jnp.ones((D_MODEL,), jnp.float32), 'bn1_b': jnp.zeros((D_MODEL,), jnp.float32), 'bn2_g': jnp.ones((D_MODEL,), jnp.float32), 'bn2_b': jnp.zeros((D_MODEL,), jnp.float32)}
        return inp
    _L3_gnn_all = _L3_gnn_setup()
    _L3_gnn_in = {k: v for k, v in _L3_gnn_all.items() if k in ('Wq', 'bq', 'Wk', 'bk', 'Wv', 'bv', 'Wo', 'bo', 'W1', 'b1', 'W2', 'b2', 'bn1_g', 'bn1_b', 'bn2_g', 'bn2_b')}
    del _L3_gnn_all

    def _L3_mix_setup():
        import jax, jax.numpy as jnp
        import numpy as np
        DIM = 256
        HEADS = 4
        DIM_HEAD = 32
        NUM_MEM = 4
        HIDDEN = HEADS * DIM_HEAD
        SCALE = DIM_HEAD ** (-0.5)

        def rmsnorm(x, g):
            n = jnp.linalg.norm(x, axis=-1, keepdims=True)
            return x / jnp.maximum(n, 1e-12) * g * x.shape[-1] ** 0.5
        key = jax.random.key(seed)
        ks = jax.random.split(key, 8)
        B, N = (4, 1024)
        return {'x': jax.random.normal(ks[0], (B, N, DIM), jnp.float32), 't': jax.random.normal(ks[1], (B,), jnp.float32), 'w_qkv': jax.random.normal(ks[2], (DIM, 3 * HIDDEN), jnp.float32) * 0.02, 'mem_kv': jax.random.normal(ks[3], (2, HEADS, DIM_HEAD, NUM_MEM), jnp.float32), 'w_out': jax.random.normal(ks[4], (HIDDEN, DIM), jnp.float32) * 0.02, 'b_out': jnp.zeros((DIM,), jnp.float32), 'g_out': jnp.ones((DIM,), jnp.float32), 'g_pre': jnp.ones((DIM,), jnp.float32)}
    _L3_mix_all = _L3_mix_setup()
    _L3_mix_in = {k: v for k, v in _L3_mix_all.items() if k in ('t', 'w_qkv', 'mem_kv', 'w_out', 'b_out', 'g_out', 'g_pre')}
    del _L3_mix_all

    def _L3_ffn_setup():
        import jax, jax.numpy as jnp
        import numpy as np
        B, S, D = (8, 256, 256)
        H = 4 * D
        CAPACITY = 0.5
        key = jax.random.key(seed)
        ks = jax.random.split(key, 6)
        x = jax.random.normal(ks[0], (B, S, D), dtype=jnp.float32)
        attention_mask = jnp.zeros((B, 1, 1, S), dtype=jnp.float32)
        wr = jax.random.normal(ks[1], (D, 1), dtype=jnp.float32) * 0.02
        br = jnp.zeros((1,), dtype=jnp.float32)
        w1 = jax.random.normal(ks[2], (D, H), dtype=jnp.float32) * 0.02
        b1 = jnp.zeros((H,), dtype=jnp.float32)
        w2 = jax.random.normal(ks[3], (H, D), dtype=jnp.float32) * 0.02
        b2 = jnp.zeros((D,), dtype=jnp.float32)
        return {'x': x, 'attention_mask': attention_mask, 'wr': wr, 'br': br, 'w1': w1, 'b1': b1, 'w2': w2, 'b2': b2}
    _L3_ffn_all = _L3_ffn_setup()
    _L3_ffn_in = {k: v for k, v in _L3_ffn_all.items() if k in ('attention_mask', 'wr', 'br', 'w1', 'b1', 'w2', 'b2')}
    del _L3_ffn_all
    return {'x': x, 'src': src, 'dst': dst, 'edge_attr_2': edge_attr_2, 'L0_gnn_Wq': _L0_gnn_in['Wq'], 'L0_gnn_Wk': _L0_gnn_in['Wk'], 'L0_gnn_Wv': _L0_gnn_in['Wv'], 'L0_gnn_Wo_w': _L0_gnn_in['Wo_w'], 'L0_gnn_Wo_b': _L0_gnn_in['Wo_b'], 'L0_gnn_ln1_g': _L0_gnn_in['ln1_g'], 'L0_gnn_ln1_b': _L0_gnn_in['ln1_b'], 'L0_gnn_ln2_g': _L0_gnn_in['ln2_g'], 'L0_gnn_ln2_b': _L0_gnn_in['ln2_b'], 'L0_gnn_ffn_w1': _L0_gnn_in['ffn_w1'], 'L0_gnn_ffn_b1': _L0_gnn_in['ffn_b1'], 'L0_gnn_ffn_w2': _L0_gnn_in['ffn_w2'], 'L0_gnn_ffn_b2': _L0_gnn_in['ffn_b2'], 'L0_mix_wq': _L0_mix_in['wq'], 'L0_mix_wk': _L0_mix_in['wk'], 'L0_mix_wv': _L0_mix_in['wv'], 'L0_mix_wo': _L0_mix_in['wo'], 'L0_mix_bo': _L0_mix_in['bo'], 'L0_mix_ln_k_g': _L0_mix_in['ln_k_g'], 'L0_mix_ln_k_b': _L0_mix_in['ln_k_b'], 'L0_mix_ln_v_g': _L0_mix_in['ln_v_g'], 'L0_mix_ln_v_b': _L0_mix_in['ln_v_b'], 'L0_ffn_W_gat': _L0_ffn_in['W_gat'], 'L0_ffn_att_src': _L0_ffn_in['att_src'], 'L0_ffn_att_dst': _L0_ffn_in['att_dst'], 'L0_ffn_b_gat': _L0_ffn_in['b_gat'], 'L0_ffn_ln_gamma': _L0_ffn_in['ln_gamma'], 'L0_ffn_ln_beta': _L0_ffn_in['ln_beta'], 'L0_ffn_W1': _L0_ffn_in['W1'], 'L0_ffn_b1': _L0_ffn_in['b1'], 'L0_ffn_W2': _L0_ffn_in['W2'], 'L0_ffn_b2': _L0_ffn_in['b2'], 'L0_ffn_edge_index': _L0_ffn_in['edge_index'], 'L1_gnn_W': _L1_gnn_in['W'], 'L1_gnn_b': _L1_gnn_in['b'], 'L1_mix_Wq': _L1_mix_in['Wq'], 'L1_mix_Wk': _L1_mix_in['Wk'], 'L1_mix_Wv': _L1_mix_in['Wv'], 'L1_mix_Wm': _L1_mix_in['Wm'], 'L1_mix_W1': _L1_mix_in['W1'], 'L1_mix_W2': _L1_mix_in['W2'], 'L1_mix_g1': _L1_mix_in['g1'], 'L1_mix_b1': _L1_mix_in['b1'], 'L1_mix_g2': _L1_mix_in['g2'], 'L1_mix_b2': _L1_mix_in['b2'], 'L1_ffn_sW1': _L1_ffn_in['sW1'], 'L1_ffn_sb1': _L1_ffn_in['sb1'], 'L1_ffn_sW2': _L1_ffn_in['sW2'], 'L1_ffn_sb2': _L1_ffn_in['sb2'], 'L1_ffn_sW3': _L1_ffn_in['sW3'], 'L1_ffn_sb3': _L1_ffn_in['sb3'], 'L1_ffn_eW1': _L1_ffn_in['eW1'], 'L1_ffn_eb1': _L1_ffn_in['eb1'], 'L1_ffn_eW2': _L1_ffn_in['eW2'], 'L1_ffn_eb2': _L1_ffn_in['eb2'], 'L1_ffn_eW3': _L1_ffn_in['eW3'], 'L1_ffn_eb3': _L1_ffn_in['eb3'], 'L1_ffn_gW': _L1_ffn_in['gW'], 'L1_ffn_gb': _L1_ffn_in['gb'], 'L2_gnn_W_forward': _L2_gnn_in['W_forward'], 'L2_gnn_W_reverse': _L2_gnn_in['W_reverse'], 'L2_gnn_attn_forward': _L2_gnn_in['attn_forward'], 'L2_mix_w_qkv': _L2_mix_in['w_qkv'], 'L2_mix_b_qkv': _L2_mix_in['b_qkv'], 'L2_mix_norm_g': _L2_mix_in['norm_g'], 'L2_mix_norm_b': _L2_mix_in['norm_b'], 'L2_mix_w_fc1': _L2_mix_in['w_fc1'], 'L2_mix_b_fc1': _L2_mix_in['b_fc1'], 'L2_mix_w_fc2': _L2_mix_in['w_fc2'], 'L2_mix_b_fc2': _L2_mix_in['b_fc2'], 'L2_ffn_Wr': _L2_ffn_in['Wr'], 'L2_ffn_br': _L2_ffn_in['br'], 'L2_ffn_ln_g': _L2_ffn_in['ln_g'], 'L2_ffn_ln_b': _L2_ffn_in['ln_b'], 'L2_ffn_W1': _L2_ffn_in['W1'], 'L2_ffn_b1': _L2_ffn_in['b1'], 'L2_ffn_W2': _L2_ffn_in['W2'], 'L2_ffn_b2': _L2_ffn_in['b2'], 'L3_gnn_Wq': _L3_gnn_in['Wq'], 'L3_gnn_bq': _L3_gnn_in['bq'], 'L3_gnn_Wk': _L3_gnn_in['Wk'], 'L3_gnn_bk': _L3_gnn_in['bk'], 'L3_gnn_Wv': _L3_gnn_in['Wv'], 'L3_gnn_bv': _L3_gnn_in['bv'], 'L3_gnn_Wo': _L3_gnn_in['Wo'], 'L3_gnn_bo': _L3_gnn_in['bo'], 'L3_gnn_W1': _L3_gnn_in['W1'], 'L3_gnn_b1': _L3_gnn_in['b1'], 'L3_gnn_W2': _L3_gnn_in['W2'], 'L3_gnn_b2': _L3_gnn_in['b2'], 'L3_gnn_bn1_g': _L3_gnn_in['bn1_g'], 'L3_gnn_bn1_b': _L3_gnn_in['bn1_b'], 'L3_gnn_bn2_g': _L3_gnn_in['bn2_g'], 'L3_gnn_bn2_b': _L3_gnn_in['bn2_b'], 'L3_mix_t': _L3_mix_in['t'], 'L3_mix_w_qkv': _L3_mix_in['w_qkv'], 'L3_mix_mem_kv': _L3_mix_in['mem_kv'], 'L3_mix_w_out': _L3_mix_in['w_out'], 'L3_mix_b_out': _L3_mix_in['b_out'], 'L3_mix_g_out': _L3_mix_in['g_out'], 'L3_mix_g_pre': _L3_mix_in['g_pre'], 'L3_ffn_attention_mask': _L3_ffn_in['attention_mask'], 'L3_ffn_wr': _L3_ffn_in['wr'], 'L3_ffn_br': _L3_ffn_in['br'], 'L3_ffn_w1': _L3_ffn_in['w1'], 'L3_ffn_b1': _L3_ffn_in['b1'], 'L3_ffn_w2': _L3_ffn_in['w2'], 'L3_ffn_b2': _L3_ffn_in['b2']}

def reference(x, src, dst, edge_attr_2, L0_gnn_Wq, L0_gnn_Wk, L0_gnn_Wv, L0_gnn_Wo_w, L0_gnn_Wo_b, L0_gnn_ln1_g, L0_gnn_ln1_b, L0_gnn_ln2_g, L0_gnn_ln2_b, L0_gnn_ffn_w1, L0_gnn_ffn_b1, L0_gnn_ffn_w2, L0_gnn_ffn_b2, L0_mix_wq, L0_mix_wk, L0_mix_wv, L0_mix_wo, L0_mix_bo, L0_mix_ln_k_g, L0_mix_ln_k_b, L0_mix_ln_v_g, L0_mix_ln_v_b, L0_ffn_W_gat, L0_ffn_att_src, L0_ffn_att_dst, L0_ffn_b_gat, L0_ffn_ln_gamma, L0_ffn_ln_beta, L0_ffn_W1, L0_ffn_b1, L0_ffn_W2, L0_ffn_b2, L0_ffn_edge_index, L1_gnn_W, L1_gnn_b, L1_mix_Wq, L1_mix_Wk, L1_mix_Wv, L1_mix_Wm, L1_mix_W1, L1_mix_W2, L1_mix_g1, L1_mix_b1, L1_mix_g2, L1_mix_b2, L1_ffn_sW1, L1_ffn_sb1, L1_ffn_sW2, L1_ffn_sb2, L1_ffn_sW3, L1_ffn_sb3, L1_ffn_eW1, L1_ffn_eb1, L1_ffn_eW2, L1_ffn_eb2, L1_ffn_eW3, L1_ffn_eb3, L1_ffn_gW, L1_ffn_gb, L2_gnn_W_forward, L2_gnn_W_reverse, L2_gnn_attn_forward, L2_mix_w_qkv, L2_mix_b_qkv, L2_mix_norm_g, L2_mix_norm_b, L2_mix_w_fc1, L2_mix_b_fc1, L2_mix_w_fc2, L2_mix_b_fc2, L2_ffn_Wr, L2_ffn_br, L2_ffn_ln_g, L2_ffn_ln_b, L2_ffn_W1, L2_ffn_b1, L2_ffn_W2, L2_ffn_b2, L3_gnn_Wq, L3_gnn_bq, L3_gnn_Wk, L3_gnn_bk, L3_gnn_Wv, L3_gnn_bv, L3_gnn_Wo, L3_gnn_bo, L3_gnn_W1, L3_gnn_b1, L3_gnn_W2, L3_gnn_b2, L3_gnn_bn1_g, L3_gnn_bn1_b, L3_gnn_bn2_g, L3_gnn_bn2_b, L3_mix_t, L3_mix_w_qkv, L3_mix_mem_kv, L3_mix_w_out, L3_mix_b_out, L3_mix_g_out, L3_mix_g_pre, L3_ffn_attention_mask, L3_ffn_wr, L3_ffn_br, L3_ffn_w1, L3_ffn_b1, L3_ffn_w2, L3_ffn_b2):
    import jax
    import jax.numpy as jnp

    def _L0_gnn_ref(x, edge_index, batch, Wq, Wk, Wv, Wo_w, Wo_b, ln1_g, ln1_b, ln2_g, ln2_b, ffn_w1, ffn_b1, ffn_w2, ffn_b2):
        import jax, jax.numpy as jnp
        import numpy as np
        N, E = (3125, 50000)
        IN_DIM = 256
        OUT_DIM = 256
        H = 8
        D = OUT_DIM // H
        SCALE = D ** (-0.5)
        LN_EPS = 1e-05

        def _layernorm(x, g, b):
            mu = jnp.mean(x, axis=-1, keepdims=True)
            var = jnp.mean((x - mu) ** 2, axis=-1, keepdims=True)
            return (x - mu) * jax.lax.rsqrt(var + LN_EPS) * g + b
        n = x.shape[0]
        residual = x
        Q = (x @ Wq).reshape(n, H, D)
        K = (x @ Wk).reshape(n, H, D)
        V = (x @ Wv).reshape(n, H, D)
        src, dst = (edge_index[0], edge_index[1])
        scores = jnp.einsum('ehd,ehd->eh', Q[dst], K[src]) * SCALE
        attn_max = jnp.zeros((n, H), scores.dtype).at[dst].max(scores)
        w = jnp.exp(scores - attn_max[dst])
        attn_sum = jnp.zeros((n, H), w.dtype).at[dst].add(w)
        w = w / (attn_sum[dst] + 1e-08)
        msg = V[src] * w[:, :, None]
        out = jnp.zeros((n, H, D), msg.dtype).at[dst].add(msg)
        out = out.reshape(n, OUT_DIM) @ Wo_w + Wo_b
        out = _layernorm(residual + out, ln1_g, ln1_b)
        ffn = jax.nn.gelu(out @ ffn_w1 + ffn_b1, approximate=False) @ ffn_w2 + ffn_b2
        out = _layernorm(out + ffn, ln2_g, ln2_b)
        return out

    def _L0_mix_ref(seq, wq, wk, wv, wo, bo, ln_k_g, ln_k_b, ln_v_g, ln_v_b):
        import jax, jax.numpy as jnp
        import numpy as np
        import math
        EMBED = 256
        HEADS = 4
        HEAD_DIM = EMBED // HEADS
        OUT_DIM = 256
        LN_EPS = 1e-05

        def _qkv_init(key):
            spread = math.sqrt(3.0 / EMBED)
            gain, delta = (0.01, 0.01)
            w = jax.random.uniform(key, (EMBED, EMBED), minval=-spread, maxval=spread) * gain
            return w + delta * jnp.eye(EMBED, dtype=w.dtype)

        def _layer_norm(x, g, b):
            mu = jnp.mean(x, axis=-1, keepdims=True)
            var = jnp.mean(jnp.square(x - mu), axis=-1, keepdims=True)
            return (x - mu) * jax.lax.rsqrt(var + LN_EPS) * g + b

        def _split_heads(x, B, S):
            return x.reshape(B, S, HEADS, HEAD_DIM).transpose(0, 2, 1, 3)
        B, S, _ = seq.shape
        q = _split_heads(seq @ wq.T, B, S)
        k = _split_heads(seq @ wk.T, B, S)
        v = _split_heads(seq @ wv.T, B, S)
        k = _layer_norm(k, ln_k_g, ln_k_b)
        v = _layer_norm(v, ln_v_g, ln_v_b)
        kv = jnp.einsum('bhsd,bhse->bhde', k, v) / S
        ga = jnp.einsum('bhsd,bhde->bhse', q, kv)
        ga = ga.transpose(0, 2, 1, 3).reshape(B, S, EMBED)
        return ga @ wo.T + bo

    def _L0_ffn_ref(x, W_gat, att_src, att_dst, b_gat, ln_gamma, ln_beta, W1, b1, W2, b2, edge_index):
        import jax, jax.numpy as jnp
        import numpy as np
        B, N, D = (16, 256, 256)
        NUM_EXPERTS, TOP_K, HEADS = (4, 2, 4)
        N_EDGES = 65536
        LN_EPS = 1e-05

        def _layernorm(x, g, b):
            mu = x.mean(-1, keepdims=True)
            var = ((x - mu) ** 2).mean(-1, keepdims=True)
            return (x - mu) * jax.lax.rsqrt(var + LN_EPS) * g + b

        def _forward(x, edge_index, W_gat, att_src, att_dst, b_gat, ln_gamma, ln_beta, W1, b1, W2, b2):
            Bc, Nc, Dc = x.shape
            M = Bc * Nc
            x_flat = x.reshape(M, Dc)
            h = (x_flat @ W_gat).reshape(M, HEADS, NUM_EXPERTS)
            loops = jnp.arange(M, dtype=edge_index.dtype)
            src = jnp.concatenate([edge_index[0], loops])
            dst = jnp.concatenate([edge_index[1], loops])
            a_src = (h * att_src).sum(-1)
            a_dst = (h * att_dst).sum(-1)
            e = jax.nn.leaky_relu(a_src[src] + a_dst[dst], negative_slope=0.2)
            e_max = jax.ops.segment_max(e, dst, num_segments=M)
            ee = jnp.exp(e - e_max[dst])
            denom = jax.ops.segment_sum(ee, dst, num_segments=M)
            alpha = ee / (denom[dst] + 1e-16)
            msg = h[src] * alpha[:, :, None]
            agg = jax.ops.segment_sum(msg, dst, num_segments=M).reshape(M, HEADS * NUM_EXPERTS) + b_gat
            scores = _layernorm(agg, ln_gamma, ln_beta).reshape(M, HEADS, NUM_EXPERTS).mean(1)
            scores = scores.reshape(Bc, Nc, NUM_EXPERTS)
            topk_s, topk_i = jax.lax.top_k(scores, TOP_K)
            w = jax.nn.softmax(topk_s, axis=-1)
            out = jnp.zeros_like(x)
            for ei in range(NUM_EXPERTS):
                g = jnp.where(topk_i == ei, w, 0.0).sum(-1)
                hh = jax.nn.gelu(x @ W1[ei] + b1[ei], approximate=False)
                out = out + g[..., None] * (hh @ W2[ei] + b2[ei])
            return out
        return _forward(x, edge_index, W_gat, att_src, att_dst, b_gat, ln_gamma, ln_beta, W1, b1, W2, b2)

    def _L1_gnn_ref(x, edge_index, W, b):
        import jax, jax.numpy as jnp
        import numpy as np
        N_NODES = 3125
        N_EDGES = 50000
        D_IN = 256
        D_OUT = 256
        N = x.shape[0]
        loop = jnp.arange(N, dtype=edge_index.dtype)
        src = jnp.concatenate([edge_index[0], loop])
        dst = jnp.concatenate([edge_index[1], loop])
        deg = jax.ops.segment_sum(jnp.ones_like(src, dtype=x.dtype), dst, num_segments=N)
        deg_inv_sqrt = jnp.where(deg > 0, jax.lax.rsqrt(jnp.maximum(deg, 1.0)), 0.0)
        norm = deg_inv_sqrt[src] * deg_inv_sqrt[dst]
        h = jnp.einsum('nd,od->no', x, W)
        msg = h[src] * norm[:, None]
        out = jax.ops.segment_sum(msg, dst, num_segments=N) + b
        return jax.nn.relu(out)

    def _L1_mix_ref(x, Wq, Wk, Wv, Wm, W1, W2, g1, b1, g2, b2):
        import jax, jax.numpy as jnp
        import numpy as np
        NHEAD = 8
        ATT_EPS = 1e-06
        LN_EPS = 1e-05

        def _layernorm(x, g, b):
            mu = jnp.mean(x, axis=-1, keepdims=True)
            var = jnp.mean(jnp.square(x - mu), axis=-1, keepdims=True)
            return (x - mu) * jax.lax.rsqrt(var + LN_EPS) * g + b
        N, L, C = x.shape
        H = NHEAD
        D = C // H
        q = (x @ Wq).reshape(N, L, H, D)
        k = (x @ Wk).reshape(N, L, H, D)
        v = (x @ Wv).reshape(N, L, H, D)
        Q = jax.nn.elu(q) + 1.0
        K = jax.nn.elu(k) + 1.0
        v = v / L
        KV = jnp.einsum('nshd,nshv->nhdv', K, v)
        Z = 1.0 / (jnp.einsum('nlhd,nhd->nlh', Q, K.sum(axis=1)) + ATT_EPS)
        msg = jnp.einsum('nlhd,nhdv,nlh->nlhv', Q, KV, Z) * L
        msg = msg.reshape(N, L, C) @ Wm
        msg = _layernorm(msg, g1, b1)
        h = jnp.concatenate([x, msg], axis=-1) @ W1
        h = jax.nn.relu(h) @ W2
        msg = _layernorm(h, g2, b2)
        return x + msg

    def _L1_ffn_ref(x, sW1, sb1, sW2, sb2, sW3, sb3, eW1, eb1, eW2, eb2, eW3, eb3, gW, gb):
        import jax, jax.numpy as jnp
        import numpy as np
        B, A = (256, 8)
        IN, OUT = (256, 256)
        SH1, SH2 = (256, 128)
        EH1, EH2 = (128, 64)
        E, TOPK = (4, 2)

        def _shared_mlp(x, W1, b1, W2, b2, W3, b3):
            h = jax.nn.relu(x @ W1 + b1)
            h = jax.nn.relu(h @ W2 + b2)
            return h @ W3 + b3

        def _experts_mlp(x, eW1, eb1, eW2, eb2, eW3, eb3):
            h = jax.nn.relu(jnp.einsum('baf,efh->ebah', x, eW1) + eb1[:, None, None, :])
            h = jax.nn.relu(jnp.einsum('ebah,ehg->ebag', h, eW2) + eb2[:, None, None, :])
            o = jnp.einsum('ebag,ego->ebao', h, eW3) + eb3[:, None, None, :]
            return jnp.moveaxis(o, 0, -1)
        all_out = _experts_mlp(x, eW1, eb1, eW2, eb2, eW3, eb3)
        shared = _shared_mlp(x, sW1, sb1, sW2, sb2, sW3, sb3)
        gates = jax.nn.softmax(x @ gW + gb, axis=-1)
        topv, topi = jax.lax.top_k(gates, TOPK)
        topw = jax.nn.softmax(topv, axis=-1)
        sel = jnp.take_along_axis(all_out, topi[:, :, None, :], axis=-1)
        gated = jnp.sum(sel * topw[:, :, None, :], axis=-1)
        return shared + gated

    def _L2_gnn_ref(h, adj, direction, W_forward, W_reverse, attn_forward):
        import jax, jax.numpy as jnp
        import numpy as np
        N_NODES = 6250
        N_EDGES = 100000
        IN_FEATS = 256
        OUT_FEATS = 64
        NUM_HEADS = 4
        N = h.shape[0]
        H = attn_forward.shape[1]
        h_fwd = h @ W_forward.T
        h_rev = h @ W_reverse.T
        src, dst = (adj[0], adj[1])
        messages = h_fwd[src] * direction[:, 0:1] + h_rev[src] * direction[:, 1:2]
        scores = jnp.einsum('ef,hf->eh', messages, attn_forward[0])
        scores = jax.nn.leaky_relu(scores, negative_slope=0.2)
        exp_scores = jnp.exp(scores - scores.max(axis=0, keepdims=True))
        sum_exp = jax.ops.segment_sum(exp_scores, dst, num_segments=N)
        norm = exp_scores / (sum_exp[dst] + 1e-10)
        outs = [jax.ops.segment_sum(messages * norm[:, hd:hd + 1], dst, num_segments=N) for hd in range(H)]
        out = jnp.stack(outs, axis=1)
        return out.reshape(N, -1)

    def _L2_mix_ref(x, w_qkv, b_qkv, norm_g, norm_b, w_fc1, b_fc1, w_fc2, b_fc2):
        import jax, jax.numpy as jnp
        import numpy as np
        DIM = 256
        HEADS = 4
        HEAD_DIM = DIM // HEADS
        MLP_HIDDEN = DIM * 3
        B, N = (8, 256)
        EPS = 1e-05

        def _layernorm(x, g, b):
            mu = jnp.mean(x, axis=-1, keepdims=True)
            var = jnp.mean(jnp.square(x - mu), axis=-1, keepdims=True)
            return (x - mu) * jax.lax.rsqrt(var + EPS) * g + b
        Bx, Nx, C = x.shape
        scale = HEAD_DIM ** (-0.5)
        qkv = (x @ w_qkv + b_qkv).reshape(Bx, Nx, 3, HEADS, HEAD_DIM)
        qkv = jnp.transpose(qkv, (2, 0, 3, 1, 4))
        q, k, v = (qkv[0], qkv[1], qkv[2])
        k = k * scale
        attn = jnp.einsum('bhnd,bhne->bhde', k, v)
        attn = jax.nn.softmax(attn, axis=-1)
        xf = jnp.einsum('bhde,bhne->bhnd', attn, q)
        xf = jnp.transpose(xf, (0, 2, 1, 3)).reshape(Bx, Nx, C)
        x = x + xf
        h = _layernorm(x, norm_g, norm_b)
        h = jax.nn.gelu(h @ w_fc1 + b_fc1, approximate=False) @ w_fc2 + b_fc2
        return x + h

    def _L2_ffn_ref(x, Wr, br, ln_g, ln_b, W1, b1, W2, b2):
        import jax, jax.numpy as jnp
        import numpy as np
        TOP_K = 2
        LN_EPS = 1e-05
        B, S, D = x.shape
        N = B * S
        xt = x.reshape(N, D)
        logits = xt @ Wr + br
        probs = jax.nn.softmax(logits, axis=-1)
        top_p, top_idx = jax.lax.top_k(probs, TOP_K)
        weights = top_p / top_p.sum(axis=-1, keepdims=True)
        mu = xt.mean(axis=-1, keepdims=True)
        var = ((xt - mu) ** 2).mean(axis=-1, keepdims=True)
        xn = (xt - mu) * jax.lax.rsqrt(var + LN_EPS)
        xe = xn[None, :, :] * ln_g[:, None, :] + ln_b[:, None, :]
        h = jax.nn.gelu(jnp.einsum('end,edh->enh', xe, W1) + b1[:, None, :], approximate=False)
        y = jnp.einsum('enh,ehd->end', h, W2) + b2[:, None, :]
        y_tok = jnp.transpose(y, (1, 0, 2))
        sel = jnp.take_along_axis(y_tok, top_idx[:, :, None], axis=1)
        out = (weights[:, :, None] * sel).sum(axis=1)
        return out.reshape(B, S, D)

    def _L3_gnn_ref(x, edge_index, Wq, bq, Wk, bk, Wv, bv, Wo, bo, W1, b1, W2, b2, bn1_g, bn1_b, bn2_g, bn2_b):
        import jax, jax.numpy as jnp
        import numpy as np
        N_NODES = 3125
        N_EDGES = 50000
        D_MODEL = 256
        NUM_HEADS = 8
        HEAD_DIM = D_MODEL // NUM_HEADS
        D_FF = 2 * D_MODEL
        NEG_SLOPE = 0.2
        BN_EPS = 1e-05

        def _batch_norm(h, g, b):
            mean = jnp.mean(h, axis=0)
            var = jnp.mean((h - mean) ** 2, axis=0)
            return (h - mean) * jax.lax.rsqrt(var + BN_EPS) * g + b
        N = x.shape[0]
        Qh = (x @ Wq + bq).reshape(N, NUM_HEADS, HEAD_DIM)
        Kh = (x @ Wk + bk).reshape(N, NUM_HEADS, HEAD_DIM)
        Vh = (x @ Wv + bv).reshape(N, NUM_HEADS, HEAD_DIM)
        s = jnp.einsum('nhc,nhc->nh', Qh, Kh) / jnp.sqrt(jnp.float32(HEAD_DIM))
        loops = jnp.arange(N, dtype=edge_index.dtype)
        src = jnp.concatenate([edge_index[0], loops])
        dst = jnp.concatenate([edge_index[1], loops])
        alpha = jax.nn.leaky_relu(s[src] + s[dst], NEG_SLOPE)
        m = jax.ops.segment_max(alpha, dst, num_segments=N)
        e = jnp.exp(alpha - m[dst])
        denom = jax.ops.segment_sum(e, dst, num_segments=N)
        a = e / denom[dst]
        msg = Vh[src] * a[:, :, None]
        attn = jax.ops.segment_sum(msg, dst, num_segments=N).reshape(N, D_MODEL)
        h = attn @ Wo + bo
        h = x + h
        h = _batch_norm(h, bn1_g, bn1_b)
        h2 = jax.nn.relu(h @ W1 + b1) @ W2 + b2
        h = _batch_norm(h + h2, bn2_g, bn2_b)
        return h

    def _L3_mix_ref(x, t, w_qkv, mem_kv, w_out, b_out, g_out, g_pre):
        import jax, jax.numpy as jnp
        import numpy as np
        DIM = 256
        HEADS = 4
        DIM_HEAD = 32
        NUM_MEM = 4
        HIDDEN = HEADS * DIM_HEAD
        SCALE = DIM_HEAD ** (-0.5)

        def rmsnorm(x, g):
            n = jnp.linalg.norm(x, axis=-1, keepdims=True)
            return x / jnp.maximum(n, 1e-12) * g * x.shape[-1] ** 0.5
        b, n, c = x.shape
        xn = rmsnorm(x, g_pre)
        qkv = xn @ w_qkv
        q, k, v = jnp.split(qkv, 3, axis=-1)

        def to_heads(z):
            return z.reshape(b, n, HEADS, DIM_HEAD).transpose(0, 2, 3, 1)
        q, k, v = map(to_heads, (q, k, v))
        mk = jnp.broadcast_to(mem_kv[0], (b, HEADS, DIM_HEAD, NUM_MEM))
        mv = jnp.broadcast_to(mem_kv[1], (b, HEADS, DIM_HEAD, NUM_MEM))
        k = jnp.concatenate([mk, k], axis=-1)
        v = jnp.concatenate([mv, v], axis=-1)
        q = jax.nn.softmax(q, axis=-2) * SCALE
        k = jax.nn.softmax(k, axis=-1)
        context = jnp.einsum('bhdn,bhen->bhde', k, v)
        out = jnp.einsum('bhde,bhdn->bhen', context, q)
        out = out.transpose(0, 3, 1, 2).reshape(b, n, HIDDEN)
        out = rmsnorm(out @ w_out + b_out, g_out)
        return out + x

    def _L3_ffn_ref(x, attention_mask, wr, br, w1, b1, w2, b2):
        import jax, jax.numpy as jnp
        import numpy as np
        B, S, D = (8, 256, 256)
        H = 4 * D
        CAPACITY = 0.5
        b, s, d = x.shape
        weights = (jnp.einsum('bsd,do->bso', x, wr) + br)[..., 0]
        k = max(1, int(CAPACITY * s))
        kk = k - 1 if k > 1 else 1
        _, idx = jax.lax.top_k(weights, k)
        sel_idx = idx[:, :kk]
        sel = jnp.take_along_axis(x, sel_idx[:, :, None], axis=1)
        h = jax.nn.gelu(jnp.einsum('bkd,dh->bkh', sel, w1) + b1)
        y = jnp.einsum('bkh,hd->bkd', h, w2) + b2
        w_sel = jnp.take_along_axis(weights, sel_idx, axis=1)
        y = y * w_sel[..., None]
        batch_idx = jnp.arange(b)[:, None]
        processed = jnp.zeros_like(x).at[batch_idx, sel_idx].set(y)
        return processed + x
    edge_index = jnp.stack([src, dst])
    batch0 = jnp.zeros((3125,), jnp.int32)
    xn = _layernorm(x, axis=-1)
    x = x + _L0_gnn_ref(xn, edge_index, batch0, L0_gnn_Wq, L0_gnn_Wk, L0_gnn_Wv, L0_gnn_Wo_w, L0_gnn_Wo_b, L0_gnn_ln1_g, L0_gnn_ln1_b, L0_gnn_ln2_g, L0_gnn_ln2_b, L0_gnn_ffn_w1, L0_gnn_ffn_b1, L0_gnn_ffn_w2, L0_gnn_ffn_b2) + _L0_mix_ref(xn[None], L0_mix_wq, L0_mix_wk, L0_mix_wv, L0_mix_wo, L0_mix_bo, L0_mix_ln_k_g, L0_mix_ln_k_b, L0_mix_ln_v_g, L0_mix_ln_v_b)[0]
    x = x + _L0_ffn_ref(_layernorm(x, axis=-1)[None], L0_ffn_W_gat, L0_ffn_att_src, L0_ffn_att_dst, L0_ffn_b_gat, L0_ffn_ln_gamma, L0_ffn_ln_beta, L0_ffn_W1, L0_ffn_b1, L0_ffn_W2, L0_ffn_b2, L0_ffn_edge_index)[0]
    xn = _layernorm(x, axis=-1)
    x = x + _L1_gnn_ref(xn, edge_index, L1_gnn_W, L1_gnn_b) + _L1_mix_ref(xn[None], L1_mix_Wq, L1_mix_Wk, L1_mix_Wv, L1_mix_Wm, L1_mix_W1, L1_mix_W2, L1_mix_g1, L1_mix_b1, L1_mix_g2, L1_mix_b2)[0]
    x = x + _L1_ffn_ref(_layernorm(x, axis=-1)[None], L1_ffn_sW1, L1_ffn_sb1, L1_ffn_sW2, L1_ffn_sb2, L1_ffn_sW3, L1_ffn_sb3, L1_ffn_eW1, L1_ffn_eb1, L1_ffn_eW2, L1_ffn_eb2, L1_ffn_eW3, L1_ffn_eb3, L1_ffn_gW, L1_ffn_gb)[0]
    xn = _layernorm(x, axis=-1)
    x = x + _L2_gnn_ref(xn, edge_index, edge_attr_2, L2_gnn_W_forward, L2_gnn_W_reverse, L2_gnn_attn_forward) + _L2_mix_ref(xn[None], L2_mix_w_qkv, L2_mix_b_qkv, L2_mix_norm_g, L2_mix_norm_b, L2_mix_w_fc1, L2_mix_b_fc1, L2_mix_w_fc2, L2_mix_b_fc2)[0]
    x = x + _L2_ffn_ref(_layernorm(x, axis=-1)[None], L2_ffn_Wr, L2_ffn_br, L2_ffn_ln_g, L2_ffn_ln_b, L2_ffn_W1, L2_ffn_b1, L2_ffn_W2, L2_ffn_b2)[0]
    xn = _layernorm(x, axis=-1)
    x = x + _L3_gnn_ref(xn, edge_index, L3_gnn_Wq, L3_gnn_bq, L3_gnn_Wk, L3_gnn_bk, L3_gnn_Wv, L3_gnn_bv, L3_gnn_Wo, L3_gnn_bo, L3_gnn_W1, L3_gnn_b1, L3_gnn_W2, L3_gnn_b2, L3_gnn_bn1_g, L3_gnn_bn1_b, L3_gnn_bn2_g, L3_gnn_bn2_b) + _L3_mix_ref(xn[None], L3_mix_t, L3_mix_w_qkv, L3_mix_mem_kv, L3_mix_w_out, L3_mix_b_out, L3_mix_g_out, L3_mix_g_pre)[0]
    x = x + _L3_ffn_ref(_layernorm(x, axis=-1)[None], L3_ffn_attention_mask, L3_ffn_wr, L3_ffn_br, L3_ffn_w1, L3_ffn_b1, L3_ffn_w2, L3_ffn_b2)[0]
    return x

_drawn_inputs = setup_inputs


def setup_inputs(seed=0):
    import zlib

    import numpy as np

    out = dict(_drawn_inputs(seed))
    spreads = {'L0_gnn_Wo_b': (0.0, 0.1),
     'L0_gnn_ln1_g': (1.0, 0.2),
     'L0_gnn_ln1_b': (0.0, 0.1),
     'L0_gnn_ln2_g': (1.0, 0.2),
     'L0_gnn_ln2_b': (0.0, 0.1),
     'L0_gnn_ffn_b1': (0.0, 0.1),
     'L0_gnn_ffn_b2': (0.0, 0.1),
     'L0_mix_ln_k_g': (1.0, 0.6),
     'L0_mix_ln_k_b': (0.0, 0.8),
     'L0_mix_ln_v_g': (1.0, 0.6),
     'L0_mix_ln_v_b': (0.0, 0.8),
     'L0_ffn_b_gat': (0.0, 0.1),
     'L0_ffn_ln_gamma': (1.0, 0.2),
     'L0_ffn_ln_beta': (0.0, 0.1),
     'L0_ffn_b1': (0.0, 0.1),
     'L0_ffn_b2': (0.0, 0.1),
     'L1_gnn_b': (0.0, 0.334),
     'L1_mix_g1': (1.0, 0.2),
     'L1_mix_b1': (0.0, 0.1),
     'L1_mix_g2': (1.0, 0.2),
     'L1_mix_b2': (0.0, 0.1),
     'L1_ffn_sb1': (0.0, 0.8),
     'L1_ffn_sb2': (0.0, 0.573),
     'L1_ffn_sb3': (0.0, 0.1),
     'L1_ffn_eb1': (0.0, 0.8),
     'L1_ffn_eb2': (0.0, 0.8),
     'L1_ffn_eb3': (0.0, 0.322),
     'L1_ffn_gb': (0.0, 0.8),
     'L2_mix_b_qkv': (0.0, 0.1),
     'L2_mix_norm_g': (1.0, 0.6),
     'L2_mix_norm_b': (0.0, 0.8),
     'L2_mix_b_fc1': (0.0, 0.8),
     'L2_mix_b_fc2': (0.0, 0.365),
     'L2_ffn_br': (0.0, 0.397),
     'L2_ffn_ln_g': (1.0, 0.6),
     'L2_ffn_ln_b': (0.0, 0.657),
     'L2_ffn_b1': (0.0, 0.661),
     'L2_ffn_b2': (0.0, 0.445),
     'L3_gnn_bq': (0.0, 0.8),
     'L3_gnn_bk': (0.0, 0.8),
     'L3_gnn_bv': (0.0, 0.8),
     'L3_gnn_bo': (0.0, 0.8),
     'L3_gnn_b1': (0.0, 0.8),
     'L3_gnn_b2': (0.0, 0.8),
     'L3_gnn_bn1_g': (1.0, 0.6),
     'L3_gnn_bn1_b': (0.0, 0.8),
     'L3_gnn_bn2_g': (1.0, 0.2),
     'L3_gnn_bn2_b': (0.0, 0.518),
     'L3_mix_b_out': (0.0, 0.1),
     'L3_mix_g_out': (1.0, 0.54),
     'L3_mix_g_pre': (1.0, 0.6),
     'L3_ffn_b1': (0.0, 0.8),
     'L3_ffn_b2': (0.0, 0.8)}
    factors = {'L0_gnn_Wq': 3.359,
     'L0_gnn_Wk': 3.383,
     'L0_mix_wq': 8.0,
     'L0_mix_wk': 8.0,
     'L0_mix_wv': 8.0,
     'L0_mix_wo': 8.0,
     'L0_ffn_att_src': 2.806,
     'L0_ffn_att_dst': 3.967,
     'L1_mix_Wq': 4.182,
     'L1_ffn_eW1': 3.545,
     'L1_ffn_eW2': 3.228,
     'L3_gnn_Wq': 8.0,
     'L3_gnn_Wk': 8.0,
     'L3_gnn_Wv': 4.639,
     'L3_gnn_Wo': 4.618,
     'L3_mix_w_qkv': 8.0,
     'L3_mix_mem_kv': 8.0,
     'L3_mix_w_out': 8.0,
     'L3_ffn_wr': 8.0,
     'L3_ffn_w1': 8.0,
     'L3_ffn_w2': 8.0}
    for name, (base, spread) in spreads.items():
        noise = np.random.default_rng([zlib.crc32(name.encode()), seed]).standard_normal(out[name].shape)
        drawn = base * np.exp(spread * noise) if base else spread * noise
        out[name] = jnp.asarray(drawn.astype(out[name].dtype))
    for name, factor in factors.items():
        out[name] = (out[name] * factor).astype(out[name].dtype)
    return out
```

```python
from contextlib import ExitStack

import concourse.bass as bass
from concourse import mybir

F32 = mybir.dt.float32
BF16 = mybir.dt.bfloat16
I32 = mybir.dt.int32
ALU = mybir.AluOpType
ACT = mybir.ActivationFunctionType
AX = mybir.AxisListType

N = 3125
NP = 125
T = N // NP
D = 256
FAR = 1e30


class Scope:

    spent = []

    def __init__(self, nc, name):
        self.nc, self.name, self.stack, self.mine = nc, name, ExitStack(), []

    def __enter__(self):
        self.stack.__enter__()
        return self

    def __exit__(self, *why):
        left = self.stack.__exit__(*why)
        Scope.spent += self.mine
        if len(Scope.spent) > 72:
            numbers = sorted(Scope.spent)
            starts = [n for n in numbers if n - 1 not in numbers]
            ends = [n + 1 for n in numbers if n + 1 not in numbers]
            for a, b in zip(starts, ends):
                self.nc.gpsimd.sem_clear(range(a, b))
            self.nc.all_engine_barrier()
            Scope.spent = []
        return left

    def sb(self, n, shape, dtype=F32):
        return self.stack.enter_context(self.nc.sbuf_tensor(f"{self.name}_{n}", shape, dtype))

    def ps(self, n, shape, dtype=F32):
        return self.stack.enter_context(self.nc.psum_tensor(f"{self.name}_{n}", shape, dtype))

    def sem(self, n):
        handle = self.stack.enter_context(self.nc.semaphore(f"{self.name}_{n}"))
        self.mine.append(handle.num)
        return handle

    def own_sem(self, n):
        return self.nc.alloc_semaphore(f"{self.name}_{n}")


def constants(nc, const):
    with Scope(nc, "constants") as k:
        counted = k.sb("counted", [128, 128], I32)
        set_up, cut = k.sem("set_up"), k.sem("cut")
        with nc.Block() as block:
            @block.gpsimd
            def _(pool):
                pool.iota(counted[:, :], pattern=[[1, 128]], base=0, channel_multiplier=0).then_inc(cut, 1)
                pool.memset(const["ones"][:, :], 1.0)
                pool.memset(const["before"][:, :], 1.0).then_inc(set_up, 1)
                pool.memset(const["eye"][:, :], 0.0).then_inc(set_up, 1)
                pool.wait_ge(set_up, 2)
                pool.affine_select(out=const["eye"][:, :], in_=const["eye"][:, :], compare_op=ALU.not_equal, fill=1.0, base=0, pattern=[[-1, 128]], channel_multiplier=1).then_inc(cut, 1)
                pool.affine_select(out=const["before"][:, :], in_=const["before"][:, :], compare_op=ALU.is_gt, fill=0.0, base=0, pattern=[[1, 128]], channel_multiplier=-1).then_inc(cut, 1)

            @block.vector
            def _(dve):
                dve.wait_ge(cut, 3)
                dve.tensor_copy(const["ramp"][:, :], counted[:, :])
                for c in range(4):
                    dve.tensor_copy(const["eye4_bf"][:, c * 128:(c + 1) * 128], const["eye"][:, :])


def group_edges(nc, edge, src, dst, attr, E, count, const, scratch, name):
    J = count
    cols = edge["cols"]
    SUPER = cols // 2
    full, rest = E // J, E % J
    with Scope(nc, name) as k:
        sb, ps, sem = k.sb, k.ps, k.sem

        src_i, dst_i = sb("src_i", [128, J], I32), sb("dst_i", [128, J], I32)
        load = sb("load", [128, J, 4])
        dst_f, tile_f, work = sb("dst_f", [128, J]), sb("tile_f", [128, J]), sb("work", [128, J])
        mask, whole = sb("mask", [128, J], I32), sb("whole", [128, J], I32)
        slot = sb("slot", [128, J])
        row, spare = sb("row", [128, J], I32), sb("spare", [128, J], I32)
        ones = sb("ones", [128, J])
        at = sb("at", [128, J, 2]) if attr is not None else None
        per_bin, base = sb("per_bin", [128, T]), sb("base", [128, T])
        ends, starts = sb("ends", [128, T]), sb("starts", [128, T])
        pad_i = sb("pad_i", [128, T], I32)
        first = sb("first", [128, SUPER])
        past = sb("past", [128, SUPER, T])
        tile_fs = sb("tile_fs", [128, SUPER])
        ring_row, ring_load = sb("ring_row", [128, 4, 1], I32), sb("ring_load", [128, 4, 4])
        sums = ps("sums", [128, 2, T])
        cleared, loaded, made = sem("cleared"), sem("loaded"), sem("made")
        step, counted, summed, filled = sem("step"), sem("counted"), sem("summed"), sem("filled")
        rows_ready, staged, back = sem("rows_ready"), sem("staged"), sem("back")
        scattered = [k.own_sem(f"scattered{u}") for u in range(4)]
        ids = edge["tile_of"]
        steps = [0]

        with nc.Block() as block:
            @block.sync
            def _(sp):
                sp.wait_ge(cleared, 3)
                for to, of in ((src_i, src), (dst_i, dst)):
                    sp.dma_start(to[0:full, :], of[0:full * J].rearrange("(p j) -> p j", j=J)).then_inc(loaded, 16)
                    if rest:
                        sp.dma_start(to[full:full + 1, 0:rest], of[full * J:E].rearrange("(p j) -> p j", p=1)).then_inc(loaded, 16)
                if at is not None:
                    sp.dma_start(at[0:full, :, :], attr[0:full * J, :].rearrange("(p j) c -> p j c", j=J)).then_inc(loaded, 16)
                    if rest:
                        sp.dma_start(at[full:full + 1, 0:rest, :], attr[full * J:E, :].rearrange("(p j) c -> p j c", p=1)).then_inc(loaded, 16)
                sp.wait_ge(made, 1)
                sp.dma_start(scratch[0:128 * cols, :].rearrange("(p c) f -> p (c f)", c=cols), edge["data"][:, 0:cols, :].rearrange("p c f -> p (c f)")).then_inc(filled, 16)
                for u in range(4):
                    sp.wait_ge(scattered[u], 16 * (J // 4))
                sp.wait_ge(filled, 16)
                sp.dma_start(edge["data"][:, 0:cols, :].rearrange("p c f -> p (c f)"), scratch[0:128 * cols, :].rearrange("(p c) f -> p (c f)", c=cols)).then_inc(back, 16)
                sp.wait_ge(back, 16)

            n_loads = (2 + (attr is not None)) * (1 + bool(rest))

            @block.gpsimd
            def _(pool):
                pool.iota(spare[:, :], pattern=[[1, J]], base=128 * cols, channel_multiplier=J).then_inc(made, 1)
                pool.iota(row[:, 0:SUPER], pattern=[[256, SUPER]], base=0, channel_multiplier=0).then_inc(made, 1)
                pool.wait_ge(filled, 16)
                with pool.Fori(0, J // 4) as i:
                    for u in range(4):
                        pool.wait_ge(staged, i * 4 + u + 1)
                        pool.nop(nofuse=True)
                        pool.indirect_dma_start(scratch, bass.IndirectOffsetOnAxis(ap=ring_row[:, u, :], axis=0), ring_load[:, u, :], None).then_inc(scattered[u], 16)
                for u in range(4):
                    pool.wait_ge(scattered[u], 16 * (J // 4))

            @block.tensor
            def _(pe):
                pe.wait_ge(counted, 1)
                pe.matmul(sums[:, 0, :], const["before"][:, :], per_bin[:, :], start=True, stop=True)
                pe.matmul(sums[:, 1, :], const["ones"][:, 0:128], per_bin[:, :], start=True, stop=True).then_inc(summed, 1)

            @block.vector
            def _(dve):
                def then(ins):
                    steps[0] += 1
                    ins.then_inc(step, 1)
                    dve.wait_ge(step, steps[0])

                dve.memset(src_i[:, :], 0).then_inc(cleared, 1)
                dve.memset(dst_i[:, :], 1 << 20).then_inc(cleared, 1)
                if at is not None:
                    dve.memset(at[:, :, :], 0.0)
                dve.memset(load[:, :, :], 0.0)
                then(dve.memset(edge["data"][:, :, :], 0.0))
                dve.memset(edge["data"][:, :, 1], -1.0).then_inc(made, 1)
                dve.memset(slot[:, :], 0.0)
                dve.memset(ones[:, :], 1.0).then_inc(cleared, 1)
                dve.wait_ge(cleared, 3)
                dve.wait_ge(loaded, 16 * n_loads)
                then(dve.tensor_copy(dst_f[:, :], dst_i[:, :]))
                then(dve.tensor_scalar(work[:, :], dst_f[:, :], 1.0 / NP, None, ALU.mult))
                then(dve.tensor_copy(whole[:, :], work[:, :]))
                then(dve.tensor_copy(tile_f[:, :], whole[:, :]))
                then(dve.scalar_tensor_tensor(out=work[:, :], in0=tile_f[:, :], scalar=-float(NP), in1=dst_f[:, :], op0=ALU.mult, op1=ALU.add))
                then(dve.tensor_scalar(slot[:, :], work[:, :], 0.0, None, ALU.is_lt))
                then(dve.tensor_tensor(tile_f[:, :], tile_f[:, :], slot[:, :], ALU.subtract))
                then(dve.tensor_scalar(slot[:, :], work[:, :], float(NP), None, ALU.is_ge))
                then(dve.tensor_tensor(tile_f[:, :], tile_f[:, :], slot[:, :], ALU.add))
                then(dve.scalar_tensor_tensor(out=load[:, :, 1], in0=tile_f[:, :], scalar=-float(NP), in1=dst_f[:, :], op0=ALU.mult, op1=ALU.add))
                then(dve.tensor_copy(work[:, :], src_i[:, :]))
                then(dve.tensor_scalar(work[:, :], work[:, :], float(N - 1), 0.0, ALU.min, ALU.max))
                then(dve.tensor_copy(load[:, :, 0].bitcast(I32), work[:, :]))
                if at is not None:
                    then(dve.tensor_copy(load[:, :, 2:4], at[:, :, :]))
                for b in range(T):
                    then(dve.tensor_scalar(work[:, :], tile_f[:, :], float(b), None, ALU.is_equal))
                    then(dve.reduce_sum(per_bin[:, b:b + 1], work[:, :], axis=AX.X))
                dve.memset(slot[:, :], 0.0).then_inc(counted, 1)
                dve.wait_ge(summed, 1)
                then(dve.tensor_scalar(ends[:, :], sums[:, 1, :], 255.0, None, ALU.add))
                then(dve.tensor_copy(pad_i[:, :], ends[:, :]))
                then(dve.tensor_scalar(pad_i[:, :], pad_i[:, :], 8, 8, ALU.arith_shift_right, ALU.arith_shift_left))
                then(dve.tensor_copy(starts[:, :], pad_i[:, :]))
                then(dve.tensor_tensor_scan(ends[:, :], ones[:, 0:T], starts[:, :], 0.0, ALU.mult, ALU.add))
                then(dve.tensor_tensor(starts[:, :], ends[:, :], starts[:, :], ALU.subtract))
                then(dve.tensor_tensor(base[:, :], starts[:, :], sums[:, 0, :], ALU.add))
                dve.wait_ge(made, 3)
                then(dve.tensor_copy(first[:, :], row[:, 0:SUPER]))
                then(dve.tensor_tensor(past[:, :, :], ends[:, :].unsqueeze(1).to_broadcast([128, SUPER, T]), first[:, :].unsqueeze(2).to_broadcast([128, SUPER, T]), ALU.is_le))
                then(dve.reduce_sum(tile_fs[:, :], past[:, :, :], axis=AX.X))
                then(dve.tensor_scalar(tile_fs[:, :], tile_fs[:, :], float(T - 1), None, ALU.min))
                then(dve.memset(ids[:, :], 0))
                then(dve.tensor_copy(ids[:, 0:SUPER], tile_fs[:, :]))
                for b in range(T):
                    then(dve.tensor_scalar(mask[:, :], tile_f[:, :], float(b), None, ALU.is_equal))
                    then(dve.tensor_tensor_scan(work[:, :], ones[:, :], mask[:, :], base[:, b:b + 1], ALU.mult, ALU.add))
                    then(dve.copy_predicated(slot[:, :], mask[:, :], work[:, :]))
                then(dve.tensor_scalar(work[:, :], slot[:, :], -1.0, None, ALU.add))
                then(dve.tensor_copy(whole[:, :], work[:, :]))
                then(dve.tensor_scalar(mask[:, :], whole[:, :], 127, None, ALU.bitwise_and))
                then(dve.tensor_scalar(whole[:, :], whole[:, :], 7, None, ALU.arith_shift_right))
                then(dve.tensor_copy(work[:, :], mask[:, :]))
                then(dve.tensor_copy(dst_f[:, :], whole[:, :]))
                then(dve.scalar_tensor_tensor(out=work[:, :], in0=work[:, :], scalar=float(cols), in1=dst_f[:, :], op0=ALU.mult, op1=ALU.add))
                then(dve.tensor_copy(row[:, :], work[:, :]))
                then(dve.tensor_scalar(mask[:, :], tile_f[:, :], float(T), None, ALU.is_ge))
                then(dve.copy_predicated(row[:, :], mask[:, :], spare[:, :]))
                then(dve.tensor_scalar(mask[:, :], tile_f[:, :], 0.0, None, ALU.is_lt))
                then(dve.copy_predicated(row[:, :], mask[:, :], spare[:, :]))
                dve.wait_ge(filled, 16)
                for u in range(4):
                    dve.tensor_copy(ring_row[:, u, :], row[:, u:u + 1])
                    dve.tensor_copy(ring_load[:, u, :], load[:, u, :]).then_inc(staged, 1)
                with dve.Fori(1, J // 4) as i:
                    for u in range(4):
                        dve.wait_ge(scattered[u], i * 16)
                        dve.tensor_copy(ring_row[:, u, :], row[:, bass.ds(i * 4 + u, 1)])
                        dve.tensor_copy(ring_load[:, u, :], load[:, bass.ds(i * 4 + u, 1), :].rearrange("p a f -> p (a f)")).then_inc(staged, 1)


def edge_pass(nc, edge, table, kind, H, dv, row_width, per_target, scores, state, const, name):
    SUPER = edge["cols"] // 2
    W = H * (dv + 1) if kind != "sum" else row_width
    count_targets = kind == "dot"
    WA = W + (1 if count_targets else 0)
    QW = {"dot": D, "add": H, "mix": 0, "sum": 0}[kind]
    soft = kind != "sum"
    with Scope(nc, name) as k:
        sb, ps, sem = k.sb, k.ps, k.sem

        ids = edge["tile_of"]
        source = sb("source", [128, 2, 2], I32)
        rows = sb("rows", [128, 2, 2, row_width])
        hot = sb("hot", [128, 2, 2, NP])
        hot_ps = ps("hot_ps", [128, 4, 128])
        sum_ps = ps("sum_ps", [128, 512])
        source_read, sources, gathered = sem("source_read"), sem("sources"), [k.own_sem("gathered0"), k.own_sem("gathered1")]
        hot_ready, sum_ready, acc_done = sem("hot_ready"), sem("sum_ready"), sem("acc_done")
        if soft:
            hotT = sb("hotT", [128, 2, 2, 128])
            away = sb("away", [128, 2, NP], BF16)
            score = sb("score", [128, 2, 2, H])
            prod = sb("prod", [128, 2, D])
            diag = sb("diag", [128, 2, H, 128])
            below = sb("below", [128, 2, H])
            local = sb("local", [128, H])
            raised = sb("raised", [128, 2, H])
            drop = sb("drop", [128, H])
            scale = sb("scale", [128, 2, H])
            msg = sb("msg", [128, 2, 2, WA])
            mixed = sb("mixed", [128, 2, 64])
            gap = sb("gap", [128, 2, H])
            term = sb("term", [128, 2, H])
            scaled = sb("scaled", [128, W])
            own_ps = ps("own_ps", [128, 2, 256])
            back_ps = ps("back_ps", [128, 2, 256])
            max_ps = ps("max_ps", [128, 2, H * 128])
            (turned, turned_sb, own_ready, diag_ready, max_ready, new_max, max_back, below_ready, drop_ready,
             weight_ready, scale_ready, msg_ready, chain) = (sem(n) for n in (
                 "turned", "turned_sb", "own_ready", "diag_ready", "max_ready", "new_max", "max_back",
                 "below_ready", "drop_ready", "weight_ready", "scale_ready", "msg_ready", "chain"))
        rows_free = sem("rows_free")
        acc, run = state["acc"], state.get("m")

        with nc.Block() as block:
            @block.gpsimd
            def _(pool):
                def gather(s, u, turn):
                    pool.wait_ge(rows_free, s + 1)
                    pool.tensor_copy(source[:, u, :], edge["data"][:, bass.ds(2 * s, 2), 0].bitcast(I32)).then_inc(sources, 1)
                    pool.wait_ge(sources, s + 1)
                    pool.nop(nofuse=True)
                    for q in range(2):
                        pool.indirect_dma_start(rows[:, u, q, :], None, table, bass.IndirectOffsetOnAxis(ap=source[:, u, q:q + 1], axis=0)).then_inc(gathered[u], 16)

                gather(0, 0, 1)
                with pool.Fori(0, SUPER // 2) as i:
                    gather(2 * i + 1, 1, i + 1)
                    gather(2 * i + 2, 0, i + 2)

            @block.tensor
            def _(pe):
                def turn(s, u):
                    pe.wait_ge(hot_ready, s + 1)
                    for q in range(2):
                        ins = pe.transpose(hot_ps[0:NP, q, :], hot[:, u, q, :], const["eye"][:, :])
                    ins.then_inc(turned, 1)

                def own(s, u):
                    pe.wait_ge(turned_sb, s + 1)
                    if QW:
                        t = pe.value_load(ids[0:1, bass.ds(s, 1)], min_val=0, max_val=T - 1)
                        for q in range(2):
                            ins = pe.matmul(own_ps[:, q, 0:QW], hotT[0:NP, u, q, :], per_target[0:NP, bass.ds(t, 1), :].rearrange("p a w -> p (a w)"), start=True, stop=True)
                        ins.then_inc(own_ready, 1)

                def spread(s, u):
                    pe.wait_ge(diag_ready, s + 1)
                    for q in range(2):
                        for h in range(0, H, 4):
                            pe.matmul(max_ps[0:NP, q, h * 128:(h + 4) * 128], hot[:, u, q, :], diag[:, q, h:h + 4, :].rearrange("p h e -> p (h e)"), start=True, stop=False)
                            ins = pe.matmul(max_ps[0:NP, q, h * 128:(h + 4) * 128], away[:, q, :], const["eye4_bf"][:, :], start=False, stop=True)
                    ins.then_inc(max_ready, 1)

                def maxima(s, u):
                    pe.wait_ge(new_max, s + 1)
                    for q in range(2):
                        ins = pe.matmul(back_ps[:, q, 0:H], hotT[0:NP, u, q, :], raised[0:NP, u, :], start=True, stop=True)
                    ins.then_inc(max_back, 1)

                def total(s, u):
                    if soft:
                        pe.wait_ge(msg_ready, s + 1)
                    else:
                        pe.wait_ge(hot_ready, s + 1)
                        pe.wait_ge(rows_free, s + 2)
                    for q in range(2):
                        ins = pe.matmul(sum_ps[0:NP, 0:WA], hot[:, u, q, :], msg[:, u, q, :] if soft else rows[:, u, q, :], start=(q == 0), stop=(q == 1))
                    ins.then_inc(sum_ready, 1)

                if soft:
                    turn(0, 0)
                    own(0, 0)
                with pe.Fori(0, SUPER // 2) as i:
                    for u in range(2):
                        s = 2 * i + u
                        if soft:
                            spread(s, u)
                            turn(s + 1, 1 - u)
                            own(s + 1, 1 - u)
                            maxima(s, u)
                        else:
                            pe.wait_ge(gathered[u], 32 * (i + 1))
                        total(s, u)

            @block.scalar
            def _(act):
                if not soft:
                    return

                def turned_copy(s, u):
                    act.wait_ge(turned, s + 1)
                    act.copy(hotT[0:NP, u, :, :], hot_ps[0:NP, 0:2, :]).then_inc(turned_sb, 1)

                turned_copy(0, 0)
                with act.Fori(0, SUPER // 2) as i:
                    for u in range(2):
                        s = 2 * i + u
                        turned_copy(s + 1, 1 - u)
                        act.wait_ge(drop_ready, s + 1)
                        act.activation(scale[0:NP, u, :], drop[0:NP, :], ACT.Exp).then_inc(scale_ready, 1)
                        act.wait_ge(below_ready, s + 1)
                        act.activation(msg[:, u, :, 0:W].rearrange("p q (h v) -> p q h v", h=H)[:, :, :, dv], below[:, :, :], ACT.Exp).then_inc(weight_ready, 1)

            @block.vector
            def _(dve):
                def one_hot(s, u):
                    dve.tensor_tensor(hot[:, u, :, :], const["ramp"][:, 0:NP].unsqueeze(1).to_broadcast([128, 2, NP]),
                                      edge["data"][:, bass.ds(2 * s, 2), 1:2].to_broadcast([128, 2, NP]), ALU.is_equal).then_inc(hot_ready, 1)

                def keep_away(s, u):
                    dve.wait_ge(hot_ready, s + 1)
                    dve.tensor_scalar(away[:, :, :], hot[:, u, :, :], 1.0, FAR, ALU.subtract, ALU.mult).then_inc(chain, 1)

                def scores_of(s, u, turn):
                    dve.wait_ge(gathered[u], 32 * turn)
                    to = score[:, u, :, :]
                    if kind == "dot":
                        dve.wait_ge(own_ready, s + 1)
                        dve.tensor_tensor(prod[:, :, :], own_ps[:, :, :], rows[:, u, :, 0:D], ALU.mult)
                        dve.drain()
                        dve.reduce_sum(term[:, :, :], prod[:, :, :].rearrange("p q (h e) -> p q h e", h=H), axis=AX.X)
                        dve.drain()
                        dve.tensor_scalar(to, term[:, :, :], scores, None, ALU.mult)
                    elif kind == "add":
                        dve.wait_ge(own_ready, s + 1)
                        dve.tensor_tensor(term[:, :, :], own_ps[:, :, 0:H], rows[:, u, :, H * dv:H * dv + H], ALU.add)
                        dve.drain()
                        dve.scalar_tensor_tensor(out=to, in0=term[:, :, :], scalar=scores, in1=term[:, :, :], op0=ALU.mult, op1=ALU.max)
                    else:
                        part = [edge["data"][:, bass.ds(2 * s, 2), c:c + 1].to_broadcast([128, 2, H]) for c in (2, 3)]
                        dve.tensor_tensor(term[:, :, :], rows[:, u, :, 2 * dv:2 * dv + H], part[0], ALU.mult)
                        dve.tensor_tensor(prod[:, :, 0:H], rows[:, u, :, 2 * dv + H:2 * dv + 2 * H], part[1], ALU.mult)
                        dve.drain()
                        dve.tensor_tensor(prod[:, :, H:2 * H], term[:, :, :], prod[:, :, 0:H], ALU.add)
                        dve.drain()
                        dve.scalar_tensor_tensor(out=to, in0=prod[:, :, H:2 * H], scalar=scores, in1=prod[:, :, H:2 * H], op0=ALU.mult, op1=ALU.max)

                def diagonals(s, u):
                    for q in range(2):
                        ins = dve.tensor_tensor(diag[:, q, :, :], score[:, u, q, :].unsqueeze(2).to_broadcast([128, H, 128]),
                                                const["eye"][:, :].unsqueeze(1).to_broadcast([128, H, 128]), ALU.mult)
                    ins.then_inc(diag_ready, 1)

                def raise_max(s, u, t):
                    dve.wait_ge(max_ready, s + 1)
                    dve.tensor_reduce(local[0:NP, :], max_ps[0:NP, :, :].rearrange("p q (h e) -> p h q e", h=H), AX.XY, ALU.max)
                    dve.drain()
                    at = run[0:NP, bass.ds(t, 1), :].rearrange("p a h -> p (a h)")
                    dve.tensor_tensor(raised[0:NP, u, :], at, local[0:NP, :], ALU.max).then_inc(new_max, 1)
                    dve.wait_ge(new_max, s + 1)
                    dve.tensor_tensor(drop[0:NP, :], at, raised[0:NP, u, :], ALU.subtract).then_inc(drop_ready, 1)
                    dve.drain()
                    dve.tensor_copy(at, raised[0:NP, u, :])

                def weigh(s, u):
                    dve.wait_ge(max_back, s + 1)
                    dve.tensor_tensor(gap[:, :, :], score[:, u, :, :], back_ps[:, :, 0:H], ALU.subtract)
                    dve.drain()
                    dve.tensor_scalar(below[:, :, :], gap[:, :, :], 0.0, None, ALU.min).then_inc(below_ready, 1)

                def message(s, u):
                    dve.wait_ge(weight_ready, s + 1)
                    for q in range(2):
                        m = msg[:, u, q, 0:W].rearrange("p (h v) -> p h v", h=H)
                        weight = m[:, :, dv:dv + 1].to_broadcast([128, H, dv])
                        if kind == "mix":
                            dve.tensor_scalar(prod[:, q, 0:dv], rows[:, u, q, 0:dv], edge["data"][:, bass.ds(2 * s + q, 1), 2], None, ALU.mult)
                            dve.drain()
                            dve.scalar_tensor_tensor(out=mixed[:, q, :], in0=rows[:, u, q, dv:2 * dv], scalar=edge["data"][:, bass.ds(2 * s + q, 1), 3],
                                                     in1=prod[:, q, 0:dv], op0=ALU.mult, op1=ALU.add)
                            dve.drain()
                            values = mixed[:, q, :].unsqueeze(1).to_broadcast([128, H, dv])
                        else:
                            a = D if kind == "dot" else 0
                            values = rows[:, u, q, a:a + H * dv].rearrange("p (h v) -> p h v", h=H)
                        ins = dve.tensor_tensor(m[:, :, 0:dv], values, weight, ALU.mult)
                    ins.then_inc(msg_ready, 1)

                def accumulate(s, u, t):
                    at = acc[0:NP, bass.ds(t, 1), :].rearrange("p a w -> p (a w)")
                    if soft:
                        dve.wait_ge(scale_ready, s + 1)
                        dve.tensor_tensor(scaled[0:NP, :].rearrange("p (h v) -> p h v", h=H), at[:, 0:W].rearrange("p (h v) -> p h v", h=H),
                                          scale[0:NP, u, :].unsqueeze(2).to_broadcast([NP, H, dv + 1]), ALU.mult)
                        dve.drain()
                        dve.wait_ge(sum_ready, s + 1)
                        ins = dve.tensor_tensor(at[:, 0:W], scaled[0:NP, :], sum_ps[0:NP, 0:W], ALU.add)
                        if count_targets:
                            ins = dve.tensor_tensor(at[:, W:WA], at[:, W:WA], sum_ps[0:NP, W:WA], ALU.add)
                    else:
                        dve.wait_ge(sum_ready, s + 1)
                        ins = dve.tensor_tensor(at, at, sum_ps[0:NP, 0:WA], ALU.add)
                    ins.then_inc(rows_free, 1)

                if count_targets:
                    dve.memset(msg[:, :, :, W:WA], 1.0)
                dve.memset(hot[:, 0, :, :], 0.0).then_inc(rows_free, 1)
                dve.memset(hot[:, 1, :, :], 0.0).then_inc(rows_free, 1)
                dve.drain()
                one_hot(0, 0)
                if soft:
                    keep_away(0, 0)
                    scores_of(0, 0, 1)
                    dve.drain()
                    diagonals(0, 0)
                with dve.Fori(0, SUPER // 2) as i:
                    for u in range(2):
                        s = 2 * i + u
                        t = dve.value_load(ids[0:1, bass.ds(s, 1)], min_val=0, max_val=T - 1)
                        one_hot(s + 1, 1 - u)
                        if soft:
                            raise_max(s, u, t)
                            scores_of(s + 1, 1 - u, i + 1 + u)
                            weigh(s, u)
                            keep_away(s + 1, 1 - u)
                            message(s, u)
                            diagonals(s + 1, 1 - u)
                        accumulate(s, u, t)
                if not soft:
                    return



CHUNKS = [(c * 500, 500) for c in range(6)] + [(3000, 125)]
TILES = [range(c * 4, min(c * 4 + 4, T)) for c in range(7)]


def flat(ap):
    return ap.rearrange("p a b -> p (a b)")


def along(row, parts):
    return row.unsqueeze(0).to_broadcast([parts] + list(row.shape))


def on_vector(nc, name, steps, loads=(), stores=(), roots=()):
    with Scope(nc, name) as k:
        asked, given = k.sem("asked"), k.sem("given")
        turn = [0]

        def root(dve):
            turn[0] += 1
            dve.drain().then_inc(asked, 1)
            dve.wait_ge(given, turn[0])

        loaded, done, stored = k.sem("loaded"), k.sem("done"), k.sem("stored")
        with nc.Block() as block:
            @block.sync
            def _(sp):
                for to, of in loads:
                    sp.dma_start(to, of).then_inc(loaded, 16)
                if stores:
                    sp.wait_ge(done, 1)
                    for to, of in stores:
                        sp.dma_start(to, of).then_inc(stored, 16)
                    sp.wait_ge(stored, 16 * len(stores))

            @block.vector
            def _(dve):
                if loads:
                    dve.wait_ge(loaded, 16 * len(loads))
                if roots:
                    steps(dve, root)
                else:
                    steps(dve)
                dve.drain().then_inc(done, 1)

            @block.scalar
            def _(act):
                for n, at in enumerate(roots):
                    act.wait_ge(asked, n + 1)
                    act.activation(at, at, ACT.Sqrt).then_inc(given, 1)


def tile_norm(nc, x, out, name, width=D, gain=None, shift=None, eps=1e-5, groups=1, add_to=None, tiles=T, square=None):
    G = groups
    with Scope(nc, name) as k:
        mean, var = k.sb("mean", [128, tiles, G]), k.sb("var", [128, tiles, G])
        if square is None:
            square = k.sb("square", [128, tiles, G * width])
        loads = []
        if gain is not None:
            g_row, b_row = k.sb("gain", [128, gain.shape[-1]]), k.sb("shift", [128, gain.shape[-1]])
            loads = [(g_row[0:NP, :], along(gain, NP)), (b_row[0:NP, :], along(shift, NP))]
        cut = [lambda a: a[0:NP, :, :].rearrange("p t (g w) -> p (t g) w", g=G)][0]
        wide = [NP, tiles * G, width]
        m, v = flat(mean[0:NP, :, :]), flat(var[0:NP, :, :])

        def steps(dve, root):
            dve.reduce_sum(m, cut(x), axis=AX.X)
            dve.drain()
            dve.tensor_scalar(m, m, 1.0 / width, None, ALU.mult)
            dve.drain()
            dve.tensor_tensor(cut(out), cut(x), m.unsqueeze(2).to_broadcast(wide), ALU.subtract)
            dve.drain()
            dve.tensor_tensor(cut(square), cut(out), cut(out), ALU.mult)
            dve.drain()
            dve.reduce_sum(v, cut(square), axis=AX.X)
            dve.drain()
            dve.tensor_scalar(v, v, 1.0 / width, eps, ALU.mult, ALU.add)
            root(dve)
            dve.reciprocal(v, v)
            dve.drain()
            dve.tensor_tensor(cut(out), cut(out), v.unsqueeze(2).to_broadcast(wide), ALU.mult)
            dve.drain()
            if gain is not None:
                if gain.shape[-1] == width and G > 1:
                    rows = [r[0:NP, :].unsqueeze(1).to_broadcast(wide) for r in (g_row, b_row)]
                    view = cut(out)
                else:
                    rows = [r[0:NP, :].unsqueeze(1).to_broadcast([NP, tiles, G * width]) for r in (g_row, b_row)]
                    view = out[0:NP, :, :]
                dve.tensor_tensor(view, view, rows[0], ALU.mult)
                dve.drain()
                dve.tensor_tensor(view, view, rows[1], ALU.add)
                dve.drain()
            if add_to is not None:
                dve.tensor_tensor(add_to[0:NP, :, :], add_to[0:NP, :, :], out[0:NP, :, :], ALU.add)

        on_vector(nc, name, steps, loads, roots=[v])


def turn_rows(nc, rows, turned, const, name, halves=2):
    with Scope(nc, name) as k:
        bank = [k.ps(f"bank{b}", [128, 4, 128]) for b in range(4)]
        made, copied = k.sem("made"), [k.sem("copied_act"), k.sem("copied_dve")]
        jobs = [(h, c) for h in range(halves) for c in range(7)]
        with nc.Block() as block:
            @block.tensor
            def _(pe):
                for n, (h, c) in enumerate(jobs):
                    if n >= 4:
                        pe.wait_ge(copied[n % 2], (n - 4) // 2 + 1)
                    for j, t in enumerate(TILES[c]):
                        ins = pe.transpose(bank[n % 4][:, j, 0:NP], rows[0:NP, t, h * 128:(h + 1) * 128], const["eye"][0:NP, 0:NP])
                    ins.then_inc(made, 1)

            def copies(eng, which, copy):
                for n, (h, c) in enumerate(jobs):
                    if n % 2 != which:
                        continue
                    eng.wait_ge(made, n + 1)
                    m = len(TILES[c])
                    copy(turned[:, h, CHUNKS[c][0]:CHUNKS[c][0] + m * NP].rearrange("p (j n) -> p j n", n=NP), bank[n % 4][:, 0:m, 0:NP]).then_inc(copied[which], 1)

            @block.scalar
            def _(act):
                copies(act, 0, act.copy)

            @block.vector
            def _(dve):
                copies(dve, 1, dve.tensor_copy)


def project(nc, parts, weights, cols, put, name, bias=None, loads=(), last=None, weights_sb=None, bias_sb=None):
    with Scope(nc, name) as k:
        K = len(parts)
        pk = parts[0].shape[0]
        w = weights_sb if weights_sb is not None else k.sb("w", [pk, K, cols])
        banks = [k.ps(f"bank{b}", [128, 512]) for b in range(4)]
        b_row = bias_sb
        if bias is not None:
            b_row = k.sb("b", [128, cols])
        loaded, made, used = k.sem("loaded"), k.sem("made"), k.sem("used")
        todo = list(loads)
        if weights is not None:
            todo.append((w[:, :, :], weights.rearrange("(k p) n -> p k n", p=pk)))
        if bias is not None:
            todo.append((b_row[0:NP, :], along(bias, NP)))
        with nc.Block() as block:
            @block.sync
            def _(sp):
                for to, of in todo:
                    sp.dma_start(to, of).then_inc(loaded, 16)

            @block.tensor
            def _(pe):
                if todo:
                    pe.wait_ge(loaded, 16 * len(todo))
                for t in range(T):
                    if t >= 4:
                        pe.wait_ge(used, t - 3)
                    for q in range(K):
                        ins = pe.matmul(banks[t % 4][0:NP, 0:cols], parts[q][:, t * NP:(t + 1) * NP], w[:, q, 0:cols], start=(q == 0), stop=(q == K - 1))
                    ins.then_inc(made, 1)

            @block.vector
            def _(dve):
                if todo:
                    dve.wait_ge(loaded, 16 * len(todo))
                for t in range(T):
                    dve.wait_ge(made, t + 1)
                    put(dve, t, banks[t % 4][0:NP, 0:cols], b_row[0:NP, 0:cols] if b_row is not None else None).then_inc(used, 1)
                if last is not None:
                    dve.drain()
                    last(dve)


def put_rows(to, add=None):
    def put(dve, t, bank, bias):
        at = to[0:NP, t, 0:bank.shape[-1]]
        if bias is not None:
            if add is None:
                return dve.tensor_tensor(at, bank, bias, ALU.add)
            dve.tensor_tensor(at, add[0:NP, t, :], bias, ALU.add)
            dve.drain()
            return dve.tensor_tensor(at, bank, at, ALU.add)
        if add is not None:
            return dve.tensor_tensor(at, bank, add[0:NP, t, :], ALU.add)
        return dve.tensor_copy(at, bank)
    return put


def perceptron(nc, parts, layers, E, func, y, name, gates=None, affine=None):
    KIN = len(parts)
    dims = [KIN * 128] + [l[0].shape[-1] for l in layers]
    hidden = len(layers) - 1
    SLOTS = 1 if E == 1 else 2
    blocks = [max(1, d // 128) for d in dims]
    size = [min(128, d) for d in dims]
    BANKS = 4
    MADE = 7 * sum(blocks[1:-1])
    with Scope(nc, name) as k:
        w = [[k.sb(f"w{l}_{s}", [size[l], blocks[l], dims[l + 1]]) for l in range(len(layers))] for s in range(SLOTS)]
        b = [[k.sb(f"b{l}_{s}", [size[l + 1], blocks[l + 1]]) for l in range(hidden)] for s in range(SLOTS)]
        b_last = [k.sb(f"b_last{s}", [128, D]) for s in range(SLOTS)]
        h = [[k.sb(f"h{l}_{c}", [size[l], blocks[l], 500]) for c in range(2)] for l in range(1, hidden + 1)]
        biased = k.sb("biased", [128, 2, D])
        own = own_gb = None
        if affine is not None:
            own = [k.sb(f"own{c}", [128, KIN, 500]) for c in range(2)]
            own_gb = [k.sb(f"own_gb{s}", [128, 2, KIN]) for s in range(SLOTS)]
        h_bank = [k.ps(f"h_bank{n}", [128, 512]) for n in range(BANKS)]
        y_bank = [k.ps(f"y_bank{n}", [128, 512]) for n in range(2)]
        loaded = [k.sem(f"loaded{s}") for s in range(SLOTS)]
        h_made, h_ready, y_made, y_free, y_added, own_ready = (k.sem(n) for n in ("h_made", "h_ready", "y_made", "y_free", "y_added", "own_ready"))
        NL = 2 * len(layers) + (2 if affine is not None else 0)
        BODY = SLOTS
        flow = [(s, c) for s in range(BODY) for c in range(7)]

        def nth_hidden(f, l, m):
            return order.index((f, l, m))

        order = []
        for f in range(len(flow)):
            for ff, l in ([(0, 1)] if f == 0 else []) + ([(f + 1, 1)] if f + 1 < len(flow) else []) + [(f, l) for l in range(2, hidden + 1)]:
                order += [(ff, l, m) for m in range(blocks[l])]

        def loop(eng, body, start=0):
            if E == 1:
                body(0)
            elif start < E // 2:
                with eng.Fori(start, E // 2) as i:
                    body(i)

        with nc.Block() as block:
            @block.sync
            def _(sp):
                def load(i, s):
                    e = i * BODY + s if E > 1 else 0
                    for l in range(len(layers)):
                        wd, bd = layers[l]
                        sp.dma_start(w[s][l][:, :, :], wd[bass.ds(e, 1), :, :].rearrange("a (k p) n -> p (a k) n", p=size[l])).then_inc(loaded[s], 16)
                        if l < hidden:
                            sp.dma_start(b[s][l][:, :], bd[bass.ds(e, 1), :, :].rearrange("a p k -> p (a k)")).then_inc(loaded[s], 16)
                        else:
                            sp.dma_start(b_last[s][0:NP, :].unsqueeze(1), bd[bass.ds(e, 1), :].unsqueeze(0).to_broadcast([NP, 1, D])).then_inc(loaded[s], 16)
                    if affine is not None:
                        for q in range(2):
                            sp.dma_start(own_gb[s][:, q, :], affine[q][bass.ds(e, 1), :, :].rearrange("a p k -> p (a k)")).then_inc(loaded[s], 16)

                for s in range(SLOTS):
                    load(0, s)

                def body(i):
                    for s in range(SLOTS):
                        sp.wait_ge(y_added, (i - 1) * BODY * T + T * (s + 1))
                        load(i, s)
                if E > 1:
                    loop(sp, body, 1)

            @block.tensor
            def _(pe):
                def make_hidden(i, f, l):
                    s, c = flow[f]
                    n0, n = CHUNKS[c]
                    for m in range(blocks[l]):
                        at = nth_hidden(f, l, m)
                        need = at + 1
                        if l > 1:
                            need = max(need, BANKS + nth_hidden(f, l - 1, blocks[l - 1] - 1) + 1)
                        pe.wait_ge(h_ready, i * MADE * BODY + need)
                        if l == 1 and m == 0 and affine is not None:
                            pe.wait_ge(own_ready, i * len(flow) + f + 1)
                        for q in range(blocks[l - 1]):
                            if l > 1:
                                of = h[l - 2][f % 2][:, q, 0:n]
                            elif affine is not None:
                                of = own[f % 2][:, q, 0:n]
                            else:
                                of = parts[q][:, n0:n0 + n]
                            ins = pe.matmul(h_bank[at % BANKS][0:size[l], 0:n], w[s][l - 1][:, q, m * 128:m * 128 + size[l]], of, start=(q == 0), stop=(q == blocks[l - 1] - 1))
                        ins.then_inc(h_made, 1)

                def body(i):
                    for f, (s, c) in enumerate(flow):
                        if c == 0:
                            pe.wait_ge(loaded[s], 16 * NL * (i + 1))
                        if f == 0:
                            make_hidden(i, 0, 1)
                        if f + 1 < len(flow):
                            if flow[f + 1][1] == 0:
                                pe.wait_ge(loaded[flow[f + 1][0]], 16 * NL * (i + 1))
                            make_hidden(i, f + 1, 1)
                        for l in range(2, hidden + 1):
                            make_hidden(i, f, l)
                        pe.wait_ge(h_ready, i * MADE * BODY + BANKS + nth_hidden(f, hidden, blocks[hidden] - 1) + 1)
                        for j, t in enumerate(TILES[c]):
                            n = s * T + t
                            pe.wait_ge(y_free, i * BODY * T + n + 1)
                            for q in range(blocks[hidden]):
                                ins = pe.matmul(y_bank[n % 2][0:NP, 0:D], h[hidden - 1][f % 2][:, q, j * NP:(j + 1) * NP], w[s][hidden][:, q, :], start=(q == 0), stop=(q == blocks[hidden] - 1))
                            ins.then_inc(y_made, 1)
                loop(pe, body)

            @block.scalar
            def _(act):
                act.sem_inc(h_ready, BANKS)

                def body(i):
                    for at, (f, l, m) in enumerate(order):
                        s, c = flow[f]
                        n = CHUNKS[c][1]
                        act.wait_ge(h_made, i * MADE * BODY + at + 1)
                        act.activation(h[l - 1][f % 2][:, m, 0:n], h_bank[at % BANKS][0:size[l], 0:n], func, bias=b[s][l - 1][:, m:m + 1]).then_inc(h_ready, 1)
                loop(act, body)

            @block.vector
            def _(dve):
                dve.sem_inc(y_free, 2)

                def own_input(i, f):
                    s, c = flow[f]
                    n0, n = CHUNKS[c]
                    for q in range(KIN):
                        ins = dve.tensor_scalar(own[f % 2][:, q, 0:n], parts[q][:, n0:n0 + n], own_gb[s][:, 0, q:q + 1], own_gb[s][:, 1, q:q + 1], ALU.mult, ALU.add)
                    ins.then_inc(own_ready, 1)

                def body(i):
                    if affine is not None:
                        dve.wait_ge(loaded[0], 16 * NL * (i + 1))
                        own_input(i, 0)
                        own_input(i, 1)
                    for f, (s, c) in enumerate(flow):
                        if c == 0:
                            dve.wait_ge(loaded[s], 16 * NL * (i + 1))
                        for t in TILES[c]:
                            n = s * T + t
                            dve.wait_ge(y_made, i * BODY * T + n + 1)
                            dve.tensor_tensor(biased[0:NP, n % 2, :], y_bank[n % 2][0:NP, 0:D], b_last[s][0:NP, :], ALU.add).then_inc(y_free, 1)
                            dve.drain()
                            to = y[0:NP, t, :]
                            if gates is not None:
                                e = i * BODY + s if E > 1 else 0
                                gate = flat(gates[0:NP, t:t + 1, bass.ds(e, 1)])
                                dve.scalar_tensor_tensor(out=to, in0=biased[0:NP, n % 2, :], scalar=gate, in1=to, op0=ALU.mult, op1=ALU.add).then_inc(y_added, 1)
                            else:
                                dve.tensor_tensor(to, to, biased[0:NP, n % 2, :], ALU.add).then_inc(y_added, 1)
                        if affine is not None and f + 2 < len(flow):
                            if flow[f + 2][1] == 0:
                                dve.wait_ge(loaded[flow[f + 2][0]], 16 * NL * (i + 1))
                            own_input(i, f + 2)
                loop(dve, body)


def gram(nc, left, right, out, name, m_cols=D, n_cols=D, extra=None):
    blocks = m_cols // 128
    with Scope(nc, name) as k:
        bank = [k.ps(f"bank{m}", [128, 512]) for m in range(blocks)]
        made = k.sem("made")
        with nc.Block() as block:
            @block.tensor
            def _(pe):
                for m in range(blocks):
                    for t in range(T):
                        ins = pe.matmul(bank[m][:, 0:n_cols], left[0:NP, t, m * 128:(m + 1) * 128], right[0:NP, t, 0:n_cols], start=(t == 0), stop=(t == T - 1 and extra is None))
                    if extra is not None:
                        ins = pe.matmul(bank[m][:, 0:n_cols], extra[0], extra[1], start=False, stop=True)
                    ins.then_inc(made, 1)

            @block.vector
            def _(dve):
                for m in range(blocks):
                    dve.wait_ge(made, m + 1)
                    dve.tensor_copy(out[:, m, 0:n_cols], bank[m][:, 0:n_cols])


def product(nc, left, right, out, name, bank_parts=128, scale=None):
    blocks = max(1, left[0].shape[-1] // 128)
    cols = right[0].shape[-1]
    rows = min(128, left[0].shape[-1])
    with Scope(nc, name) as k:
        bank = [k.ps(f"bank{m}", [128, 512]) for m in range(blocks)]
        made = k.sem("made")
        with nc.Block() as block:
            @block.tensor
            def _(pe):
                for m in range(blocks):
                    for q in range(len(left)):
                        ins = pe.matmul(bank[m][0:rows, 0:cols], left[q][:, m * 128:m * 128 + rows], right[q], start=(q == 0), stop=(q == len(left) - 1))
                    ins.then_inc(made, 1)

            @block.vector
            def _(dve):
                for m in range(blocks):
                    dve.wait_ge(made, m + 1)
                    if scale is None:
                        dve.tensor_copy(out[0:rows, m, 0:cols], bank[m][0:rows, 0:cols])
                    else:
                        dve.tensor_scalar(out[0:rows, m, 0:cols], bank[m][0:rows, 0:cols], scale, None, ALU.mult)


def keep_blocks(nc, mats, size, name, fill=0.0):
    with Scope(nc, name) as k:
        cut, cut2 = k.sem("cut"), k.sem("cut2")
        with nc.Block() as block:
            @block.gpsimd
            def _(pool):
                n = 0
                for row0, mat, cols in mats:
                    for b in range(0, cols, size):
                        v = mat[:, b:b + size]
                        pool.affine_select(out=v, in_=v, compare_op=ALU.is_ge, fill=fill, base=row0 - b, pattern=[[0, size]], channel_multiplier=1).then_inc(cut, 1)
                        n += 1
                        pool.wait_ge(cut, n)
                        pool.affine_select(out=v, in_=v, compare_op=ALU.is_ge, fill=fill, base=b + size - 1 - row0, pattern=[[0, size]], channel_multiplier=-1).then_inc(cut, 1)
                        n += 1


def top_two(dve, s, gt, eq, rank, keep, lower, E):
    wide = [NP, T, E, E]
    for t in range(T):
        mine = s[0:NP, t, :].unsqueeze(2).to_broadcast([NP, E, E])
        other = s[0:NP, t, :].unsqueeze(1).to_broadcast([NP, E, E])
        dve.tensor_tensor(gt[0:NP, t, :, :], other, mine, ALU.is_gt)
        dve.tensor_tensor(eq[0:NP, t, :, :], other, mine, ALU.is_equal)
    dve.drain()
    g, q = gt[0:NP, :, :, :].rearrange("p t e j -> p t (e j)"), eq[0:NP, :, :, :].rearrange("p t e j -> p t (e j)")
    dve.tensor_tensor(q, q, flat(lower[0:NP, :, :]).unsqueeze(1).to_broadcast([NP, T, E * E]), ALU.mult)
    dve.drain()
    dve.tensor_tensor(g, g, q, ALU.add)
    dve.drain()
    dve.reduce_sum(flat(rank[0:NP, :, :]), gt[0:NP, :, :, :].rearrange("p t e j -> p (t e) j"), axis=AX.X)
    dve.drain()
    dve.tensor_scalar(keep[0:NP, :, :], rank[0:NP, :, :], 2.0, None, ALU.is_lt)
    dve.drain()


def on_scalar(nc, name, steps):
    with nc.Block() as block:
        @block.scalar
        def _(act):
            steps(act)


def fill(nc, pairs):
    with nc.Block() as block:
        @block.vector
        def _(dve):
            for to, value in pairs:
                dve.memset(to, value)


def finish_heads(nc, acc, H, dv, out, name, eps=0.0, eps_rows=None):
    with Scope(nc, name) as k:
        inverse = k.sb("inverse", [128, T, H])

        def steps(dve):
            heads = acc[0:NP, :, 0:H * (dv + 1)].rearrange("p t (h v) -> p t h v", h=H)
            if eps_rows is None:
                dve.tensor_scalar(inverse[0:NP, :, :], heads[:, :, :, dv], eps, None, ALU.add)
            else:
                dve.tensor_tensor(inverse[0:NP, :, :], heads[:, :, :, dv], eps_rows[0:NP, :, :], ALU.add)
            dve.drain()
            dve.reciprocal(inverse[0:NP, :, :], inverse[0:NP, :, :])
            dve.drain()
            for t in range(T):
                dve.tensor_tensor(out[0:NP, t, 0:H * dv].rearrange("p (h v) -> p h v", h=H), heads[:, t, :, 0:dv], inverse[0:NP, t, :].unsqueeze(2).to_broadcast([NP, H, dv]), ALU.mult)

        on_vector(nc, name, steps)


def start_with_self(dve, acc, run, values, own, H, dv, tmp, slope=0.2):
    dve.scalar_tensor_tensor(out=run[0:NP, :, :], in0=own, scalar=slope, in1=own, op0=ALU.mult, op1=ALU.max)
    for t in range(T):
        at = acc[0:NP, t, 0:H * (dv + 1)].rearrange("p (h v) -> p h v", h=H)
        dve.tensor_copy(at[:, :, 0:dv], values[0:NP, t, 0:H * dv].rearrange("p (h v) -> p h v", h=H))
        dve.memset(at[:, :, dv:dv + 1], 1.0)


def add_rows(nc, to, of, name, also=None):
    def steps(dve):
        dve.tensor_tensor(to[0:NP, :, :], to[0:NP, :, :], of[0:NP, :, :], ALU.add)
        if also is not None:
            dve.drain()
            dve.tensor_tensor(to[0:NP, :, :], to[0:NP, :, :], also[0:NP, :, :], ALU.add)
    on_vector(nc, name, steps)


def table_rows(table):
    return table.rearrange("(t p) w -> p t w", p=NP)


def softmax_of(nc, s, E, name, keep=None, normal=True):
    with Scope(nc, name) as k:
        top = k.sb("top", [128, T])
        wide = [NP, T, E]

        def before(dve):
            dve.tensor_reduce(top[0:NP, :], s[0:NP, :, :], AX.X, ALU.max)
            dve.drain()
            dve.tensor_tensor(s[0:NP, :, :], s[0:NP, :, :], top[0:NP, :].unsqueeze(2).to_broadcast(wide), ALU.subtract)

        def after(dve):
            if keep is not None:
                dve.tensor_tensor(s[0:NP, :, :], s[0:NP, :, :], keep[0:NP, :, :], ALU.mult)
                dve.drain()
            normalise(dve, s, top, E)

        on_vector(nc, name + "_b", before)
        on_scalar(nc, name + "_e", lambda act: act.activation(s[0:NP, :, :], s[0:NP, :, :], ACT.Exp))
        on_vector(nc, name + "_a", after)


def normalise(dve, s, total, E):
    dve.reduce_sum(total[0:NP, :], s[0:NP, :, :], axis=AX.X)
    dve.drain()
    dve.reciprocal(total[0:NP, :], total[0:NP, :])
    dve.drain()
    dve.tensor_tensor(s[0:NP, :, :], s[0:NP, :, :], total[0:NP, :].unsqueeze(2).to_broadcast([NP, T, E]), ALU.mult)


def choose_two(nc, s, keep, lower, E, name):
    with Scope(nc, name) as k:
        gt, eq, rank = k.sb("gt", [128, T, E, E]), k.sb("eq", [128, T, E, E]), k.sb("rank", [128, T, E])
        on_vector(nc, name, lambda dve: top_two(dve, s, gt, eq, rank, keep, lower, E))


def node_norm(nc, x, square, gain, shift, const, name):
    with Scope(nc, name) as k:
        bank = [k.ps("bank0", [128, 512]), k.ps("bank1", [128, 512])]
        mean, rstd = k.sb("mean", [128, D]), k.sb("rstd", [128, D])
        g_row, b_row = k.sb("g", [128, D]), k.sb("b", [128, D])
        loaded, squared, summed = k.sem("loaded"), k.sem("squared"), k.sem("summed")
        asked, given = k.sem("asked"), k.sem("given")
        wide = [NP, T, D]
        with nc.Block() as block:
            @block.sync
            def _(sp):
                sp.dma_start(g_row[0:NP, :], along(gain, NP)).then_inc(loaded, 16)
                sp.dma_start(b_row[0:NP, :], along(shift, NP)).then_inc(loaded, 16)

            @block.tensor
            def _(pe):
                for n, of in enumerate((x, square)):
                    if n:
                        pe.wait_ge(squared, 1)
                    for t in range(T):
                        ins = pe.matmul(bank[n][0:NP, 0:D], const["ones"][0:NP, 0:NP], of[0:NP, t, :], start=(t == 0), stop=(t == T - 1))
                    ins.then_inc(summed, 1)

            @block.scalar
            def _(act):
                act.wait_ge(asked, 1)
                act.activation(rstd[0:NP, :], rstd[0:NP, :], ACT.Sqrt).then_inc(given, 1)

            @block.vector
            def _(dve):
                dve.wait_ge(summed, 1)
                dve.tensor_scalar(mean[0:NP, :], bank[0][0:NP, 0:D], 1.0 / N, None, ALU.mult)
                dve.drain()
                dve.tensor_tensor(x[0:NP, :, :], x[0:NP, :, :], mean[0:NP, :].unsqueeze(1).to_broadcast(wide), ALU.subtract)
                dve.drain()
                dve.tensor_tensor(square[0:NP, :, :], x[0:NP, :, :], x[0:NP, :, :], ALU.mult).then_inc(squared, 1)
                dve.wait_ge(summed, 2)
                dve.tensor_scalar(rstd[0:NP, :], bank[1][0:NP, 0:D], 1.0 / N, 1e-5, ALU.mult, ALU.add).then_inc(asked, 1)
                dve.wait_ge(given, 1)
                dve.reciprocal(rstd[0:NP, :], rstd[0:NP, :])
                dve.drain()
                dve.wait_ge(loaded, 32)
                dve.tensor_tensor(rstd[0:NP, :], rstd[0:NP, :], g_row[0:NP, :], ALU.mult)
                dve.drain()
                dve.tensor_tensor(x[0:NP, :, :], x[0:NP, :, :], rstd[0:NP, :].unsqueeze(1).to_broadcast(wide), ALU.mult)
                dve.drain()
                dve.tensor_tensor(x[0:NP, :, :], x[0:NP, :, :], b_row[0:NP, :].unsqueeze(1).to_broadcast(wide), ALU.add)


def rms_norm(nc, x, out, gain, name):
    with Scope(nc, name) as k:
        total, g_row = k.sb("total", [128, T]), k.sb("g", [128, D])

        def steps(dve, root):
            dve.tensor_tensor(out[0:NP, :, :], x[0:NP, :, :], x[0:NP, :, :], ALU.mult)
            dve.drain()
            dve.reduce_sum(total[0:NP, :], out[0:NP, :, :], axis=AX.X)
            dve.drain()
            dve.tensor_scalar(total[0:NP, :], total[0:NP, :], 1e-24, None, ALU.max)
            root(dve)
            dve.reciprocal(total[0:NP, :], total[0:NP, :])
            dve.drain()
            dve.tensor_scalar(total[0:NP, :], total[0:NP, :], float(D) ** 0.5, None, ALU.mult)
            dve.drain()
            dve.tensor_tensor(out[0:NP, :, :], x[0:NP, :, :], total[0:NP, :].unsqueeze(2).to_broadcast([NP, T, D]), ALU.mult)
            dve.drain()
            dve.tensor_tensor(out[0:NP, :, :], out[0:NP, :, :], g_row[0:NP, :].unsqueeze(1).to_broadcast([NP, T, D]), ALU.mult)

        on_vector(nc, name, steps, [(g_row[0:NP, :], along(gain, NP))], roots=[total[0:NP, :]])


def halves(xt):
    return [xt[:, 0, :], xt[:, 1, :]]


def experts(nc, xt, weights, E, func, y, name, **more):
    perceptron(nc, halves(xt) if not isinstance(xt, list) else xt, weights, E, func, y, name, **more)


def layer0_graph(nc, I, X, inv_deg, edge, const):
    with Scope(nc, "a") as k:
        A, Q = k.sb("A", [128, T, D]), k.sb("Q", [128, T, D])
        keys_values = nc.dram_tensor("a_table", (N, 2 * D), F32, kind="Internal").ap()
        tile_norm(nc, X, A, "a_norm")
        with Scope(nc, "a1") as j:
            XT = j.sb("XT", [128, 2, N])
            turn_rows(nc, A, XT, const, "a_turn")
            with Scope(nc, "am") as m:
                K, V = m.sb("K", [128, T, D]), m.sb("V", [128, T, D])
                VK, P1, P2 = m.sb("VK", [128, 2, D]), m.sb("P1", [128, 2, D]), m.sb("P2", [128, 2, D])
                wo, wq = m.sb("wo", [128, 2, D]), m.sb("wq", [128, 2, D])
                loads = [(wo[:, :, :], I["L0_mix_woT"].rearrange("(k p) n -> p k n", p=128)), (wq[:, :, :], I["L0_mix_wq"].rearrange("(k p) n -> p k n", p=128))]
                project(nc, halves(XT), I["L0_mix_wkT"], D, put_rows(K), "am_k", loads=loads)
                project(nc, halves(XT), I["L0_mix_wvT"], D, put_rows(V), "am_v")
                tile_norm(nc, K, K, "am_nk", width=64, groups=4, gain=I["L0_mix_ln_k_g"], shift=I["L0_mix_ln_k_b"], square=Q)
                tile_norm(nc, V, V, "am_nv", width=64, groups=4, gain=I["L0_mix_ln_v_g"], shift=I["L0_mix_ln_v_b"], square=Q)
                gram(nc, V, K, VK, "am_g")
                keep_blocks(nc, [(0, VK[:, 0, :], D), (128, VK[:, 1, :], D)], 64, "am_b")
                product(nc, halves(VK), halves(wo), P1, "am_p", scale=1.0 / N)
                product(nc, halves(wq), halves(P1), P2, "am_q")
                project(nc, halves(XT), None, D, put_rows(X, add=X), "am_x", bias=I["L0_mix_bo"], weights_sb=P2)
            project(nc, halves(XT), I["L0_gnn_Wq"], D, put_rows(Q), "a_q")
            with Scope(nc, "a2") as m:
                KV = m.sb("KV", [128, T, 2 * D])
                project(nc, halves(XT), I["L0_gnn_Wkv"], 2 * D, put_rows(KV), "a_kv")
                on_vector(nc, "a_store", lambda dve: None, stores=[(table_rows(keys_values), KV[0:NP, :, :])])
        with Scope(nc, "a3") as j:
            acc, run = j.sb("acc", [128, T, 8 * 33 + 1]), j.sb("run", [128, T, 8])
            fill(nc, [(acc[:, :, :], 0.0), (run[:, :, :], 0.0)])
            edge_pass(nc, edge, keys_values, "dot", 8, 32, 2 * D, Q, 32 ** -0.5, dict(acc=acc, m=run), const, "ae")
            finish_heads(nc, acc, 8, 32, Q, "a_fin", eps=1e-8)

            def degrees(dve, root):
                dve.tensor_scalar(inv_deg[0:NP, :], acc[0:NP, :, 264], 1.0, None, ALU.add)
                root(dve)
                dve.reciprocal(inv_deg[0:NP, :], inv_deg[0:NP, :])
            on_vector(nc, "a_deg", degrees, roots=[inv_deg[0:NP, :]])
        B = Q
        with Scope(nc, "a4") as j:
            XT = j.sb("XT", [128, 2, N])
            turn_rows(nc, B, XT, const, "a_turn2")
            project(nc, halves(XT), I["L0_gnn_Wo_w"], D, put_rows(B, add=A), "a_o", bias=I["L0_gnn_Wo_b"])
            tile_norm(nc, B, B, "a_n1", gain=I["L0_gnn_ln1_g"], shift=I["L0_gnn_ln1_b"])
            turn_rows(nc, B, XT, const, "a_turn3")
            experts(nc, XT, [(I["L0_gnn_ffn_w1"], I["L0_gnn_ffn_b1"]), (I["L0_gnn_ffn_w2"], I["L0_gnn_ffn_b2"])], 1, ACT.Gelu, B, "a_mlp")
            tile_norm(nc, B, B, "a_n2", gain=I["L0_gnn_ln2_g"], shift=I["L0_gnn_ln2_b"], add_to=X)


def layer0_experts(nc, I, X, edge, const, lower):
    with Scope(nc, "b") as k:
        XT, gates = k.sb("XT", [128, 2, N]), k.sb("gates", [128, T, 4])
        table = nc.dram_tensor("b_table", (N, 20), F32, kind="Internal").ap()
        with Scope(nc, "b1") as j:
            A = j.sb("A", [128, T, D])
            tile_norm(nc, X, A, "b_norm")
            turn_rows(nc, A, XT, const, "b_turn")
        with Scope(nc, "b2") as j:
            h, a_dst, own = j.sb("h", [128, T, 20]), j.sb("a_dst", [128, T, 4]), j.sb("own", [128, T, 4])
            acc, run, agg = j.sb("acc", [128, T, 20]), j.sb("run", [128, T, 4]), j.sb("agg", [128, T, 16])
            tmp = j.sb("tmp", [128, T, 16])
            att = j.sb("att", [128, 3, 16])
            keep = j.sb("keep", [128, T, 4])
            project(nc, halves(XT), I["L0_ffn_W_gat"], 16, put_rows(h), "b_h", loads=[(att[0:NP, n, :], along(I[v], NP)) for n, v in enumerate(("L0_ffn_att_src", "L0_ffn_att_dst", "L0_ffn_b_gat"))])

            def attention(dve):
                for n, to in enumerate((h[0:NP, :, 16:20], a_dst[0:NP, :, :])):
                    dve.tensor_tensor(tmp[0:NP, :, :], h[0:NP, :, 0:16], att[0:NP, n, :].unsqueeze(1).to_broadcast([NP, T, 16]), ALU.mult)
                    dve.drain()
                    dve.reduce_sum(to, tmp[0:NP, :, :].rearrange("p t (h e) -> p t h e", h=4), axis=AX.X)
                    dve.drain()
                dve.tensor_tensor(own[0:NP, :, :], h[0:NP, :, 16:20], a_dst[0:NP, :, :], ALU.add)
                dve.drain()
                start_with_self(dve, acc, run, h, own[0:NP, :, :], 4, 4, tmp)
            on_vector(nc, "b_att", attention, stores=[(table_rows(table), h[0:NP, :, :])])
            edge_pass(nc, edge, table, "add", 4, 4, 20, a_dst, 0.2, dict(acc=acc, m=run), const, "be")
            finish_heads(nc, acc, 4, 4, agg, "b_fin", eps=1e-16)
            on_vector(nc, "b_bias", lambda dve: dve.tensor_tensor(agg[0:NP, :, :], agg[0:NP, :, :], att[0:NP, 2, :].unsqueeze(1).to_broadcast([NP, T, 16]), ALU.add))
            tile_norm(nc, agg, agg, "b_n", width=16, gain=I["L0_ffn_ln_gamma"], shift=I["L0_ffn_ln_beta"])

            def score(dve):
                dve.reduce_sum(gates[0:NP, :, :], agg[0:NP, :, :].rearrange("p t (h e) -> p t e h", h=4), axis=AX.X)
                dve.drain()
                dve.tensor_scalar(gates[0:NP, :, :], gates[0:NP, :, :], 0.25, None, ALU.mult)
            on_vector(nc, "b_score", score)
            choose_two(nc, gates, keep, lower[4], 4, "b_two")
            softmax_of(nc, gates, 4, "b_soft", keep=keep)
        experts(nc, XT, [(I["L0_ffn_W1"], I["L0_ffn_b1"]), (I["L0_ffn_W2"], I["L0_ffn_b2"])], 4, ACT.Gelu, X, "b_mlp", gates=gates)


def elu_plus_one(nc, x, e, parts, name):
    cut = [a[0:parts, :, :] for a in (x, e)]
    on_vector(nc, name + "_a", lambda dve: dve.tensor_scalar(cut[1], cut[0], 0.0, None, ALU.min))
    on_scalar(nc, name + "_b", lambda act: act.activation(cut[1], cut[1], ACT.Exp))
    on_vector(nc, name + "_c", lambda dve: dve.scalar_tensor_tensor(out=cut[0], in0=cut[0], scalar=0.0, in1=cut[1], op0=ALU.max, op1=ALU.add))


def layer1_graph(nc, I, X, inv_deg, edge, const):
    with Scope(nc, "c") as k:
        XT = k.sb("XT", [128, 2, N])
        table = nc.dram_tensor("c_table", (N, D), F32, kind="Internal").ap()
        with Scope(nc, "c1") as j:
            A, acc = j.sb("A", [128, T, D]), j.sb("acc", [128, T, D])
            b_row = j.sb("b", [128, D])
            tile_norm(nc, X, A, "c_norm")
            turn_rows(nc, A, XT, const, "c_turn")
            project(nc, halves(XT), I["L1_gnn_WT"], D, lambda dve, t, bank, bias: dve.tensor_scalar(acc[0:NP, t, :], bank, inv_deg[0:NP, t:t + 1], None, ALU.mult), "c_h")
            on_vector(nc, "c_store", lambda dve: None, stores=[(table_rows(table), acc[0:NP, :, :])])
            edge_pass(nc, edge, table, "sum", 0, 0, D, None, None, dict(acc=acc), const, "ce")

            def close(dve):
                dve.tensor_tensor(acc[0:NP, :, :], acc[0:NP, :, :], inv_deg[0:NP, :].unsqueeze(2).to_broadcast([NP, T, D]), ALU.mult)
                dve.drain()
                dve.tensor_tensor(acc[0:NP, :, :], acc[0:NP, :, :], b_row[0:NP, :].unsqueeze(1).to_broadcast([NP, T, D]), ALU.add)
                dve.drain()
                dve.scalar_tensor_tensor(out=X[0:NP, :, :], in0=acc[0:NP, :, :], scalar=0.0, in1=X[0:NP, :, :], op0=ALU.max, op1=ALU.add)
                dve.drain()
                dve.tensor_tensor(X[0:NP, :, :], X[0:NP, :, :], A[0:NP, :, :], ALU.add)
            on_vector(nc, "c_close", close, [(b_row[0:NP, :], along(I["L1_gnn_b"], NP))])
        B, QT = k.sb("B", [128, T, D]), k.sb("QT", [128, 2, N])
        with Scope(nc, "c2") as j:
            V, G = j.sb("V", [128, T, D + 1]), j.sb("G", [128, 2, 264])
            with Scope(nc, "c3") as m:
                E = m.sb("E", [128, T, D])
                project(nc, halves(XT), I["L1_mix_Wq"], D, put_rows(B), "c_q")
                elu_plus_one(nc, B, E, NP, "c_eq")
                turn_rows(nc, B, QT, const, "c_tq")
                project(nc, halves(XT), I["L1_mix_Wk"], D, put_rows(B), "c_k")
                elu_plus_one(nc, B, E, NP, "c_ek")
                project(nc, halves(XT), I["L1_mix_Wv"], D, put_rows(V), "c_v")
                fill(nc, [(V[:, :, D:D + 1], 1.0)])
            gram(nc, B, V, G, "c_g", n_cols=D + 1)

            def denominators(dve):
                for m in range(2):
                    dve.tensor_copy(G[:, m, D + 1:264], G[:, m, D:D + 1].to_broadcast([128, 7]))
            on_vector(nc, "c_d", denominators)
            keep_blocks(nc, [(0, G[:, 0, :], D), (128, G[:, 1, :], D)], 32, "c_b")
            keep_head_columns(nc, G, 32, 8, D, "c_hc")
            inv = j.sb("inv", [128, 2, 8])

            def put(dve, t, bank, bias):
                dve.tensor_scalar(inv[0:NP, t % 2, :], bank[:, D:264], 1e-6, None, ALU.add)
                dve.drain()
                dve.reciprocal(inv[0:NP, t % 2, :], inv[0:NP, t % 2, :])
                dve.drain()
                return dve.tensor_tensor(B[0:NP, t, :].rearrange("p (h v) -> p h v", h=8), bank[:, 0:D].rearrange("p (h v) -> p h v", h=8), inv[0:NP, t % 2, :].unsqueeze(2).to_broadcast([NP, 8, 32]), ALU.mult)
            project(nc, halves(QT), None, 264, put, "c_m", weights_sb=G)
        turn_rows(nc, B, QT, const, "c_tm")
        project(nc, halves(QT), I["L1_mix_Wm"], D, put_rows(B), "c_wm")
        tile_norm(nc, B, B, "c_n1", gain=I["L1_mix_g1"], shift=I["L1_mix_b1"])
        turn_rows(nc, B, QT, const, "c_tn")
        fill(nc, [(B[:, :, :], 0.0)])
        experts(nc, halves(XT) + halves(QT), [(I["L1_mix_W1"], I["zeros512"]), (I["L1_mix_W2"], I["zeros256"])], 1, ACT.Relu, B, "c_mlp")
        tile_norm(nc, B, B, "c_n2", gain=I["L1_mix_g2"], shift=I["L1_mix_b2"], add_to=X)


def keep_head_columns(nc, mat, size, heads, col0, name):
    with Scope(nc, name) as k:
        cut = k.sem("cut")
        with nc.Block() as block:
            @block.gpsimd
            def _(pool):
                n = 0
                for m in range(2):
                    v = mat[:, m, col0:col0 + heads]
                    pool.affine_select(out=v, in_=v, compare_op=ALU.is_ge, fill=0.0, base=m * 128, pattern=[[-size, heads]], channel_multiplier=1).then_inc(cut, 1)
                    n += 1
                    pool.wait_ge(cut, n)
                    pool.affine_select(out=v, in_=v, compare_op=ALU.is_ge, fill=0.0, base=size - 1 - m * 128, pattern=[[size, heads]], channel_multiplier=-1).then_inc(cut, 1)
                    n += 1


def layer1_experts(nc, I, X, const, lower):
    with Scope(nc, "d") as k:
        XT, gates = k.sb("XT", [128, 2, N]), k.sb("gates", [128, T, 4])
        with Scope(nc, "d1") as j:
            A, keep = j.sb("A", [128, T, D]), j.sb("keep", [128, T, 4])
            tile_norm(nc, X, A, "d_norm")
            turn_rows(nc, A, XT, const, "d_turn")
            project(nc, halves(XT), I["L1_ffn_gW"], 4, put_rows(gates), "d_g", bias=I["L1_ffn_gb"])
            softmax_of(nc, gates, 4, "d_s1")
            choose_two(nc, gates, keep, lower[4], 4, "d_two")
            softmax_of(nc, gates, 4, "d_s2", keep=keep)
        experts(nc, XT, [(I["L1_ffn_sW1"], I["L1_ffn_sb1"]), (I["L1_ffn_sW2"], I["L1_ffn_sb2"]), (I["L1_ffn_sW3"], I["L1_ffn_sb3"])], 1, ACT.Relu, X, "d_shared")
        experts(nc, XT, [(I["L1_ffn_eW1"], I["L1_ffn_eb1"]), (I["L1_ffn_eW2"], I["L1_ffn_eb2"]), (I["L1_ffn_eW3"], I["L1_ffn_eb3"])], 4, ACT.Relu, X, "d_own", gates=gates)


def layer2_graph(nc, I, X, edge, const):
    with Scope(nc, "e") as k:
        XT = k.sb("XT", [128, 2, N])
        A = k.sb("A", [128, T, D])
        table = nc.dram_tensor("e_table", (N, 136), F32, kind="Internal").ap()
        tile_norm(nc, X, A, "e_norm")
        turn_rows(nc, A, XT, const, "e_turn")
        with Scope(nc, "e1") as j:
            W, f, r = j.sb("W", [128, 2, 136]), j.sb("f", [128, 2, 4]), j.sb("r", [128, 2, 4])
            wf, wr, at = j.sb("wf", [64, D]), j.sb("wr", [64, D]), j.sb("at", [64, 4])
            rows = j.sb("rows", [128, T, 136])
            on_vector(nc, "e_load", lambda dve: None, loads=[(wf[:, :], I["L2_gnn_W_forward"]), (wr[:, :], I["L2_gnn_W_reverse"]), (at[:, :], I["L2_gnn_attnT"]),
                                                         (W[:, :, 0:64], I["L2_gnn_WfT"].rearrange("(k p) n -> p k n", p=128)), (W[:, :, 64:128], I["L2_gnn_WrT"].rearrange("(k p) n -> p k n", p=128))])
            product(nc, [wf[:, :]], [at[:, :]], f, "e_f")
            product(nc, [wr[:, :]], [at[:, :]], r, "e_r")

            def columns(dve):
                dve.tensor_copy(W[:, :, 128:132], f[:, :, :])
                dve.tensor_copy(W[:, :, 132:136], r[:, :, :])
            on_vector(nc, "e_c", columns)
            project(nc, halves(XT), None, 136, put_rows(rows), "e_p", weights_sb=W)
            on_vector(nc, "e_store", lambda dve: None, stores=[(table_rows(table), rows[0:NP, :, :])])
        with Scope(nc, "e2") as j:
            acc, run, top = j.sb("acc", [128, T, 4 * 65]), j.sb("run", [128, T, 4]), j.sb("top", [128, 4])
            res = j.sb("res", [128, T, D])
            fill(nc, [(acc[:, :, :], 0.0), (run[:, :, :], -FAR)])
            edge_pass(nc, edge, table, "mix", 4, 64, 136, None, 0.2, dict(acc=acc, m=run), const, "ee")
            every_max(nc, run, top, const, "e_max")

            def relative(dve):
                dve.tensor_tensor(run[0:NP, :, :], top[0:NP, :].unsqueeze(1).to_broadcast([NP, T, 4]), run[0:NP, :, :], ALU.subtract)
                dve.drain()
                dve.tensor_scalar(run[0:NP, :, :], run[0:NP, :, :], 80.0, None, ALU.min)
            on_vector(nc, "e_rel", relative)
            on_scalar(nc, "e_exp", lambda act: act.activation(run[0:NP, :, :], run[0:NP, :, :], ACT.Exp))
            on_vector(nc, "e_eps", lambda dve: dve.tensor_scalar(run[0:NP, :, :], run[0:NP, :, :], 1e-10, None, ALU.mult))
            finish_heads(nc, acc, 4, 64, res, "e_fin", eps_rows=run)
            add_rows(nc, X, res, "e_add")
        B, C = k.sb("B", [128, T, D]), k.sb("C", [128, T, D])
        with Scope(nc, "e3") as j:
            G, PT, M = j.sb("G", [128, 2, D]), j.sb("PT", [128, 2, D]), j.sb("M", [128, 2, D])
            wq, bq, bq_wide, bq_row = j.sb("wq", [128, 2, D]), j.sb("bq", [128, 2]), j.sb("bq_wide", [128, 2, 128]), j.sb("bq_row", [128, 1, D])
            top, total = j.sb("top", [128, 2]), j.sb("total", [128, 2])
            project(nc, halves(XT), I["L2_mix_wk"], D, put_rows(B), "e_k", bias=I["L2_mix_bk"],
                    loads=[(wq[:, :, :], I["L2_mix_wqT"].rearrange("(k p) n -> p k n", p=128)), (bq[:, :], I["L2_mix_bq"])])
            project(nc, halves(XT), I["L2_mix_wv"], D, put_rows(C), "e_v", bias=I["L2_mix_bv"])
            gram(nc, B, C, G, "e_g")
            on_vector(nc, "e_sc", lambda dve: dve.tensor_scalar(G[:, :, :], G[:, :, :], 64 ** -0.5, None, ALU.mult))
            keep_blocks(nc, [(0, G[:, 0, :], D), (128, G[:, 1, :], D)], 64, "e_b", fill=-FAR)

            def less_top(dve):
                dve.tensor_reduce(top[:, :], G[:, :, :], AX.X, ALU.max)
                dve.memset(PT[:, :, :], 0.0)
                dve.drain()
                dve.tensor_tensor(G[:, :, :], G[:, :, :], top[:, :].unsqueeze(2).to_broadcast([128, 2, D]), ALU.subtract)
                for m in range(2):
                    dve.tensor_copy(bq_wide[:, m, :], bq[:, m:m + 1].to_broadcast([128, 128]))
            on_vector(nc, "e_s1", less_top)
            on_scalar(nc, "e_s2", lambda act: act.activation(G[:, :, :], G[:, :, :], ACT.Exp))

            def shares(dve):
                dve.reduce_sum(total[:, :], G[:, :, :], axis=AX.X)
                dve.drain()
                dve.reciprocal(total[:, :], total[:, :])
                dve.drain()
                dve.tensor_tensor(G[:, :, :], G[:, :, :], total[:, :].unsqueeze(2).to_broadcast([128, 2, D]), ALU.mult)
            on_vector(nc, "e_s3", shares)
            turn_blocks(nc, [(G[:, m, m * 128:(m + 1) * 128], PT[:, m, m * 128:(m + 1) * 128]) for m in range(2)], const, "e_t")
            product(nc, halves(wq), halves(PT), M, "e_m")
            product(nc, [bq_wide[:, m, 0:NP] for m in range(2)], halves(PT), bq_row, "e_bq")
            project(nc, halves(XT), None, D, put_rows(B, add=A), "e_x", weights_sb=M, bias_sb=bq_row[:, 0, :])
            tile_norm(nc, B, C, "e_n", gain=I["L2_mix_norm_g"], shift=I["L2_mix_norm_b"], square=A)
        turn_rows(nc, C, XT, const, "e_turn2")
        experts(nc, XT, [(I["L2_mix_w_fc1"], I["L2_mix_b_fc1"]), (I["L2_mix_w_fc2"], I["L2_mix_b_fc2"])], 1, ACT.Gelu, B, "e_mlp")
        add_rows(nc, X, B, "e_add2")


def turn_blocks(nc, pairs, const, name):
    with Scope(nc, name) as k:
        banks = [k.ps(f"bank{n}", [128, 512]) for n in range(len(pairs))]
        made = k.sem("made")
        with nc.Block() as block:
            @block.tensor
            def _(pe):
                for n, (of, to) in enumerate(pairs):
                    p, c = of.shape
                    pe.transpose(banks[n][0:c, 0:p], of, const["eye"][0:p, 0:p]).then_inc(made, 1)

            @block.vector
            def _(dve):
                for n, (of, to) in enumerate(pairs):
                    p, c = of.shape
                    dve.wait_ge(made, n + 1)
                    dve.tensor_copy(to, banks[n][0:c, 0:p])


def every_max(nc, run, top, const, name):
    with Scope(nc, name) as k:
        mine, turned, wide = k.sb("mine", [128, 4]), k.sb("turned", [4, 1]), k.sb("wide", [4, 128])
        b0, b1 = k.ps("b0", [128, 512]), k.ps("b1", [128, 512])
        first, across, second, back = (k.sem(n) for n in ("first", "across", "second", "back"))
        with nc.Block() as block:
            @block.tensor
            def _(pe):
                pe.wait_ge(first, 1)
                pe.transpose(b0[0:4, 0:NP], mine[0:NP, :], const["eye"][0:NP, 0:NP]).then_inc(across, 1)
                pe.wait_ge(second, 1)
                pe.matmul(b1[0:NP, 0:4], wide[:, 0:NP], const["eye"][0:4, 0:4], start=True, stop=True).then_inc(back, 1)

            @block.vector
            def _(dve):
                dve.tensor_reduce(mine[0:NP, :], run[0:NP, :, :].rearrange("p t h -> p h t"), AX.X, ALU.max).then_inc(first, 1)
                dve.wait_ge(across, 1)
                dve.tensor_reduce(turned[:, :], b0[0:4, 0:NP], AX.X, ALU.max)
                dve.drain()
                dve.tensor_copy(wide[:, :], turned[:, :].to_broadcast([4, 128])).then_inc(second, 1)
                dve.wait_ge(back, 1)
                dve.tensor_copy(top[0:NP, :], b1[0:NP, 0:4])


def layer2_experts(nc, I, X, const, lower):
    with Scope(nc, "f") as k:
        XT, gates = k.sb("XT", [128, 2, N]), k.sb("gates", [128, T, 8])
        with Scope(nc, "f1") as j:
            A, keep, total = j.sb("A", [128, T, D]), j.sb("keep", [128, T, 8]), j.sb("total", [128, T])
            tile_norm(nc, X, A, "f_norm")
            turn_rows(nc, A, XT, const, "f_turn")
            project(nc, halves(XT), I["L2_ffn_Wr"], 8, put_rows(gates), "f_g", bias=I["L2_ffn_br"])
            softmax_of(nc, gates, 8, "f_s")
            choose_two(nc, gates, keep, lower[8], 8, "f_two")

            def shares(dve):
                dve.tensor_tensor(gates[0:NP, :, :], gates[0:NP, :, :], keep[0:NP, :, :], ALU.mult)
                dve.drain()
                normalise(dve, gates, total, 8)
            on_vector(nc, "f_sh", shares)
            tile_norm(nc, A, A, "f_norm2")
            turn_rows(nc, A, XT, const, "f_turn2")
        experts(nc, XT, [(I["L2_ffn_W1"], I["L2_ffn_b1"]), (I["L2_ffn_W2"], I["L2_ffn_b2"])], 8, ACT.Gelu, X, "f_mlp", gates=gates, affine=(I["L2_ffn_ln_g"], I["L2_ffn_ln_b"]))


def layer3_graph(nc, I, X, edge, const):
    with Scope(nc, "g") as k:
        A, B = k.sb("A", [128, T, D]), k.sb("B", [128, T, D])
        table = nc.dram_tensor("g_table", (N, 264), F32, kind="Internal").ap()
        tile_norm(nc, X, A, "g_norm")
        with Scope(nc, "g1") as j:
            s, own, acc, run = j.sb("s", [128, T, 8]), j.sb("own", [128, T, 8]), j.sb("acc", [128, T, 264]), j.sb("run", [128, T, 8])
            with Scope(nc, "g2") as m:
                XT, VS = m.sb("XT", [128, 2, N]), m.sb("VS", [128, T, 264])
                turn_rows(nc, A, XT, const, "g_turn")
                project(nc, halves(XT), I["L3_gnn_Wq"], D, put_rows(B), "g_q", bias=I["L3_gnn_bq"])
                project(nc, halves(XT), I["L3_gnn_Wk"], D, lambda dve, t, bank, bias: key_row(dve, VS, t, bank, bias), "g_k", bias=I["L3_gnn_bk"])

                def scores(dve):
                    dve.tensor_tensor(B[0:NP, :, :], B[0:NP, :, :], VS[0:NP, :, 0:D], ALU.mult)
                    dve.drain()
                    dve.reduce_sum(s[0:NP, :, :], B[0:NP, :, :].rearrange("p t (h e) -> p t h e", h=8), axis=AX.X)
                    dve.drain()
                    dve.tensor_scalar(s[0:NP, :, :], s[0:NP, :, :], 32 ** -0.5, None, ALU.mult)
                    dve.drain()
                    dve.tensor_scalar(own[0:NP, :, :], s[0:NP, :, :], 2.0, None, ALU.mult)
                    dve.tensor_copy(VS[0:NP, :, D:264], s[0:NP, :, :])
                on_vector(nc, "g_s", scores)
                project(nc, halves(XT), I["L3_gnn_Wv"], D, put_rows(VS), "g_v", bias=I["L3_gnn_bv"])
                on_vector(nc, "g_st", lambda dve: start_with_self(dve, acc, run, VS, own[0:NP, :, :], 8, 32, None), stores=[(table_rows(table), VS[0:NP, :, :])])
            edge_pass(nc, edge, table, "add", 8, 32, 264, s, 0.2, dict(acc=acc, m=run), const, "ge")
            finish_heads(nc, acc, 8, 32, B, "g_fin")
        with Scope(nc, "g3") as j:
            XT, C = j.sb("XT", [128, 2, N]), j.sb("C", [128, T, D])
            turn_rows(nc, B, XT, const, "g_turn2")
            project(nc, halves(XT), I["L3_gnn_Wo"], D, put_rows(B, add=A), "g_o", bias=I["L3_gnn_bo"])
            node_norm(nc, B, C, I["L3_gnn_bn1_g"], I["L3_gnn_bn1_b"], const, "g_bn1")
            turn_rows(nc, B, XT, const, "g_turn3")
            experts(nc, XT, [(I["L3_gnn_W1"], I["L3_gnn_b1"]), (I["L3_gnn_W2"], I["L3_gnn_b2"])], 1, ACT.Relu, B, "g_mlp")
            node_norm(nc, B, C, I["L3_gnn_bn2_g"], I["L3_gnn_bn2_b"], const, "g_bn2")
            add_rows(nc, X, B, "g_add", also=A)
        with Scope(nc, "g4") as j:
            XT = j.sb("XT", [128, 2, N])
            rms_norm(nc, A, B, I["L3_mix_g_pre"], "g_rms")
            turn_rows(nc, B, XT, const, "g_turn4")
            q, kv = j.sb("q", [128, T, 128]), j.sb("kv", [128, T, 257])

            def put(dve, t, bank, bias):
                dve.tensor_copy(q[0:NP, t, :], bank[:, 0:128])
                return dve.tensor_copy(kv[0:NP, t, 0:256], bank[:, 128:384])
            project(nc, halves(XT), I["L3_mix_w_qkv"], 384, put, "g_qkv")
            fill(nc, [(kv[:, :, 256:257], 1.0)])
            mem_k, mem_v, mem_kT = j.sb("mem_k", [128, 4]), j.sb("mem_v", [4, 129]), j.sb("mem_kT", [4, 128])
            G, GT, M2, w_out = j.sb("G", [128, 1, 129]), j.sb("GT", [128, 128]), j.sb("M2", [128, 1, D]), j.sb("w_out", [128, D])
            top_q, cols = j.sb("top_q", [128, T * 4]), j.sb("cols", [128, 128])
            top_k, top_wide, top_row, inv = j.sb("top_k", [128, 1]), j.sb("top_wide", [128, 128]), j.sb("top_row", [128, 1, 128]), j.sb("inv", [128, 1])
            turned = j.sb("turned", [128, 128])
            q4 = q[0:NP, :, :].rearrange("p t (h e) -> p (t h) e", h=4)
            heads = [NP, T * 4, 32]

            def tops(dve):
                dve.memset(mem_v[:, 128:129], 1.0)
                dve.tensor_reduce(top_q[0:NP, :], q4, AX.X, ALU.max)
                dve.tensor_reduce(cols[0:NP, :], kv[0:NP, :, 0:128].rearrange("p t d -> p d t"), AX.X, ALU.max)
                dve.drain()
                dve.tensor_tensor(q4, q4, top_q[0:NP, :].unsqueeze(2).to_broadcast(heads), ALU.subtract)
            on_vector(nc, "g_m1", tops, loads=[(mem_k[:, :], I["L3_mem_k"]), (mem_v[:, 0:128], I["L3_mem_vT"]), (w_out[:, :], I["L3_mix_w_out"])])
            turn_blocks(nc, [(cols[0:NP, :], turned[:, 0:NP])], const, "g_m2")

            def key_top(dve):
                dve.memset(turned[:, NP:128], -FAR)
                dve.drain()
                dve.tensor_copy(turned[:, NP:NP + 1], mem_k[:, 0:1])
                dve.tensor_copy(turned[:, NP + 1:128], mem_k[:, 1:3])
                dve.drain()
                dve.tensor_reduce(top_k[:, :], turned[:, :], AX.X, ALU.max)
                dve.drain()
                dve.tensor_tensor(top_k[:, :], top_k[:, :], mem_k[:, 3:4], ALU.max)
                dve.drain()
                dve.tensor_copy(top_wide[:, :], top_k[:, :].to_broadcast([128, 128]))
                dve.tensor_tensor(mem_k[:, :], mem_k[:, :], top_k[:, :].to_broadcast([128, 4]), ALU.subtract)
            on_vector(nc, "g_m3", key_top)
            product(nc, [top_wide[:, :]], [const["eye"][:, :]], top_row, "g_m4")
            on_vector(nc, "g_m5", lambda dve: dve.tensor_tensor(kv[0:NP, :, 0:128], kv[0:NP, :, 0:128], top_row[0:NP, :, :].to_broadcast([NP, T, 128]), ALU.subtract))

            def exps(act):
                act.activation(q4, q4, ACT.Exp)
                act.activation(kv[0:NP, :, 0:128], kv[0:NP, :, 0:128], ACT.Exp)
                act.activation(mem_k[:, :], mem_k[:, :], ACT.Exp)
            on_scalar(nc, "g_m6", exps)

            def query_shares(dve):
                dve.reduce_sum(top_q[0:NP, :], q4, axis=AX.X)
                dve.drain()
                dve.reciprocal(top_q[0:NP, :], top_q[0:NP, :])
                dve.drain()
                dve.tensor_tensor(q4, q4, top_q[0:NP, :].unsqueeze(2).to_broadcast(heads), ALU.mult)
            on_vector(nc, "g_m7", query_shares)
            turn_blocks(nc, [(mem_k[:, :], mem_kT[:, :])], const, "g_m8")
            gram(nc, kv, kv[:, :, 128:257], G, "g_gram", m_cols=128, n_cols=129, extra=(mem_kT[:, :], mem_v[:, :]))

            def context(dve):
                dve.reciprocal(inv[:, :], G[:, 0, 128:129])
                dve.drain()
                dve.tensor_scalar(G[:, 0, 0:128], G[:, 0, 0:128], inv[:, 0:1], 32 ** -0.5, ALU.mult, ALU.mult)
            on_vector(nc, "g_m9", context)
            keep_blocks(nc, [(0, G[:, 0, :], 128)], 32, "g_kb")
            turn_blocks(nc, [(G[:, 0, 0:128], GT[:, :])], const, "g_m10")
            product(nc, [GT[:, :]], [w_out[:, :]], M2, "g_m11")
            turn_rows(nc, q, XT, const, "g_turn5", halves=1)
            project(nc, [XT[:, 0, :]], None, D, put_rows(B), "g_out", weights_sb=M2, bias=I["L3_mix_b_out"])
            rms_norm(nc, B, A, I["L3_mix_g_out"], "g_rms2")
            add_rows(nc, X, A, "g_add2")


def key_row(dve, to, t, bank, bias):
    return dve.tensor_tensor(to[0:NP, t, 0:D], bank, bias, ALU.add)


def layer3_tokens(nc, I, X, const):
    KEEP = max(1, N // 2) - 1
    with Scope(nc, "h") as k:
        XT, gates = k.sb("XT", [128, 2, N]), k.sb("gates", [128, T, 1])
        stored_w = nc.dram_tensor("h_w", (N, 1), F32, kind="Internal").ap()
        with Scope(nc, "h1") as j:
            A = j.sb("A", [128, T, D])
            tile_norm(nc, X, A, "h_norm")
            turn_rows(nc, A, XT, const, "h_turn")
            add_rows(nc, X, A, "h_add")
            w = j.sb("w", [128, 2, 1])
            project(nc, halves(XT), None, 1, put_rows(gates), "h_w", bias=I["L3_ffn_br"], weights_sb=w, loads=[(w[:, :, :].rearrange("p k n -> p (k n)"), I["L3_ffn_wr"])])
            with nc.allow_non_contiguous_dma(reason="one weight per node, 12.5 KB in all"):
                on_vector(nc, "h_st", lambda dve: None, stores=[(table_rows(stored_w), gates[0:NP, :, :])])
        with Scope(nc, "h2") as j:
            every, index, before, same = (j.sb(n, [128, N]) for n in ("every", "index", "before", "same"))
            whole, mine_i = j.sb("whole", [128, N], I32), j.sb("mine_i", [128, T], I32)
            mine, more, ties = j.sb("mine", [128, T]), j.sb("more", [128, T]), j.sb("ties", [128, T])
            counted = j.sem("counted")
            with nc.Block() as block:
                @block.gpsimd
                def _(pool):
                    pool.iota(whole[:, :], pattern=[[1, N]], base=0, channel_multiplier=0)
                    pool.iota(mine_i[:, :], pattern=[[NP, T]], base=0, channel_multiplier=1)

            def rank(dve):
                dve.tensor_copy(index[:, :], whole[:, :])
                dve.tensor_copy(mine[:, :], mine_i[:, :])
                dve.drain()
                for t in range(T):
                    w = gates[0:NP, t, :]
                    dve.tensor_scalar(same[0:NP, :], every[0:NP, :], w, 0.0, ALU.is_gt, ALU.add, accum_out=more[0:NP, t:t + 1])
                    dve.tensor_scalar(before[0:NP, :], index[0:NP, :], mine[0:NP, t:t + 1], None, ALU.is_lt)
                    dve.drain()
                    dve.scalar_tensor_tensor(out=same[0:NP, :], in0=every[0:NP, :], scalar=w, in1=before[0:NP, :], op0=ALU.is_equal, op1=ALU.mult)
                    dve.drain()
                    dve.reduce_sum(ties[0:NP, t:t + 1], same[0:NP, :], axis=AX.X)
                    dve.drain()
                dve.tensor_tensor(more[0:NP, :], more[0:NP, :], ties[0:NP, :], ALU.add)
                dve.drain()
                dve.tensor_scalar(more[0:NP, :], more[0:NP, :], float(KEEP), None, ALU.is_lt)
                dve.drain()
                dve.tensor_tensor(flat(gates[0:NP, :, :]), flat(gates[0:NP, :, :]), more[0:NP, :], ALU.mult)
            on_vector(nc, "h_rank", rank, loads=[(every[0:NP, :], along(stored_w.rearrange("n a -> (n a)"), NP))])
        experts(nc, XT, [(I["L3_ffn_w1"], I["L3_ffn_b1"]), (I["L3_ffn_w2"], I["L3_ffn_b2"])], 1, ACT.Gelu_apprx_tanh, X, "h_mlp", gates=gates)


E_MAIN, COLS_MAIN, J_MAIN = 100000, 832, 784
E_GAT, COLS_GAT, J_GAT = 65536, 564, 512


def program(nc, I, out):
    with Scope(nc, "net") as k:
        const = dict(eye=k.sb("eye", [128, 128]), ones=k.sb("ones", [128, 128]), before=k.sb("before", [128, 128]),
                     ramp=k.sb("ramp", [128, 128]), eye4_bf=k.sb("eye4_bf", [128, 512], BF16))
        lower = {4: k.sb("lower4", [128, 4, 4]), 8: k.sb("lower8", [128, 8, 8])}
        X, inv_deg = k.sb("X", [128, T, D]), k.sb("inv_deg", [128, T])
        main = dict(data=k.sb("main_data", [128, COLS_MAIN + 2, 4]), tile_of=k.sb("main_tile", [128, COLS_MAIN // 2 + 1], I32), cols=COLS_MAIN)
        gat = dict(data=k.sb("gat_data", [128, COLS_GAT + 2, 4]), tile_of=k.sb("gat_tile", [128, COLS_GAT // 2 + 1], I32), cols=COLS_GAT)
        constants(nc, const)
        cut = k.sem("lower_cut")
        with nc.Block() as block:
            @block.gpsimd
            def _(pool):
                for n, E in enumerate((4, 8)):
                    pool.memset(lower[E][:, :, :], 1.0).then_inc(cut, 1)
                    pool.wait_ge(cut, n + 1)
                    pool.affine_select(out=lower[E][:, :, :], in_=lower[E][:, :, :], compare_op=ALU.is_gt, fill=0.0, base=0, pattern=[[1, E], [-1, E]], channel_multiplier=0)
        on_vector(nc, "x_in", lambda dve: None, loads=[(X[0:NP, :, :], table_rows(I["x"]))])
        rows_main = nc.dram_tensor("edges_main", (128 * COLS_MAIN + 128 * J_MAIN, 4), F32, kind="Internal").ap()
        rows_gat = nc.dram_tensor("edges_gat", (128 * COLS_GAT + 128 * J_GAT, 4), F32, kind="Internal").ap()
        group_edges(nc, main, I["src"], I["dst"], I["edge_attr_2"], E_MAIN, J_MAIN, const, rows_main, "em")
        group_edges(nc, gat, I["gat_src"], I["gat_dst"], None, E_GAT, J_GAT, const, rows_gat, "eg")
        stages = [lambda: layer0_graph(nc, I, X, inv_deg, main, const), lambda: layer0_experts(nc, I, X, gat, const, lower),
                  lambda: layer1_graph(nc, I, X, inv_deg, main, const), lambda: layer1_experts(nc, I, X, const, lower),
                  lambda: layer2_graph(nc, I, X, main, const), lambda: layer2_experts(nc, I, X, const, lower),
                  lambda: layer3_graph(nc, I, X, main, const), lambda: layer3_tokens(nc, I, X, const)]
        for stage in stages:
            stage()
        on_vector(nc, "x_out", lambda dve: None, stores=[(table_rows(out), X[0:NP, :, :])])


def layouts(a):
    import numpy as np

    a = dict(a)
    for name in ("L0_gnn_ffn_w1", "L0_gnn_ffn_w2", "L0_gnn_ffn_b1", "L0_gnn_ffn_b2", "L1_mix_W1", "L1_mix_W2", "L1_ffn_sW1", "L1_ffn_sW2", "L1_ffn_sW3",
                 "L1_ffn_sb1", "L1_ffn_sb2", "L1_ffn_sb3", "L2_mix_w_fc1", "L2_mix_w_fc2", "L2_mix_b_fc1", "L2_mix_b_fc2", "L3_gnn_W1", "L3_gnn_W2",
                 "L3_gnn_b1", "L3_gnn_b2", "L3_ffn_w1", "L3_ffn_w2", "L3_ffn_b1", "L3_ffn_b2"):
        a[name] = a[name][None]
    for name in ("wk", "wv", "wo"):
        a[f"L0_mix_{name}T"] = a.pop(f"L0_mix_{name}").T
    a["L0_gnn_Wkv"] = np.concatenate([a.pop("L0_gnn_Wk"), a.pop("L0_gnn_Wv")], axis=1)
    a["L0_ffn_att_src"], a["L0_ffn_att_dst"] = a["L0_ffn_att_src"].reshape(-1), a["L0_ffn_att_dst"].reshape(-1)
    a["gat_src"], a["gat_dst"] = a["L0_ffn_edge_index"][0], a["L0_ffn_edge_index"][1]
    del a["L0_ffn_edge_index"]
    a["L1_gnn_WT"] = a.pop("L1_gnn_W").T
    a["zeros512"], a["zeros256"] = np.zeros((1, 512), np.float32), np.zeros((1, 256), np.float32)
    a["L2_gnn_WfT"], a["L2_gnn_WrT"] = a["L2_gnn_W_forward"].T, a["L2_gnn_W_reverse"].T
    a["L2_gnn_attnT"] = a.pop("L2_gnn_attn_forward")[0].T
    w, b = a.pop("L2_mix_w_qkv"), a.pop("L2_mix_b_qkv")
    a["L2_mix_wqT"], a["L2_mix_wk"], a["L2_mix_wv"] = w[:, 0:256].T, w[:, 256:512], w[:, 512:768]
    a["L2_mix_bq"], a["L2_mix_bk"], a["L2_mix_bv"] = b[0:256], b[256:512], b[512:768]
    mem = a.pop("L3_mix_mem_kv")
    a["L3_ffn_wr"] = a["L3_ffn_wr"].reshape(2, 128).T
    a["L3_mem_k"], a["L3_mem_vT"] = mem[0].reshape(128, 4), mem[1].reshape(128, 4).T
    for name in ("L0_gnn_ffn_b1", "L0_ffn_b1", "zeros512", "L1_ffn_sb1", "L1_ffn_sb2", "L1_ffn_eb1", "L1_ffn_eb2", "L2_mix_b_fc1", "L2_ffn_b1", "L2_ffn_ln_g",
                 "L2_ffn_ln_b", "L3_gnn_b1", "L3_ffn_b1"):
        E, n = a[name].shape
        a[name] = a[name].reshape(E, max(1, n // 128), min(128, n)).transpose(0, 2, 1)
    a["L2_mix_bq"] = a["L2_mix_bq"].reshape(2, 128).T
    return {name: np.ascontiguousarray(v) for name, v in a.items()}


def kernel(**inputs):
    import numpy as _np
    import concourse.bacc as _bacc
    from concourse import mybir as _mybir
    from concourse.bass_utils import run_bass_kernel_spmd as _run

    nc = _bacc.Bacc("TRN2", target_bir_lowering=False, num_devices=1)
    arrays, args = {}, {}
    given = {name: _np.asarray(v) for name, v in inputs.items() if name not in ("L3_mix_t", "L3_ffn_attention_mask")}
    for name, a in layouts(given).items():
        arrays[f"in_{name}_dram"] = a
        args[name] = nc.dram_tensor(f"in_{name}_dram", a.shape, _mybir.dt.from_np(a.dtype), kind="ExternalInput").ap()
    out = nc.dram_tensor("out_0_dram", (N, D), F32, kind="ExternalOutput").ap()
    program(nc, args, out)
    r = _run(nc, [arrays], core_ids=[0])
    return r.results[0]["out_0_dram"]
```

```python
from contextlib import ExitStack

import concourse.bass as bass
from concourse import mybir

F32 = mybir.dt.float32
BF16 = mybir.dt.bfloat16
I32 = mybir.dt.int32
ALU = mybir.AluOpType
ACT = mybir.ActivationFunctionType
AX = mybir.AxisListType

N = 3125
NP = 125
T = N // NP
D = 256
FAR = 1e30


class Scope:

    spent = []

    def __init__(self, nc, name):
        self.nc, self.name, self.stack, self.mine = nc, name, ExitStack(), []

    def __enter__(self):
        self.stack.__enter__()
        return self

    def __exit__(self, *why):
        left = self.stack.__exit__(*why)
        Scope.spent += self.mine
        if len(Scope.spent) > 72:
            numbers = sorted(Scope.spent)
            starts = [n for n in numbers if n - 1 not in numbers]
            ends = [n + 1 for n in numbers if n + 1 not in numbers]
            for a, b in zip(starts, ends):
                self.nc.gpsimd.sem_clear(range(a, b))
            self.nc.all_engine_barrier()
            Scope.spent = []
        return left

    def sb(self, n, shape, dtype=F32):
        return self.stack.enter_context(self.nc.sbuf_tensor(f"{self.name}_{n}", shape, dtype))

    def ps(self, n, shape, dtype=F32):
        return self.stack.enter_context(self.nc.psum_tensor(f"{self.name}_{n}", shape, dtype))

    def sem(self, n):
        handle = self.stack.enter_context(self.nc.semaphore(f"{self.name}_{n}"))
        self.mine.append(handle.num)
        return handle

    def own_sem(self, n):
        return self.nc.alloc_semaphore(f"{self.name}_{n}")


def constants(nc, const):
    with Scope(nc, "constants") as k:
        counted = k.sb("counted", [128, 128], I32)
        set_up, cut = k.sem("set_up"), k.sem("cut")
        with nc.Block() as block:
            @block.gpsimd
            def _(pool):
                pool.iota(counted[:, :], pattern=[[1, 128]], base=0, channel_multiplier=0).then_inc(cut, 1)
                pool.memset(const["ones"][:, :], 1.0)
                pool.memset(const["before"][:, :], 1.0).then_inc(set_up, 1)
                pool.memset(const["eye"][:, :], 0.0).then_inc(set_up, 1)
                pool.wait_ge(set_up, 2)
                pool.affine_select(out=const["eye"][:, :], in_=const["eye"][:, :], compare_op=ALU.not_equal, fill=1.0, base=0, pattern=[[-1, 128]], channel_multiplier=1).then_inc(cut, 1)
                pool.affine_select(out=const["before"][:, :], in_=const["before"][:, :], compare_op=ALU.is_gt, fill=0.0, base=0, pattern=[[1, 128]], channel_multiplier=-1).then_inc(cut, 1)

            @block.vector
            def _(dve):
                dve.wait_ge(cut, 3)
                dve.tensor_copy(const["ramp"][:, :], counted[:, :])
                for c in range(4):
                    dve.tensor_copy(const["eye4_bf"][:, c * 128:(c + 1) * 128], const["eye"][:, :])


def group_edges(nc, edge, src, dst, attr, E, count, const, scratch, name):
    J = count
    cols = edge["cols"]
    SUPER = cols // 2
    full, rest = E // J, E % J
    with Scope(nc, name) as k:
        sb, ps, sem = k.sb, k.ps, k.sem

        src_i, dst_i = sb("src_i", [128, J], I32), sb("dst_i", [128, J], I32)
        load = sb("load", [128, J, 4])
        dst_f, tile_f, work = sb("dst_f", [128, J]), sb("tile_f", [128, J]), sb("work", [128, J])
        mask, whole = sb("mask", [128, J], I32), sb("whole", [128, J], I32)
        slot = sb("slot", [128, J])
        row, spare = sb("row", [128, J], I32), sb("spare", [128, J], I32)
        ones = sb("ones", [128, J])
        at = sb("at", [128, J, 2]) if attr is not None else None
        per_bin, base = sb("per_bin", [128, T]), sb("base", [128, T])
        ends, starts = sb("ends", [128, T]), sb("starts", [128, T])
        pad_i = sb("pad_i", [128, T], I32)
        first = sb("first", [128, SUPER])
        past = sb("past", [128, SUPER, T])
        tile_fs = sb("tile_fs", [128, SUPER])
        ring_row, ring_load = sb("ring_row", [128, 4, 1], I32), sb("ring_load", [128, 4, 4])
        sums = ps("sums", [128, 2, T])
        cleared, loaded, made = sem("cleared"), sem("loaded"), sem("made")
        step, counted, summed, filled = sem("step"), sem("counted"), sem("summed"), sem("filled")
        rows_ready, staged, back = sem("rows_ready"), sem("staged"), sem("back")
        scattered = [k.own_sem(f"scattered{u}") for u in range(4)]
        ids = edge["tile_of"]
        steps = [0]

        with nc.Block() as block:
            @block.sync
            def _(sp):
                sp.wait_ge(cleared, 3)
                for to, of in ((src_i, src), (dst_i, dst)):
                    sp.dma_start(to[0:full, :], of[0:full * J].rearrange("(p j) -> p j", j=J)).then_inc(loaded, 16)
                    if rest:
                        sp.dma_start(to[full:full + 1, 0:rest], of[full * J:E].rearrange("(p j) -> p j", p=1)).then_inc(loaded, 16)
                if at is not None:
                    sp.dma_start(at[0:full, :, :], attr[0:full * J, :].rearrange("(p j) c -> p j c", j=J)).then_inc(loaded, 16)
                    if rest:
                        sp.dma_start(at[full:full + 1, 0:rest, :], attr[full * J:E, :].rearrange("(p j) c -> p j c", p=1)).then_inc(loaded, 16)
                sp.wait_ge(made, 1)
                sp.dma_start(scratch[0:128 * cols, :].rearrange("(p c) f -> p (c f)", c=cols), edge["data"][:, 0:cols, :].rearrange("p c f -> p (c f)")).then_inc(filled, 16)
                for u in range(4):
                    sp.wait_ge(scattered[u], 16 * (J // 4))
                sp.wait_ge(filled, 16)
                sp.dma_start(edge["data"][:, 0:cols, :].rearrange("p c f -> p (c f)"), scratch[0:128 * cols, :].rearrange("(p c) f -> p (c f)", c=cols)).then_inc(back, 16)
                sp.wait_ge(back, 16)

            n_loads = (2 + (attr is not None)) * (1 + bool(rest))

            @block.gpsimd
            def _(pool):
                pool.iota(spare[:, :], pattern=[[1, J]], base=128 * cols, channel_multiplier=J).then_inc(made, 1)
                pool.iota(row[:, 0:SUPER], pattern=[[256, SUPER]], base=0, channel_multiplier=0).then_inc(made, 1)
                pool.wait_ge(filled, 16)
                with pool.Fori(0, J // 4) as i:
                    for u in range(4):
                        pool.wait_ge(staged, i * 4 + u + 1)
                        pool.nop(nofuse=True)
                        pool.indirect_dma_start(scratch, bass.IndirectOffsetOnAxis(ap=ring_row[:, u, :], axis=0), ring_load[:, u, :], None).then_inc(scattered[u], 16)
                for u in range(4):
                    pool.wait_ge(scattered[u], 16 * (J // 4))

            @block.tensor
            def _(pe):
                pe.wait_ge(counted, 1)
                pe.matmul(sums[:, 0, :], const["before"][:, :], per_bin[:, :], start=True, stop=True)
                pe.matmul(sums[:, 1, :], const["ones"][:, 0:128], per_bin[:, :], start=True, stop=True).then_inc(summed, 1)

            @block.vector
            def _(dve):
                def then(ins):
                    steps[0] += 1
                    ins.then_inc(step, 1)
                    dve.wait_ge(step, steps[0])

                dve.memset(src_i[:, :], 0).then_inc(cleared, 1)
                dve.memset(dst_i[:, :], 1 << 20).then_inc(cleared, 1)
                if at is not None:
                    dve.memset(at[:, :, :], 0.0)
                dve.memset(load[:, :, :], 0.0)
                then(dve.memset(edge["data"][:, :, :], 0.0))
                dve.memset(edge["data"][:, :, 1], -1.0).then_inc(made, 1)
                dve.memset(slot[:, :], 0.0)
                dve.memset(ones[:, :], 1.0).then_inc(cleared, 1)
                dve.wait_ge(cleared, 3)
                dve.wait_ge(loaded, 16 * n_loads)
                then(dve.tensor_copy(dst_f[:, :], dst_i[:, :]))
                then(dve.tensor_scalar(work[:, :], dst_f[:, :], 1.0 / NP, None, ALU.mult))
                then(dve.tensor_copy(whole[:, :], work[:, :]))
                then(dve.tensor_copy(tile_f[:, :], whole[:, :]))
                then(dve.scalar_tensor_tensor(out=work[:, :], in0=tile_f[:, :], scalar=-float(NP), in1=dst_f[:, :], op0=ALU.mult, op1=ALU.add))
                then(dve.tensor_scalar(slot[:, :], work[:, :], 0.0, None, ALU.is_lt))
                then(dve.tensor_tensor(tile_f[:, :], tile_f[:, :], slot[:, :], ALU.subtract))
                then(dve.tensor_scalar(slot[:, :], work[:, :], float(NP), None, ALU.is_ge))
                then(dve.tensor_tensor(tile_f[:, :], tile_f[:, :], slot[:, :], ALU.add))
                then(dve.scalar_tensor_tensor(out=load[:, :, 1], in0=tile_f[:, :], scalar=-float(NP), in1=dst_f[:, :], op0=ALU.mult, op1=ALU.add))
                then(dve.tensor_copy(work[:, :], src_i[:, :]))
                then(dve.tensor_scalar(work[:, :], work[:, :], float(N - 1), 0.0, ALU.min, ALU.max))
                then(dve.tensor_copy(load[:, :, 0].bitcast(I32), work[:, :]))
                if at is not None:
                    then(dve.tensor_copy(load[:, :, 2:4], at[:, :, :]))
                for b in range(T):
                    then(dve.tensor_scalar(work[:, :], tile_f[:, :], float(b), None, ALU.is_equal))
                    then(dve.reduce_sum(per_bin[:, b:b + 1], work[:, :], axis=AX.X))
                dve.memset(slot[:, :], 0.0).then_inc(counted, 1)
                dve.wait_ge(summed, 1)
                then(dve.tensor_scalar(ends[:, :], sums[:, 1, :], 255.0, None, ALU.add))
                then(dve.tensor_copy(pad_i[:, :], ends[:, :]))
                then(dve.tensor_scalar(pad_i[:, :], pad_i[:, :], 8, 8, ALU.arith_shift_right, ALU.arith_shift_left))
                then(dve.tensor_copy(starts[:, :], pad_i[:, :]))
                then(dve.tensor_tensor_scan(ends[:, :], ones[:, 0:T], starts[:, :], 0.0, ALU.mult, ALU.add))
                then(dve.tensor_tensor(starts[:, :], ends[:, :], starts[:, :], ALU.subtract))
                then(dve.tensor_tensor(base[:, :], starts[:, :], sums[:, 0, :], ALU.add))
                dve.wait_ge(made, 3)
                then(dve.tensor_copy(first[:, :], row[:, 0:SUPER]))
                then(dve.tensor_tensor(past[:, :, :], ends[:, :].unsqueeze(1).to_broadcast([128, SUPER, T]), first[:, :].unsqueeze(2).to_broadcast([128, SUPER, T]), ALU.is_le))
                then(dve.reduce_sum(tile_fs[:, :], past[:, :, :], axis=AX.X))
                then(dve.tensor_scalar(tile_fs[:, :], tile_fs[:, :], float(T - 1), None, ALU.min))
                then(dve.memset(ids[:, :], 0))
                then(dve.tensor_copy(ids[:, 0:SUPER], tile_fs[:, :]))
                for b in range(T):
                    then(dve.tensor_scalar(mask[:, :], tile_f[:, :], float(b), None, ALU.is_equal))
                    then(dve.tensor_tensor_scan(work[:, :], ones[:, :], mask[:, :], base[:, b:b + 1], ALU.mult, ALU.add))
                    then(dve.copy_predicated(slot[:, :], mask[:, :], work[:, :]))
                then(dve.tensor_scalar(work[:, :], slot[:, :], -1.0, None, ALU.add))
                then(dve.tensor_copy(whole[:, :], work[:, :]))
                then(dve.tensor_scalar(mask[:, :], whole[:, :], 127, None, ALU.bitwise_and))
                then(dve.tensor_scalar(whole[:, :], whole[:, :], 7, None, ALU.arith_shift_right))
                then(dve.tensor_copy(work[:, :], mask[:, :]))
                then(dve.tensor_copy(dst_f[:, :], whole[:, :]))
                then(dve.scalar_tensor_tensor(out=work[:, :], in0=work[:, :], scalar=float(cols), in1=dst_f[:, :], op0=ALU.mult, op1=ALU.add))
                then(dve.tensor_copy(row[:, :], work[:, :]))
                then(dve.tensor_scalar(mask[:, :], tile_f[:, :], float(T), None, ALU.is_ge))
                then(dve.copy_predicated(row[:, :], mask[:, :], spare[:, :]))
                then(dve.tensor_scalar(mask[:, :], tile_f[:, :], 0.0, None, ALU.is_lt))
                then(dve.copy_predicated(row[:, :], mask[:, :], spare[:, :]))
                dve.wait_ge(filled, 16)
                for u in range(4):
                    dve.tensor_copy(ring_row[:, u, :], row[:, u:u + 1])
                    dve.tensor_copy(ring_load[:, u, :], load[:, u, :]).then_inc(staged, 1)
                with dve.Fori(1, J // 4) as i:
                    for u in range(4):
                        dve.wait_ge(scattered[u], i * 16)
                        dve.tensor_copy(ring_row[:, u, :], row[:, bass.ds(i * 4 + u, 1)])
                        dve.tensor_copy(ring_load[:, u, :], load[:, bass.ds(i * 4 + u, 1), :].rearrange("p a f -> p (a f)")).then_inc(staged, 1)


AHEAD = 6
SUM_AHEAD = 4


def edge_pass(nc, edge, table, kind, H, dv, row_width, per_target, scores, state, const, name):
    SUPER = edge["cols"] // 2
    W = H * (dv + 1)
    K = 3 * H
    HALF = H // 2
    count_targets = kind == "dot"
    WA = W + (1 if count_targets else 0)
    QW = {"dot": D, "add": H, "mix": 0}[kind]
    act_half = H * dv >= 128
    with Scope(nc, name) as k:
        sb, ps, sem = k.sb, k.ps, k.sem
        ids = edge["tile_of"]
        source = sb("source", [128, AHEAD, 2], I32)
        rows = sb("rows", [128, AHEAD, 2, row_width])
        hot = sb("hot", [128, AHEAD, 2, NP])
        hotT = sb("hotT", [128, AHEAD, 2, 128])
        awayT = sb("awayT", [128, 2, 256], BF16)
        score = sb("score", [128, AHEAD, 2, H])
        parts = sb("parts", [128, 2, 3, H], BF16)
        partsT = sb("partsT", [128, 256], BF16)
        left = sb("left", [128, 2, H])
        member = sb("member", [128, 2, H])
        head_rows = sb("head_rows", [128, H, NP], BF16)
        prod = sb("prod", [128, 2, D])
        below = sb("below", [128, 2, H])
        local = sb("local", [128, H])
        raised = sb("raised", [128, 2, H])
        drop = sb("drop", [128, 2, H])
        scale = sb("scale", [128, AHEAD, H])
        msg = sb("msg", [128, 2, 2, WA])
        mixed = sb("mixed", [128, 2, 2, 64])
        gap = sb("gap", [128, 2, H])
        term = sb("term", [128, 2, H])
        scaled = sb("scaled", [128, W])
        hot_ps = ps("hot_ps", [128, 4, 128])
        own_ps = ps("own_ps", [128, 2, 256])
        back_ps = ps("back_ps", [128, 2, 256])
        sum_ps = ps("sum_ps", [128, 512])
        max_ps = ps("max_ps", [128, H, 256])
        flip_ps = hot_ps[:, 2, :].bitcast(BF16)
        gathered = [k.own_sem(f"gathered{n}") for n in range(AHEAD)]
        (sources, hot_ready, score_ready, turned, turned_sb, own_ready, parts_ready, flipped, flipped_sb, heads_ready, max_ready, new_max,
         max_back, below_ready, drop_ready, weight_ready, scale_ready, scaled_ready, msg_ready, half_ready, mixed_ready,
         sum_ready, accumulated) = (sem(n) for n in (
             "sources", "hot_ready", "score_ready", "turned", "turned_sb", "own_ready", "parts_ready", "flipped", "flipped_sb", "heads_ready",
             "max_ready", "new_max", "max_back", "below_ready", "drop_ready", "weight_ready", "scale_ready", "scaled_ready",
             "msg_ready", "half_ready", "mixed_ready", "sum_ready", "accumulated"))
        acc, run = state["acc"], state["m"]

        with nc.Block() as block:
            @block.gpsimd
            def _(pool):
                def gather(s, n):
                    pool.wait_ge(msg_ready, s + 1)
                    if act_half:
                        pool.wait_ge(half_ready, s + 1)
                    pool.tensor_copy(source[:, n, :], edge["data"][:, bass.ds(2 * s, 2), 0].bitcast(I32)).then_inc(sources, 1)
                    pool.wait_ge(sources, s + 1)
                    pool.nop(nofuse=True)
                    for q in range(2):
                        pool.indirect_dma_start(rows[:, n, q, :], None, table, bass.IndirectOffsetOnAxis(ap=source[:, n, q:q + 1], axis=0)).then_inc(gathered[n], 16)

                def scale_down(s, n):
                    t = pool.value_load(ids[0:1, bass.ds(s, 1)], min_val=0, max_val=T - 1)
                    at = acc[0:NP, bass.ds(t, 1), :].rearrange("p a w -> p (a w)")
                    pool.wait_ge(scale_ready, s + 1)
                    pool.wait_ge(accumulated, s + 1)
                    pool.tensor_tensor(scaled[0:NP, :].rearrange("p (h v) -> p h v", h=H), at[:, 0:W].rearrange("p (h v) -> p h v", h=H),
                                       scale[0:NP, n, :].unsqueeze(2).to_broadcast([NP, H, dv + 1]), ALU.mult).then_inc(scaled_ready, 1)

                def split(s, n):
                    pool.wait_ge(score_ready, s + 1)
                    pool.tensor_tensor(left[:, :, :], score[:, n, :, :], parts[:, :, 0, :], ALU.subtract)
                    pool.drain()
                    pool.tensor_copy(parts[:, :, 1, :], left[:, :, :])
                    pool.drain()
                    pool.tensor_tensor(parts[:, :, 2, :], left[:, :, :], parts[:, :, 1, :], ALU.subtract).then_inc(parts_ready, 1)

                for s in range(4):
                    gather(s, s)
                for s in range(3):
                    split(s, s)
                with pool.Fori(0, SUPER // AHEAD) as i:
                    for u in range(AHEAD):
                        s, n = AHEAD * i + u + 1, (u + 1) % AHEAD
                        gather(s + 3, (n + 3) % AHEAD)
                        scale_down(s - 1, (n + AHEAD - 1) % AHEAD)
                        split(s + 2, (n + 2) % AHEAD)
                pool.wait_ge(gathered[(SUPER + 3) % AHEAD], 32 * ((SUPER + 3) // AHEAD + 1))

            @block.tensor
            def _(pe):
                def turn(s, n):
                    pe.wait_ge(hot_ready, s + 1)
                    for q in range(2):
                        ins = pe.transpose(hot_ps[0:NP, q, :], hot[:, n, q, :], const["eye"][:, :])
                    ins.then_inc(turned, 1)

                def tile_of(s):
                    return pe.value_load(ids[0:1, bass.ds(s, 1)], min_val=0, max_val=T - 1) if QW else None

                def own(s, n, t):
                    pe.wait_ge(turned_sb, s + 1)
                    if QW:
                        for q in range(2):
                            ins = pe.matmul(own_ps[:, q, 0:QW], hotT[0:NP, n, q, :], per_target[0:NP, bass.ds(t, 1), :].rearrange("p a w -> p (a w)"), start=True, stop=True)
                        ins.then_inc(own_ready, 1)

                def flip(s):
                    pe.wait_ge(parts_ready, s + 1)
                    for q in range(2):
                        ins = pe.transpose(flip_ps[0:K, q * 128:(q + 1) * 128], parts[:, q, :, :].rearrange("p c h -> p (c h)"), const["eye4_bf"][:, 0:128])
                    ins.then_inc(flipped, 1)

                def spread(s, n):
                    pe.wait_ge(flipped_sb, s + 1)
                    for a in range(0, H, 2):
                        pe.matmul(max_ps[0:NP, a:a + 2, :], const["eye4_bf"][0:NP, 0:NP], awayT[0:NP, n % 2:n % 2 + 1, :].to_broadcast([NP, 2, 256]), start=True, stop=False)
                        for h in (a, a + 1):
                            ins = pe.matmul(max_ps[0:NP, h, :], head_rows[0:K, h, :], partsT[0:K, :], start=False, stop=(h == a + 1))
                        if a + 2 in (HALF, H):
                            ins.then_inc(max_ready, 1)

                def maxima(s, n):
                    pe.wait_ge(new_max, s + 1)
                    for q in range(2):
                        ins = pe.matmul(back_ps[:, q, 0:H], hotT[0:NP, n, q, :], raised[0:NP, n % 2, :], start=True, stop=True)
                    ins.then_inc(max_back, 1)

                def total(s, n):
                    pe.wait_ge(msg_ready, s + 1 + AHEAD)
                    if act_half:
                        pe.wait_ge(half_ready, s + 1 + AHEAD)
                    for q in range(2):
                        ins = pe.matmul(sum_ps[0:NP, 0:WA], hot[:, n, q, :], msg[:, n % 2, q, :], start=(q == 0), stop=(q == 1))
                    ins.then_inc(sum_ready, 1)

                def one_turn(s, n, t, first=False, last=False):
                    own(s + 2, (n + 2) % AHEAD, t)
                    spread(s + 1, (n + 1) % AHEAD)
                    flip(s + 2)
                    if not first:
                        pe.wait_ge(accumulated, s)
                        total(s - 1, (n + AHEAD - 1) % AHEAD)
                    pe.wait_ge(flipped_sb, s + 3)
                    turn(s + 3, (n + 3) % AHEAD)
                    following = None if last else tile_of(s + 3)
                    maxima(s + 1, (n + 1) % AHEAD)
                    return following

                pe.wait_ge(heads_ready, 1)
                turn(0, 0)
                own(0, 0, tile_of(0))
                flip(0)
                pe.wait_ge(flipped_sb, 1)
                turn(1, 1)
                spread(0, 0)
                pe.wait_ge(parts_ready, 1)
                own(1, 1, tile_of(1))
                flip(1)
                pe.wait_ge(flipped_sb, 2)
                turn(2, 2)
                maxima(0, 0)
                one_turn(0, 0, tile_of(2), first=True, last=True)
                with pe.Fori(0, SUPER // AHEAD) as i:
                    t = tile_of(AHEAD * i + 3)
                    for u in range(AHEAD):
                        t = one_turn(AHEAD * i + u + 1, (u + 1) % AHEAD, t, last=(u == AHEAD - 1))

            @block.scalar
            def _(act):
                def turned_copy(s, n):
                    act.wait_ge(turned, s + 1)
                    act.activation(awayT[0:NP, n % 2, :], hot_ps[0:NP, 0:2, :].rearrange("p q e -> p (q e)"), ACT.Copy, bias=-FAR, scale=FAR)
                    act.copy(hotT[0:NP, n, :, :], hot_ps[0:NP, 0:2, :]).then_inc(turned_sb, 1)

                def flipped_copy(s):
                    act.wait_ge(flipped, s + 1)
                    act.copy(partsT[0:K, :], flip_ps[0:K, :]).then_inc(flipped_sb, 1)

                def scales(s, n):
                    act.wait_ge(drop_ready, s + 1)
                    act.activation(scale[0:NP, n, :], drop[0:NP, n % 2, :], ACT.Exp).then_inc(scale_ready, 1)

                def weights(s, n):
                    act.wait_ge(below_ready, s + 1)
                    act.activation(msg[:, n % 2, :, 0:W].rearrange("p q (h v) -> p q h v", h=H)[:, :, :, dv], below[:, :, :], ACT.Exp).then_inc(weight_ready, 1)

                def message_half(s, n):
                    act.wait_ge(weight_ready, s + 1)
                    if kind == "mix":
                        act.wait_ge(mixed_ready, s + 1)
                    for h in range(H):
                        a = D if kind == "dot" else 0
                        values = mixed[:, n % 2, 1, :] if kind == "mix" else rows[:, n, 1, a + h * dv:a + (h + 1) * dv]
                        at = h * (dv + 1)
                        ins = act.activation(msg[:, n % 2, 1, at:at + dv], values, ACT.Copy, scale=msg[:, n % 2, 1, at + dv:at + dv + 1])
                    ins.then_inc(half_ready, 1)

                def one_turn(s, n):
                    weights(s, n)
                    if act_half:
                        message_half(s, n)
                    flipped_copy(s + 2)
                    turned_copy(s + 3, (n + 3) % AHEAD)
                    scales(s + 1, (n + 1) % AHEAD)

                act.sem_inc(msg_ready, AHEAD)
                if act_half:
                    act.sem_inc(half_ready, AHEAD)
                turned_copy(0, 0)
                flipped_copy(0)
                turned_copy(1, 1)
                flipped_copy(1)
                turned_copy(2, 2)
                scales(0, 0)
                one_turn(0, 0)
                with act.Fori(0, SUPER // AHEAD) as i:
                    for u in range(AHEAD):
                        one_turn(AHEAD * i + u + 1, (u + 1) % AHEAD)

            @block.vector
            def _(dve):
                def one_hot(s, n):
                    dve.tensor_tensor(hot[:, n, :, :], const["ramp"][:, 0:NP].unsqueeze(1).to_broadcast([128, 2, NP]),
                                      edge["data"][:, bass.ds(2 * s, 2), 1:2].to_broadcast([128, 2, NP]), ALU.is_equal).then_inc(hot_ready, 1)

                def scores_of(s, n, nth):
                    dve.wait_ge(gathered[n], 32 * nth)
                    if kind == "dot":
                        dve.wait_ge(own_ready, s + 1)
                        dve.tensor_tensor(prod[:, :, :], own_ps[:, :, :], rows[:, n, :, 0:D], ALU.mult)
                        dve.drain()
                        dve.reduce_sum(term[:, :, :], prod[:, :, :].rearrange("p q (h e) -> p q h e", h=H), axis=AX.X)
                    elif kind == "add":
                        dve.wait_ge(own_ready, s + 1)
                        dve.tensor_tensor(term[:, :, :], own_ps[:, :, 0:H], rows[:, n, :, H * dv:H * dv + H], ALU.add)
                    else:
                        part = [edge["data"][:, bass.ds(2 * s, 2), c:c + 1].to_broadcast([128, 2, H]) for c in (2, 3)]
                        dve.tensor_tensor(prod[:, :, H:2 * H], rows[:, n, :, 2 * dv:2 * dv + H], part[0], ALU.mult)
                        dve.tensor_tensor(prod[:, :, 0:H], rows[:, n, :, 2 * dv + H:2 * dv + 2 * H], part[1], ALU.mult)
                        dve.drain()
                        dve.tensor_tensor(term[:, :, :], prod[:, :, H:2 * H], prod[:, :, 0:H], ALU.add)
                    dve.drain()
                    for to in (parts[:, :, 0, :], score[:, n, :, :]):
                        if kind == "dot":
                            ins = dve.tensor_scalar(to, term[:, :, :], scores, None, ALU.mult)
                        else:
                            ins = dve.scalar_tensor_tensor(out=to, in0=term[:, :, :], scalar=scores, in1=term[:, :, :], op0=ALU.mult, op1=ALU.max)
                    ins.then_inc(score_ready, 1)

                def raise_max(s, n, t):
                    for half in range(2):
                        a = half * HALF
                        dve.wait_ge(max_ready, 2 * s + half + 1)
                        dve.tensor_reduce(local[0:NP, a:a + HALF], max_ps[0:NP, a:a + HALF, :], AX.X, ALU.max)
                    dve.drain()
                    at = run[0:NP, bass.ds(t, 1), :].rearrange("p a h -> p (a h)")
                    dve.tensor_tensor(raised[0:NP, n % 2, :], at, local[0:NP, :], ALU.max).then_inc(new_max, 1)
                    dve.wait_ge(new_max, s + 1)
                    dve.tensor_tensor(drop[0:NP, n % 2, :], at, raised[0:NP, n % 2, :], ALU.subtract).then_inc(drop_ready, 1)
                    dve.drain()
                    dve.tensor_copy(at, raised[0:NP, n % 2, :])

                def weigh(s, n):
                    dve.wait_ge(max_back, s + 1)
                    dve.tensor_tensor(gap[:, :, :], score[:, n, :, :], back_ps[:, :, 0:H], ALU.subtract)
                    dve.drain()
                    dve.tensor_scalar(below[:, :, :], gap[:, :, :], 0.0, None, ALU.min).then_inc(below_ready, 1)
                    if kind == "mix":
                        for q in range(2):
                            dve.tensor_scalar(prod[:, q, 64:64 + dv], rows[:, n, q, 0:dv], edge["data"][:, bass.ds(2 * s + q, 1), 2], None, ALU.mult)
                        dve.drain()
                        for q in range(2):
                            ins = dve.scalar_tensor_tensor(out=mixed[:, n % 2, q, :], in0=rows[:, n, q, dv:2 * dv], scalar=edge["data"][:, bass.ds(2 * s + q, 1), 3],
                                                           in1=prod[:, q, 64:64 + dv], op0=ALU.mult, op1=ALU.add)
                        ins.then_inc(mixed_ready, 1)
                        dve.drain()

                def message(s, n):
                    dve.wait_ge(weight_ready, s + 1)
                    for q in range(1 if act_half else 2):
                        m = msg[:, n % 2, q, 0:W].rearrange("p (h v) -> p h v", h=H)
                        weight = m[:, :, dv:dv + 1].to_broadcast([128, H, dv])
                        if kind == "mix":
                            values = mixed[:, n % 2, q, :].unsqueeze(1).to_broadcast([128, H, dv])
                        else:
                            a = D if kind == "dot" else 0
                            values = rows[:, n, q, a:a + H * dv].rearrange("p (h v) -> p h v", h=H)
                        ins = dve.tensor_tensor(m[:, :, 0:dv], values, weight, ALU.mult)
                    ins.then_inc(msg_ready, 1)

                def accumulate(s, t):
                    at = acc[0:NP, bass.ds(t, 1), :].rearrange("p a w -> p (a w)")
                    dve.wait_ge(scaled_ready, s + 1)
                    dve.wait_ge(sum_ready, s + 1)
                    if count_targets:
                        dve.tensor_tensor(at[:, W:WA], at[:, W:WA], sum_ps[0:NP, W:WA], ALU.add)
                    dve.tensor_tensor(at[:, 0:W], scaled[0:NP, :], sum_ps[0:NP, 0:W], ALU.add).then_inc(accumulated, 1)

                def tile_of(s):
                    return dve.value_load(ids[0:1, bass.ds(s, 1)], min_val=0, max_val=T - 1)

                dve.sem_inc(accumulated, 1)
                if count_targets:
                    dve.memset(msg[:, :, :, W:WA], 1.0)
                dve.tensor_tensor(member[:, 0, :], const["eye"][:, 0:H], const["eye"][:, H:2 * H], ALU.add)
                dve.drain()
                dve.tensor_tensor(member[:, 1, :], member[:, 0, :], const["eye"][:, 2 * H:3 * H], ALU.add)
                dve.drain()
                dve.tensor_copy(head_rows[:, :, :], member[:, 1, :].unsqueeze(2).to_broadcast([128, H, NP])).then_inc(heads_ready, 1)
                for s in range(4):
                    one_hot(s, s)
                scores_of(0, 0, 1)
                dve.wait_ge(flipped, 1)
                scores_of(1, 1, 1)
                raise_max(0, 0, tile_of(0))
                weigh(0, 0)
                scores_of(2, 2, 1)
                raise_max(1, 1, tile_of(1))
                message(0, 0)
                with dve.Fori(0, SUPER // AHEAD) as i:
                    following = {}
                    for u in range(AHEAD):
                        s, n = AHEAD * i + u + 1, (u + 1) % AHEAD
                        following[u] = tile_of(s + 1)
                        last = following[u - 2] if u >= 2 else tile_of(s - 1)
                        weigh(s, n)
                        if QW:
                            one_hot(s + 3, (n + 3) % AHEAD)
                        scores_of(s + 2, (n + 2) % AHEAD, i + 1 + (u + 3) // AHEAD)
                        if not QW:
                            one_hot(s + 3, (n + 3) % AHEAD)
                        raise_max(s + 1, (n + 1) % AHEAD, following[u])
                        message(s, n)
                        accumulate(s - 1, last)


def sum_pass(nc, edge, table, width, acc, const, name):
    SUPER = edge["cols"] // 2
    with Scope(nc, name) as k:
        ids = edge["tile_of"]
        source, rows = k.sb("source", [128, SUM_AHEAD, 2], I32), k.sb("rows", [128, SUM_AHEAD, 2, width])
        hot = k.sb("hot", [128, SUM_AHEAD, 2, NP])
        sums = [k.ps(f"sums{n}", [128, 512]) for n in range(2)]
        gathered = [k.own_sem(f"gathered{n}") for n in range(SUM_AHEAD)]
        sources, hot_ready, sum_ready, added = (k.sem(n) for n in ("sources", "hot_ready", "sum_ready", "added"))
        with nc.Block() as block:
            @block.gpsimd
            def _(pool):
                with pool.Fori(0, SUPER // 4) as i:
                    for n in range(SUM_AHEAD):
                        pool.wait_ge(added, 4 * i + n + 1)
                        pool.tensor_copy(source[:, n, :], edge["data"][:, bass.ds(8 * i + 2 * n, 2), 0].bitcast(I32)).then_inc(sources, 1)
                        pool.wait_ge(sources, 4 * i + n + 1)
                        pool.nop(nofuse=True)
                        for q in range(2):
                            pool.indirect_dma_start(rows[:, n, q, :], None, table, bass.IndirectOffsetOnAxis(ap=source[:, n, q:q + 1], axis=0)).then_inc(gathered[n], 16)

            @block.tensor
            def _(pe):
                with pe.Fori(0, SUPER // 4) as i:
                    for n in range(SUM_AHEAD):
                        pe.wait_ge(hot_ready, 4 * i + n + 1)
                        pe.wait_ge(gathered[n], 32 * (i + 1))
                        pe.wait_ge(added, 4 * i + n + SUM_AHEAD - 1)
                        for q in range(2):
                            ins = pe.matmul(sums[n % 2][0:NP, 0:width], hot[:, n, q, :], rows[:, n, q, :], start=(q == 0), stop=(q == 1))
                        ins.then_inc(sum_ready, 1)

            @block.vector
            def _(dve):
                dve.sem_inc(added, SUM_AHEAD)

                def one_hot(s, n):
                    dve.tensor_tensor(hot[:, n, :, :], const["ramp"][:, 0:NP].unsqueeze(1).to_broadcast([128, 2, NP]),
                                      edge["data"][:, bass.ds(2 * s, 2), 1:2].to_broadcast([128, 2, NP]), ALU.is_equal).then_inc(hot_ready, 1)

                one_hot(0, 0)
                with dve.Fori(0, SUPER // 4) as i:
                    for n in range(SUM_AHEAD):
                        s = 4 * i + n
                        one_hot(s + 1, (n + 1) % SUM_AHEAD)
                        t = dve.value_load(ids[0:1, bass.ds(s, 1)], min_val=0, max_val=T - 1)
                        at = acc[0:NP, bass.ds(t, 1), :].rearrange("p a w -> p (a w)")
                        dve.wait_ge(sum_ready, s + 1)
                        dve.wait_ge(added, s + SUM_AHEAD)
                        dve.tensor_tensor(at, at, sums[n % 2][0:NP, 0:width], ALU.add).then_inc(added, 1)


CHUNKS = [(c * 500, 500) for c in range(6)] + [(3000, 125)]
TILES = [range(c * 4, min(c * 4 + 4, T)) for c in range(7)]


def flat(ap):
    return ap.rearrange("p a b -> p (a b)")


def along(row, parts):
    return row.unsqueeze(0).to_broadcast([parts] + list(row.shape))


def on_vector(nc, name, steps, loads=(), stores=(), roots=()):
    with Scope(nc, name) as k:
        asked, given = k.sem("asked"), k.sem("given")
        turn = [0]

        def root(dve):
            turn[0] += 1
            dve.drain().then_inc(asked, 1)
            dve.wait_ge(given, turn[0])

        loaded, done, stored = k.sem("loaded"), k.sem("done"), k.sem("stored")
        with nc.Block() as block:
            @block.sync
            def _(sp):
                for to, of in loads:
                    sp.dma_start(to, of).then_inc(loaded, 16)
                if stores:
                    sp.wait_ge(done, 1)
                    for to, of in stores:
                        sp.dma_start(to, of).then_inc(stored, 16)
                    sp.wait_ge(stored, 16 * len(stores))

            @block.vector
            def _(dve):
                if loads:
                    dve.wait_ge(loaded, 16 * len(loads))
                if roots:
                    steps(dve, root)
                else:
                    steps(dve)
                dve.drain().then_inc(done, 1)

            @block.scalar
            def _(act):
                for n, at in enumerate(roots):
                    act.wait_ge(asked, n + 1)
                    act.activation(at, at, ACT.Sqrt).then_inc(given, 1)


def tile_norm(nc, x, out, name, width=D, gain=None, shift=None, eps=1e-5, groups=1, add_to=None, tiles=T, square=None):
    G = groups
    with Scope(nc, name) as k:
        mean, var = k.sb("mean", [128, tiles, G]), k.sb("var", [128, tiles, G])
        if square is None:
            square = k.sb("square", [128, tiles, G * width])
        loads = []
        if gain is not None:
            g_row, b_row = k.sb("gain", [128, gain.shape[-1]]), k.sb("shift", [128, gain.shape[-1]])
            loads = [(g_row[0:NP, :], along(gain, NP)), (b_row[0:NP, :], along(shift, NP))]
        cut = [lambda a: a[0:NP, :, :].rearrange("p t (g w) -> p (t g) w", g=G)][0]
        wide = [NP, tiles * G, width]
        m, v = flat(mean[0:NP, :, :]), flat(var[0:NP, :, :])

        def steps(dve, root):
            dve.reduce_sum(m, cut(x), axis=AX.X)
            dve.drain()
            dve.tensor_scalar(m, m, 1.0 / width, None, ALU.mult)
            dve.drain()
            dve.tensor_tensor(cut(out), cut(x), m.unsqueeze(2).to_broadcast(wide), ALU.subtract)
            dve.drain()
            dve.tensor_tensor(cut(square), cut(out), cut(out), ALU.mult)
            dve.drain()
            dve.reduce_sum(v, cut(square), axis=AX.X)
            dve.drain()
            dve.tensor_scalar(v, v, 1.0 / width, eps, ALU.mult, ALU.add)
            root(dve)
            dve.reciprocal(v, v)
            dve.drain()
            dve.tensor_tensor(cut(out), cut(out), v.unsqueeze(2).to_broadcast(wide), ALU.mult)
            dve.drain()
            if gain is not None:
                if gain.shape[-1] == width and G > 1:
                    rows = [r[0:NP, :].unsqueeze(1).to_broadcast(wide) for r in (g_row, b_row)]
                    view = cut(out)
                else:
                    rows = [r[0:NP, :].unsqueeze(1).to_broadcast([NP, tiles, G * width]) for r in (g_row, b_row)]
                    view = out[0:NP, :, :]
                dve.tensor_tensor(view, view, rows[0], ALU.mult)
                dve.drain()
                dve.tensor_tensor(view, view, rows[1], ALU.add)
                dve.drain()
            if add_to is not None:
                dve.tensor_tensor(add_to[0:NP, :, :], add_to[0:NP, :, :], out[0:NP, :, :], ALU.add)

        on_vector(nc, name, steps, loads, roots=[v])


def turn_rows(nc, rows, turned, const, name, halves=2):
    with Scope(nc, name) as k:
        bank = [k.ps(f"bank{b}", [128, 4, 128]) for b in range(4)]
        made, copied = k.sem("made"), [k.sem("copied_act"), k.sem("copied_dve")]
        jobs = [(h, c) for h in range(halves) for c in range(7)]
        with nc.Block() as block:
            @block.tensor
            def _(pe):
                for n, (h, c) in enumerate(jobs):
                    if n >= 4:
                        pe.wait_ge(copied[n % 2], (n - 4) // 2 + 1)
                    for j, t in enumerate(TILES[c]):
                        ins = pe.transpose(bank[n % 4][:, j, 0:NP], rows[0:NP, t, h * 128:(h + 1) * 128], const["eye"][0:NP, 0:NP])
                    ins.then_inc(made, 1)

            def copies(eng, which, copy):
                for n, (h, c) in enumerate(jobs):
                    if n % 2 != which:
                        continue
                    eng.wait_ge(made, n + 1)
                    m = len(TILES[c])
                    copy(turned[:, h, CHUNKS[c][0]:CHUNKS[c][0] + m * NP].rearrange("p (j n) -> p j n", n=NP), bank[n % 4][:, 0:m, 0:NP]).then_inc(copied[which], 1)

            @block.scalar
            def _(act):
                copies(act, 0, act.copy)

            @block.vector
            def _(dve):
                copies(dve, 1, dve.tensor_copy)


def project(nc, parts, weights, cols, put, name, bias=None, loads=(), last=None, weights_sb=None, bias_sb=None):
    with Scope(nc, name) as k:
        K = len(parts)
        pk = parts[0].shape[0]
        w = weights_sb if weights_sb is not None else k.sb("w", [pk, K, cols])
        banks = [k.ps(f"bank{b}", [128, 512]) for b in range(4)]
        b_row = bias_sb
        if bias is not None:
            b_row = k.sb("b", [128, cols])
        loaded, made, used = k.sem("loaded"), k.sem("made"), k.sem("used")
        todo = list(loads)
        if weights is not None:
            todo.append((w[:, :, :], weights.rearrange("(k p) n -> p k n", p=pk)))
        if bias is not None:
            todo.append((b_row[0:NP, :], along(bias, NP)))
        with nc.Block() as block:
            @block.sync
            def _(sp):
                for to, of in todo:
                    sp.dma_start(to, of).then_inc(loaded, 16)

            @block.tensor
            def _(pe):
                if todo:
                    pe.wait_ge(loaded, 16 * len(todo))
                for t in range(T):
                    if t >= 4:
                        pe.wait_ge(used, t - 3)
                    for q in range(K):
                        ins = pe.matmul(banks[t % 4][0:NP, 0:cols], parts[q][:, t * NP:(t + 1) * NP], w[:, q, 0:cols], start=(q == 0), stop=(q == K - 1))
                    ins.then_inc(made, 1)

            @block.vector
            def _(dve):
                if todo:
                    dve.wait_ge(loaded, 16 * len(todo))
                for t in range(T):
                    dve.wait_ge(made, t + 1)
                    put(dve, t, banks[t % 4][0:NP, 0:cols], b_row[0:NP, 0:cols] if b_row is not None else None).then_inc(used, 1)
                if last is not None:
                    dve.drain()
                    last(dve)


def put_rows(to, add=None):
    def put(dve, t, bank, bias):
        at = to[0:NP, t, 0:bank.shape[-1]]
        if bias is not None:
            if add is None:
                return dve.tensor_tensor(at, bank, bias, ALU.add)
            dve.tensor_tensor(at, add[0:NP, t, :], bias, ALU.add)
            dve.drain()
            return dve.tensor_tensor(at, bank, at, ALU.add)
        if add is not None:
            return dve.tensor_tensor(at, bank, add[0:NP, t, :], ALU.add)
        return dve.tensor_copy(at, bank)
    return put


def perceptron(nc, parts, layers, E, func, y, name, gates=None, affine=None):
    KIN = len(parts)
    dims = [KIN * 128] + [l[0].shape[-1] for l in layers]
    hidden = len(layers) - 1
    SLOTS = 1 if E == 1 else 2
    blocks = [max(1, d // 128) for d in dims]
    size = [min(128, d) for d in dims]
    BANKS = 4
    MADE = 7 * sum(blocks[1:-1])
    with Scope(nc, name) as k:
        w = [[k.sb(f"w{l}_{s}", [size[l], blocks[l], dims[l + 1]]) for l in range(len(layers))] for s in range(SLOTS)]
        b = [[k.sb(f"b{l}_{s}", [size[l + 1], blocks[l + 1]]) for l in range(hidden)] for s in range(SLOTS)]
        b_last = [k.sb(f"b_last{s}", [128, D]) for s in range(SLOTS)]
        h = [[k.sb(f"h{l}_{c}", [size[l], blocks[l], 500]) for c in range(2)] for l in range(1, hidden + 1)]
        biased = k.sb("biased", [128, 2, D])
        own = own_gb = None
        if affine is not None:
            own = [k.sb(f"own{c}", [128, KIN, 500]) for c in range(2)]
            own_gb = [k.sb(f"own_gb{s}", [128, 2, KIN]) for s in range(SLOTS)]
        h_bank = [k.ps(f"h_bank{n}", [128, 512]) for n in range(BANKS)]
        y_bank = [k.ps(f"y_bank{n}", [128, 512]) for n in range(2)]
        loaded = [k.sem(f"loaded{s}") for s in range(SLOTS)]
        h_made, h_ready, y_made, y_free, y_added, own_ready = (k.sem(n) for n in ("h_made", "h_ready", "y_made", "y_free", "y_added", "own_ready"))
        NL = 2 * len(layers) + (2 if affine is not None else 0)
        BODY = SLOTS
        flow = [(s, c) for s in range(BODY) for c in range(7)]

        def nth_hidden(f, l, m):
            return order.index((f, l, m))

        order = []
        for f in range(len(flow)):
            for ff, l in ([(0, 1)] if f == 0 else []) + ([(f + 1, 1)] if f + 1 < len(flow) else []) + [(f, l) for l in range(2, hidden + 1)]:
                order += [(ff, l, m) for m in range(blocks[l])]

        def loop(eng, body, start=0):
            if E == 1:
                body(0)
            elif start < E // 2:
                with eng.Fori(start, E // 2) as i:
                    body(i)

        with nc.Block() as block:
            @block.sync
            def _(sp):
                def load(i, s):
                    e = i * BODY + s if E > 1 else 0
                    for l in range(len(layers)):
                        wd, bd = layers[l]
                        sp.dma_start(w[s][l][:, :, :], wd[bass.ds(e, 1), :, :].rearrange("a (k p) n -> p (a k) n", p=size[l])).then_inc(loaded[s], 16)
                        if l < hidden:
                            sp.dma_start(b[s][l][:, :], bd[bass.ds(e, 1), :, :].rearrange("a p k -> p (a k)")).then_inc(loaded[s], 16)
                        else:
                            sp.dma_start(b_last[s][0:NP, :].unsqueeze(1), bd[bass.ds(e, 1), :].unsqueeze(0).to_broadcast([NP, 1, D])).then_inc(loaded[s], 16)
                    if affine is not None:
                        for q in range(2):
                            sp.dma_start(own_gb[s][:, q, :], affine[q][bass.ds(e, 1), :, :].rearrange("a p k -> p (a k)")).then_inc(loaded[s], 16)

                for s in range(SLOTS):
                    load(0, s)

                def body(i):
                    for s in range(SLOTS):
                        sp.wait_ge(y_added, (i - 1) * BODY * T + T * (s + 1))
                        load(i, s)
                if E > 1:
                    loop(sp, body, 1)

            @block.tensor
            def _(pe):
                def make_hidden(i, f, l):
                    s, c = flow[f]
                    n0, n = CHUNKS[c]
                    for m in range(blocks[l]):
                        at = nth_hidden(f, l, m)
                        need = at + 1
                        if l > 1:
                            need = max(need, BANKS + nth_hidden(f, l - 1, blocks[l - 1] - 1) + 1)
                        pe.wait_ge(h_ready, i * MADE * BODY + need)
                        if l == 1 and m == 0 and affine is not None:
                            pe.wait_ge(own_ready, i * len(flow) + f + 1)
                        for q in range(blocks[l - 1]):
                            if l > 1:
                                of = h[l - 2][f % 2][:, q, 0:n]
                            elif affine is not None:
                                of = own[f % 2][:, q, 0:n]
                            else:
                                of = parts[q][:, n0:n0 + n]
                            ins = pe.matmul(h_bank[at % BANKS][0:size[l], 0:n], w[s][l - 1][:, q, m * 128:m * 128 + size[l]], of, start=(q == 0), stop=(q == blocks[l - 1] - 1))
                        ins.then_inc(h_made, 1)

                def body(i):
                    for f, (s, c) in enumerate(flow):
                        if c == 0:
                            pe.wait_ge(loaded[s], 16 * NL * (i + 1))
                        if f == 0:
                            make_hidden(i, 0, 1)
                        if f + 1 < len(flow):
                            if flow[f + 1][1] == 0:
                                pe.wait_ge(loaded[flow[f + 1][0]], 16 * NL * (i + 1))
                            make_hidden(i, f + 1, 1)
                        for l in range(2, hidden + 1):
                            make_hidden(i, f, l)
                        pe.wait_ge(h_ready, i * MADE * BODY + BANKS + nth_hidden(f, hidden, blocks[hidden] - 1) + 1)
                        for j, t in enumerate(TILES[c]):
                            n = s * T + t
                            pe.wait_ge(y_free, i * BODY * T + n + 1)
                            for q in range(blocks[hidden]):
                                ins = pe.matmul(y_bank[n % 2][0:NP, 0:D], h[hidden - 1][f % 2][:, q, j * NP:(j + 1) * NP], w[s][hidden][:, q, :], start=(q == 0), stop=(q == blocks[hidden] - 1))
                            ins.then_inc(y_made, 1)
                loop(pe, body)

            @block.scalar
            def _(act):
                act.sem_inc(h_ready, BANKS)

                def body(i):
                    for at, (f, l, m) in enumerate(order):
                        s, c = flow[f]
                        n = CHUNKS[c][1]
                        act.wait_ge(h_made, i * MADE * BODY + at + 1)
                        act.activation(h[l - 1][f % 2][:, m, 0:n], h_bank[at % BANKS][0:size[l], 0:n], func, bias=b[s][l - 1][:, m:m + 1]).then_inc(h_ready, 1)
                loop(act, body)

            @block.vector
            def _(dve):
                dve.sem_inc(y_free, 2)

                def own_input(i, f):
                    s, c = flow[f]
                    n0, n = CHUNKS[c]
                    for q in range(KIN):
                        ins = dve.tensor_scalar(own[f % 2][:, q, 0:n], parts[q][:, n0:n0 + n], own_gb[s][:, 0, q:q + 1], own_gb[s][:, 1, q:q + 1], ALU.mult, ALU.add)
                    ins.then_inc(own_ready, 1)

                def body(i):
                    if affine is not None:
                        dve.wait_ge(loaded[0], 16 * NL * (i + 1))
                        own_input(i, 0)
                        own_input(i, 1)
                    for f, (s, c) in enumerate(flow):
                        if c == 0:
                            dve.wait_ge(loaded[s], 16 * NL * (i + 1))
                        for t in TILES[c]:
                            n = s * T + t
                            dve.wait_ge(y_made, i * BODY * T + n + 1)
                            dve.tensor_tensor(biased[0:NP, n % 2, :], y_bank[n % 2][0:NP, 0:D], b_last[s][0:NP, :], ALU.add).then_inc(y_free, 1)
                            dve.drain()
                            to = y[0:NP, t, :]
                            if gates is not None:
                                e = i * BODY + s if E > 1 else 0
                                gate = flat(gates[0:NP, t:t + 1, bass.ds(e, 1)])
                                dve.scalar_tensor_tensor(out=to, in0=biased[0:NP, n % 2, :], scalar=gate, in1=to, op0=ALU.mult, op1=ALU.add).then_inc(y_added, 1)
                            else:
                                dve.tensor_tensor(to, to, biased[0:NP, n % 2, :], ALU.add).then_inc(y_added, 1)
                        if affine is not None and f + 2 < len(flow):
                            if flow[f + 2][1] == 0:
                                dve.wait_ge(loaded[flow[f + 2][0]], 16 * NL * (i + 1))
                            own_input(i, f + 2)
                loop(dve, body)


def gram(nc, left, right, out, name, m_cols=D, n_cols=D, extra=None):
    blocks = m_cols // 128
    with Scope(nc, name) as k:
        bank = [k.ps(f"bank{m}", [128, 512]) for m in range(blocks)]
        made = k.sem("made")
        with nc.Block() as block:
            @block.tensor
            def _(pe):
                for m in range(blocks):
                    for t in range(T):
                        ins = pe.matmul(bank[m][:, 0:n_cols], left[0:NP, t, m * 128:(m + 1) * 128], right[0:NP, t, 0:n_cols], start=(t == 0), stop=(t == T - 1 and extra is None))
                    if extra is not None:
                        ins = pe.matmul(bank[m][:, 0:n_cols], extra[0], extra[1], start=False, stop=True)
                    ins.then_inc(made, 1)

            @block.vector
            def _(dve):
                for m in range(blocks):
                    dve.wait_ge(made, m + 1)
                    dve.tensor_copy(out[:, m, 0:n_cols], bank[m][:, 0:n_cols])


def product(nc, left, right, out, name, bank_parts=128, scale=None):
    blocks = max(1, left[0].shape[-1] // 128)
    cols = right[0].shape[-1]
    rows = min(128, left[0].shape[-1])
    with Scope(nc, name) as k:
        bank = [k.ps(f"bank{m}", [128, 512]) for m in range(blocks)]
        made = k.sem("made")
        with nc.Block() as block:
            @block.tensor
            def _(pe):
                for m in range(blocks):
                    for q in range(len(left)):
                        ins = pe.matmul(bank[m][0:rows, 0:cols], left[q][:, m * 128:m * 128 + rows], right[q], start=(q == 0), stop=(q == len(left) - 1))
                    ins.then_inc(made, 1)

            @block.vector
            def _(dve):
                for m in range(blocks):
                    dve.wait_ge(made, m + 1)
                    if scale is None:
                        dve.tensor_copy(out[0:rows, m, 0:cols], bank[m][0:rows, 0:cols])
                    else:
                        dve.tensor_scalar(out[0:rows, m, 0:cols], bank[m][0:rows, 0:cols], scale, None, ALU.mult)


def keep_blocks(nc, mats, size, name, fill=0.0):
    with Scope(nc, name) as k:
        cut, cut2 = k.sem("cut"), k.sem("cut2")
        with nc.Block() as block:
            @block.gpsimd
            def _(pool):
                n = 0
                for row0, mat, cols in mats:
                    for b in range(0, cols, size):
                        v = mat[:, b:b + size]
                        pool.affine_select(out=v, in_=v, compare_op=ALU.is_ge, fill=fill, base=row0 - b, pattern=[[0, size]], channel_multiplier=1).then_inc(cut, 1)
                        n += 1
                        pool.wait_ge(cut, n)
                        pool.affine_select(out=v, in_=v, compare_op=ALU.is_ge, fill=fill, base=b + size - 1 - row0, pattern=[[0, size]], channel_multiplier=-1).then_inc(cut, 1)
                        n += 1


def top_two(dve, s, gt, eq, rank, keep, lower, E):
    wide = [NP, T, E, E]
    for t in range(T):
        mine = s[0:NP, t, :].unsqueeze(2).to_broadcast([NP, E, E])
        other = s[0:NP, t, :].unsqueeze(1).to_broadcast([NP, E, E])
        dve.tensor_tensor(gt[0:NP, t, :, :], other, mine, ALU.is_gt)
        dve.tensor_tensor(eq[0:NP, t, :, :], other, mine, ALU.is_equal)
    dve.drain()
    g, q = gt[0:NP, :, :, :].rearrange("p t e j -> p t (e j)"), eq[0:NP, :, :, :].rearrange("p t e j -> p t (e j)")
    dve.tensor_tensor(q, q, flat(lower[0:NP, :, :]).unsqueeze(1).to_broadcast([NP, T, E * E]), ALU.mult)
    dve.drain()
    dve.tensor_tensor(g, g, q, ALU.add)
    dve.drain()
    dve.reduce_sum(flat(rank[0:NP, :, :]), gt[0:NP, :, :, :].rearrange("p t e j -> p (t e) j"), axis=AX.X)
    dve.drain()
    dve.tensor_scalar(keep[0:NP, :, :], rank[0:NP, :, :], 2.0, None, ALU.is_lt)
    dve.drain()


def on_scalar(nc, name, steps):
    with nc.Block() as block:
        @block.scalar
        def _(act):
            steps(act)


def fill(nc, pairs):
    with nc.Block() as block:
        @block.vector
        def _(dve):
            for to, value in pairs:
                dve.memset(to, value)


def finish_heads(nc, acc, H, dv, out, name, eps=0.0, eps_rows=None):
    with Scope(nc, name) as k:
        inverse = k.sb("inverse", [128, T, H])

        def steps(dve):
            heads = acc[0:NP, :, 0:H * (dv + 1)].rearrange("p t (h v) -> p t h v", h=H)
            if eps_rows is None:
                dve.tensor_scalar(inverse[0:NP, :, :], heads[:, :, :, dv], eps, None, ALU.add)
            else:
                dve.tensor_tensor(inverse[0:NP, :, :], heads[:, :, :, dv], eps_rows[0:NP, :, :], ALU.add)
            dve.drain()
            dve.reciprocal(inverse[0:NP, :, :], inverse[0:NP, :, :])
            dve.drain()
            for t in range(T):
                dve.tensor_tensor(out[0:NP, t, 0:H * dv].rearrange("p (h v) -> p h v", h=H), heads[:, t, :, 0:dv], inverse[0:NP, t, :].unsqueeze(2).to_broadcast([NP, H, dv]), ALU.mult)

        on_vector(nc, name, steps)


def start_with_self(dve, acc, run, values, own, H, dv, tmp, slope=0.2):
    dve.scalar_tensor_tensor(out=run[0:NP, :, :], in0=own, scalar=slope, in1=own, op0=ALU.mult, op1=ALU.max)
    for t in range(T):
        at = acc[0:NP, t, 0:H * (dv + 1)].rearrange("p (h v) -> p h v", h=H)
        dve.tensor_copy(at[:, :, 0:dv], values[0:NP, t, 0:H * dv].rearrange("p (h v) -> p h v", h=H))
        dve.memset(at[:, :, dv:dv + 1], 1.0)


def add_rows(nc, to, of, name, also=None):
    def steps(dve):
        dve.tensor_tensor(to[0:NP, :, :], to[0:NP, :, :], of[0:NP, :, :], ALU.add)
        if also is not None:
            dve.drain()
            dve.tensor_tensor(to[0:NP, :, :], to[0:NP, :, :], also[0:NP, :, :], ALU.add)
    on_vector(nc, name, steps)


def table_rows(table):
    return table.rearrange("(t p) w -> p t w", p=NP)


def softmax_of(nc, s, E, name, keep=None, normal=True):
    with Scope(nc, name) as k:
        top = k.sb("top", [128, T])
        wide = [NP, T, E]

        def before(dve):
            dve.tensor_reduce(top[0:NP, :], s[0:NP, :, :], AX.X, ALU.max)
            dve.drain()
            dve.tensor_tensor(s[0:NP, :, :], s[0:NP, :, :], top[0:NP, :].unsqueeze(2).to_broadcast(wide), ALU.subtract)

        def after(dve):
            if keep is not None:
                dve.tensor_tensor(s[0:NP, :, :], s[0:NP, :, :], keep[0:NP, :, :], ALU.mult)
                dve.drain()
            normalise(dve, s, top, E)

        on_vector(nc, name + "_b", before)
        on_scalar(nc, name + "_e", lambda act: act.activation(s[0:NP, :, :], s[0:NP, :, :], ACT.Exp))
        on_vector(nc, name + "_a", after)


def normalise(dve, s, total, E):
    dve.reduce_sum(total[0:NP, :], s[0:NP, :, :], axis=AX.X)
    dve.drain()
    dve.reciprocal(total[0:NP, :], total[0:NP, :])
    dve.drain()
    dve.tensor_tensor(s[0:NP, :, :], s[0:NP, :, :], total[0:NP, :].unsqueeze(2).to_broadcast([NP, T, E]), ALU.mult)


def choose_two(nc, s, keep, lower, E, name):
    with Scope(nc, name) as k:
        gt, eq, rank = k.sb("gt", [128, T, E, E]), k.sb("eq", [128, T, E, E]), k.sb("rank", [128, T, E])
        on_vector(nc, name, lambda dve: top_two(dve, s, gt, eq, rank, keep, lower, E))


def node_norm(nc, x, square, gain, shift, const, name):
    with Scope(nc, name) as k:
        bank = [k.ps("bank0", [128, 512]), k.ps("bank1", [128, 512])]
        mean, rstd = k.sb("mean", [128, D]), k.sb("rstd", [128, D])
        g_row, b_row = k.sb("g", [128, D]), k.sb("b", [128, D])
        loaded, squared, summed = k.sem("loaded"), k.sem("squared"), k.sem("summed")
        asked, given = k.sem("asked"), k.sem("given")
        wide = [NP, T, D]
        with nc.Block() as block:
            @block.sync
            def _(sp):
                sp.dma_start(g_row[0:NP, :], along(gain, NP)).then_inc(loaded, 16)
                sp.dma_start(b_row[0:NP, :], along(shift, NP)).then_inc(loaded, 16)

            @block.tensor
            def _(pe):
                for n, of in enumerate((x, square)):
                    if n:
                        pe.wait_ge(squared, 1)
                    for t in range(T):
                        ins = pe.matmul(bank[n][0:NP, 0:D], const["ones"][0:NP, 0:NP], of[0:NP, t, :], start=(t == 0), stop=(t == T - 1))
                    ins.then_inc(summed, 1)

            @block.scalar
            def _(act):
                act.wait_ge(asked, 1)
                act.activation(rstd[0:NP, :], rstd[0:NP, :], ACT.Sqrt).then_inc(given, 1)

            @block.vector
            def _(dve):
                dve.wait_ge(summed, 1)
                dve.tensor_scalar(mean[0:NP, :], bank[0][0:NP, 0:D], 1.0 / N, None, ALU.mult)
                dve.drain()
                dve.tensor_tensor(x[0:NP, :, :], x[0:NP, :, :], mean[0:NP, :].unsqueeze(1).to_broadcast(wide), ALU.subtract)
                dve.drain()
                dve.tensor_tensor(square[0:NP, :, :], x[0:NP, :, :], x[0:NP, :, :], ALU.mult).then_inc(squared, 1)
                dve.wait_ge(summed, 2)
                dve.tensor_scalar(rstd[0:NP, :], bank[1][0:NP, 0:D], 1.0 / N, 1e-5, ALU.mult, ALU.add).then_inc(asked, 1)
                dve.wait_ge(given, 1)
                dve.reciprocal(rstd[0:NP, :], rstd[0:NP, :])
                dve.drain()
                dve.wait_ge(loaded, 32)
                dve.tensor_tensor(rstd[0:NP, :], rstd[0:NP, :], g_row[0:NP, :], ALU.mult)
                dve.drain()
                dve.tensor_tensor(x[0:NP, :, :], x[0:NP, :, :], rstd[0:NP, :].unsqueeze(1).to_broadcast(wide), ALU.mult)
                dve.drain()
                dve.tensor_tensor(x[0:NP, :, :], x[0:NP, :, :], b_row[0:NP, :].unsqueeze(1).to_broadcast(wide), ALU.add)


def rms_norm(nc, x, out, gain, name):
    with Scope(nc, name) as k:
        total, g_row = k.sb("total", [128, T]), k.sb("g", [128, D])

        def steps(dve, root):
            dve.tensor_tensor(out[0:NP, :, :], x[0:NP, :, :], x[0:NP, :, :], ALU.mult)
            dve.drain()
            dve.reduce_sum(total[0:NP, :], out[0:NP, :, :], axis=AX.X)
            dve.drain()
            dve.tensor_scalar(total[0:NP, :], total[0:NP, :], 1e-24, None, ALU.max)
            root(dve)
            dve.reciprocal(total[0:NP, :], total[0:NP, :])
            dve.drain()
            dve.tensor_scalar(total[0:NP, :], total[0:NP, :], float(D) ** 0.5, None, ALU.mult)
            dve.drain()
            dve.tensor_tensor(out[0:NP, :, :], x[0:NP, :, :], total[0:NP, :].unsqueeze(2).to_broadcast([NP, T, D]), ALU.mult)
            dve.drain()
            dve.tensor_tensor(out[0:NP, :, :], out[0:NP, :, :], g_row[0:NP, :].unsqueeze(1).to_broadcast([NP, T, D]), ALU.mult)

        on_vector(nc, name, steps, [(g_row[0:NP, :], along(gain, NP))], roots=[total[0:NP, :]])


def halves(xt):
    return [xt[:, 0, :], xt[:, 1, :]]


def experts(nc, xt, weights, E, func, y, name, **more):
    perceptron(nc, halves(xt) if not isinstance(xt, list) else xt, weights, E, func, y, name, **more)


def layer0_graph(nc, I, X, inv_deg, edge, const):
    with Scope(nc, "a") as k:
        A, Q = k.sb("A", [128, T, D]), k.sb("Q", [128, T, D])
        keys_values = nc.dram_tensor("a_table", (N, 2 * D), F32, kind="Internal").ap()
        tile_norm(nc, X, A, "a_norm")
        with Scope(nc, "a1") as j:
            XT = j.sb("XT", [128, 2, N])
            turn_rows(nc, A, XT, const, "a_turn")
            with Scope(nc, "am") as m:
                K, V = m.sb("K", [128, T, D]), m.sb("V", [128, T, D])
                VK, P1, P2 = m.sb("VK", [128, 2, D]), m.sb("P1", [128, 2, D]), m.sb("P2", [128, 2, D])
                wo, wq = m.sb("wo", [128, 2, D]), m.sb("wq", [128, 2, D])
                loads = [(wo[:, :, :], I["L0_mix_woT"].rearrange("(k p) n -> p k n", p=128)), (wq[:, :, :], I["L0_mix_wq"].rearrange("(k p) n -> p k n", p=128))]
                project(nc, halves(XT), I["L0_mix_wkT"], D, put_rows(K), "am_k", loads=loads)
                project(nc, halves(XT), I["L0_mix_wvT"], D, put_rows(V), "am_v")
                tile_norm(nc, K, K, "am_nk", width=64, groups=4, gain=I["L0_mix_ln_k_g"], shift=I["L0_mix_ln_k_b"], square=Q)
                tile_norm(nc, V, V, "am_nv", width=64, groups=4, gain=I["L0_mix_ln_v_g"], shift=I["L0_mix_ln_v_b"], square=Q)
                gram(nc, V, K, VK, "am_g")
                keep_blocks(nc, [(0, VK[:, 0, :], D), (128, VK[:, 1, :], D)], 64, "am_b")
                product(nc, halves(VK), halves(wo), P1, "am_p", scale=1.0 / N)
                product(nc, halves(wq), halves(P1), P2, "am_q")
                project(nc, halves(XT), None, D, put_rows(X, add=X), "am_x", bias=I["L0_mix_bo"], weights_sb=P2)
            project(nc, halves(XT), I["L0_gnn_Wq"], D, put_rows(Q), "a_q")
            with Scope(nc, "a2") as m:
                KV = m.sb("KV", [128, T, 2 * D])
                project(nc, halves(XT), I["L0_gnn_Wkv"], 2 * D, put_rows(KV), "a_kv")
                on_vector(nc, "a_store", lambda dve: None, stores=[(table_rows(keys_values), KV[0:NP, :, :])])
        with Scope(nc, "a3") as j:
            acc, run = j.sb("acc", [128, T, 8 * 33 + 1]), j.sb("run", [128, T, 8])
            fill(nc, [(acc[:, :, :], 0.0), (run[:, :, :], 0.0)])
            edge_pass(nc, edge, keys_values, "dot", 8, 32, 2 * D, Q, 32 ** -0.5, dict(acc=acc, m=run), const, "ae")
            finish_heads(nc, acc, 8, 32, Q, "a_fin", eps=1e-8)

            def degrees(dve, root):
                dve.tensor_scalar(inv_deg[0:NP, :], acc[0:NP, :, 264], 1.0, None, ALU.add)
                root(dve)
                dve.reciprocal(inv_deg[0:NP, :], inv_deg[0:NP, :])
            on_vector(nc, "a_deg", degrees, roots=[inv_deg[0:NP, :]])
        B = Q
        with Scope(nc, "a4") as j:
            XT = j.sb("XT", [128, 2, N])
            turn_rows(nc, B, XT, const, "a_turn2")
            project(nc, halves(XT), I["L0_gnn_Wo_w"], D, put_rows(B, add=A), "a_o", bias=I["L0_gnn_Wo_b"])
            tile_norm(nc, B, B, "a_n1", gain=I["L0_gnn_ln1_g"], shift=I["L0_gnn_ln1_b"])
            turn_rows(nc, B, XT, const, "a_turn3")
            experts(nc, XT, [(I["L0_gnn_ffn_w1"], I["L0_gnn_ffn_b1"]), (I["L0_gnn_ffn_w2"], I["L0_gnn_ffn_b2"])], 1, ACT.Gelu, B, "a_mlp")
            tile_norm(nc, B, B, "a_n2", gain=I["L0_gnn_ln2_g"], shift=I["L0_gnn_ln2_b"], add_to=X)


def layer0_experts(nc, I, X, edge, const, lower):
    with Scope(nc, "b") as k:
        XT, gates = k.sb("XT", [128, 2, N]), k.sb("gates", [128, T, 4])
        table = nc.dram_tensor("b_table", (N, 20), F32, kind="Internal").ap()
        with Scope(nc, "b1") as j:
            A = j.sb("A", [128, T, D])
            tile_norm(nc, X, A, "b_norm")
            turn_rows(nc, A, XT, const, "b_turn")
        with Scope(nc, "b2") as j:
            h, a_dst, own = j.sb("h", [128, T, 20]), j.sb("a_dst", [128, T, 4]), j.sb("own", [128, T, 4])
            acc, run, agg = j.sb("acc", [128, T, 20]), j.sb("run", [128, T, 4]), j.sb("agg", [128, T, 16])
            tmp = j.sb("tmp", [128, T, 16])
            att = j.sb("att", [128, 3, 16])
            keep = j.sb("keep", [128, T, 4])
            project(nc, halves(XT), I["L0_ffn_W_gat"], 16, put_rows(h), "b_h", loads=[(att[0:NP, n, :], along(I[v], NP)) for n, v in enumerate(("L0_ffn_att_src", "L0_ffn_att_dst", "L0_ffn_b_gat"))])

            def attention(dve):
                for n, to in enumerate((h[0:NP, :, 16:20], a_dst[0:NP, :, :])):
                    dve.tensor_tensor(tmp[0:NP, :, :], h[0:NP, :, 0:16], att[0:NP, n, :].unsqueeze(1).to_broadcast([NP, T, 16]), ALU.mult)
                    dve.drain()
                    dve.reduce_sum(to, tmp[0:NP, :, :].rearrange("p t (h e) -> p t h e", h=4), axis=AX.X)
                    dve.drain()
                dve.tensor_tensor(own[0:NP, :, :], h[0:NP, :, 16:20], a_dst[0:NP, :, :], ALU.add)
                dve.drain()
                start_with_self(dve, acc, run, h, own[0:NP, :, :], 4, 4, tmp)
            on_vector(nc, "b_att", attention, stores=[(table_rows(table), h[0:NP, :, :])])
            edge_pass(nc, edge, table, "add", 4, 4, 20, a_dst, 0.2, dict(acc=acc, m=run), const, "be")
            finish_heads(nc, acc, 4, 4, agg, "b_fin", eps=1e-16)
            on_vector(nc, "b_bias", lambda dve: dve.tensor_tensor(agg[0:NP, :, :], agg[0:NP, :, :], att[0:NP, 2, :].unsqueeze(1).to_broadcast([NP, T, 16]), ALU.add))
            tile_norm(nc, agg, agg, "b_n", width=16, gain=I["L0_ffn_ln_gamma"], shift=I["L0_ffn_ln_beta"])

            def score(dve):
                dve.reduce_sum(gates[0:NP, :, :], agg[0:NP, :, :].rearrange("p t (h e) -> p t e h", h=4), axis=AX.X)
                dve.drain()
                dve.tensor_scalar(gates[0:NP, :, :], gates[0:NP, :, :], 0.25, None, ALU.mult)
            on_vector(nc, "b_score", score)
            choose_two(nc, gates, keep, lower[4], 4, "b_two")
            softmax_of(nc, gates, 4, "b_soft", keep=keep)
        experts(nc, XT, [(I["L0_ffn_W1"], I["L0_ffn_b1"]), (I["L0_ffn_W2"], I["L0_ffn_b2"])], 4, ACT.Gelu, X, "b_mlp", gates=gates)


def elu_plus_one(nc, x, e, parts, name):
    cut = [a[0:parts, :, :] for a in (x, e)]
    on_vector(nc, name + "_a", lambda dve: dve.tensor_scalar(cut[1], cut[0], 0.0, None, ALU.min))
    on_scalar(nc, name + "_b", lambda act: act.activation(cut[1], cut[1], ACT.Exp))
    on_vector(nc, name + "_c", lambda dve: dve.scalar_tensor_tensor(out=cut[0], in0=cut[0], scalar=0.0, in1=cut[1], op0=ALU.max, op1=ALU.add))


def layer1_graph(nc, I, X, inv_deg, edge, const):
    with Scope(nc, "c") as k:
        XT = k.sb("XT", [128, 2, N])
        table = nc.dram_tensor("c_table", (N, D), F32, kind="Internal").ap()
        with Scope(nc, "c1") as j:
            A, acc = j.sb("A", [128, T, D]), j.sb("acc", [128, T, D])
            b_row = j.sb("b", [128, D])
            tile_norm(nc, X, A, "c_norm")
            turn_rows(nc, A, XT, const, "c_turn")
            project(nc, halves(XT), I["L1_gnn_WT"], D, lambda dve, t, bank, bias: dve.tensor_scalar(acc[0:NP, t, :], bank, inv_deg[0:NP, t:t + 1], None, ALU.mult), "c_h")
            on_vector(nc, "c_store", lambda dve: None, stores=[(table_rows(table), acc[0:NP, :, :])])
            sum_pass(nc, edge, table, D, acc, const, "ce")

            def close(dve):
                dve.tensor_tensor(acc[0:NP, :, :], acc[0:NP, :, :], inv_deg[0:NP, :].unsqueeze(2).to_broadcast([NP, T, D]), ALU.mult)
                dve.drain()
                dve.tensor_tensor(acc[0:NP, :, :], acc[0:NP, :, :], b_row[0:NP, :].unsqueeze(1).to_broadcast([NP, T, D]), ALU.add)
                dve.drain()
                dve.scalar_tensor_tensor(out=X[0:NP, :, :], in0=acc[0:NP, :, :], scalar=0.0, in1=X[0:NP, :, :], op0=ALU.max, op1=ALU.add)
                dve.drain()
                dve.tensor_tensor(X[0:NP, :, :], X[0:NP, :, :], A[0:NP, :, :], ALU.add)
            on_vector(nc, "c_close", close, [(b_row[0:NP, :], along(I["L1_gnn_b"], NP))])
        B, QT = k.sb("B", [128, T, D]), k.sb("QT", [128, 2, N])
        with Scope(nc, "c2") as j:
            V, G = j.sb("V", [128, T, D + 1]), j.sb("G", [128, 2, 264])
            with Scope(nc, "c3") as m:
                E = m.sb("E", [128, T, D])
                project(nc, halves(XT), I["L1_mix_Wq"], D, put_rows(B), "c_q")
                elu_plus_one(nc, B, E, NP, "c_eq")
                turn_rows(nc, B, QT, const, "c_tq")
                project(nc, halves(XT), I["L1_mix_Wk"], D, put_rows(B), "c_k")
                elu_plus_one(nc, B, E, NP, "c_ek")
                project(nc, halves(XT), I["L1_mix_Wv"], D, put_rows(V), "c_v")
                fill(nc, [(V[:, :, D:D + 1], 1.0)])
            gram(nc, B, V, G, "c_g", n_cols=D + 1)

            def denominators(dve):
                for m in range(2):
                    dve.tensor_copy(G[:, m, D + 1:264], G[:, m, D:D + 1].to_broadcast([128, 7]))
            on_vector(nc, "c_d", denominators)
            keep_blocks(nc, [(0, G[:, 0, :], D), (128, G[:, 1, :], D)], 32, "c_b")
            keep_head_columns(nc, G, 32, 8, D, "c_hc")
            inv = j.sb("inv", [128, 2, 8])

            def put(dve, t, bank, bias):
                dve.tensor_scalar(inv[0:NP, t % 2, :], bank[:, D:264], 1e-6, None, ALU.add)
                dve.drain()
                dve.reciprocal(inv[0:NP, t % 2, :], inv[0:NP, t % 2, :])
                dve.drain()
                return dve.tensor_tensor(B[0:NP, t, :].rearrange("p (h v) -> p h v", h=8), bank[:, 0:D].rearrange("p (h v) -> p h v", h=8), inv[0:NP, t % 2, :].unsqueeze(2).to_broadcast([NP, 8, 32]), ALU.mult)
            project(nc, halves(QT), None, 264, put, "c_m", weights_sb=G)
        turn_rows(nc, B, QT, const, "c_tm")
        project(nc, halves(QT), I["L1_mix_Wm"], D, put_rows(B), "c_wm")
        tile_norm(nc, B, B, "c_n1", gain=I["L1_mix_g1"], shift=I["L1_mix_b1"])
        turn_rows(nc, B, QT, const, "c_tn")
        fill(nc, [(B[:, :, :], 0.0)])
        experts(nc, halves(XT) + halves(QT), [(I["L1_mix_W1"], I["zeros512"]), (I["L1_mix_W2"], I["zeros256"])], 1, ACT.Relu, B, "c_mlp")
        tile_norm(nc, B, B, "c_n2", gain=I["L1_mix_g2"], shift=I["L1_mix_b2"], add_to=X)


def keep_head_columns(nc, mat, size, heads, col0, name):
    with Scope(nc, name) as k:
        cut = k.sem("cut")
        with nc.Block() as block:
            @block.gpsimd
            def _(pool):
                n = 0
                for m in range(2):
                    v = mat[:, m, col0:col0 + heads]
                    pool.affine_select(out=v, in_=v, compare_op=ALU.is_ge, fill=0.0, base=m * 128, pattern=[[-size, heads]], channel_multiplier=1).then_inc(cut, 1)
                    n += 1
                    pool.wait_ge(cut, n)
                    pool.affine_select(out=v, in_=v, compare_op=ALU.is_ge, fill=0.0, base=size - 1 - m * 128, pattern=[[size, heads]], channel_multiplier=-1).then_inc(cut, 1)
                    n += 1


def layer1_experts(nc, I, X, const, lower):
    with Scope(nc, "d") as k:
        XT, gates = k.sb("XT", [128, 2, N]), k.sb("gates", [128, T, 4])
        with Scope(nc, "d1") as j:
            A, keep = j.sb("A", [128, T, D]), j.sb("keep", [128, T, 4])
            tile_norm(nc, X, A, "d_norm")
            turn_rows(nc, A, XT, const, "d_turn")
            project(nc, halves(XT), I["L1_ffn_gW"], 4, put_rows(gates), "d_g", bias=I["L1_ffn_gb"])
            softmax_of(nc, gates, 4, "d_s1")
            choose_two(nc, gates, keep, lower[4], 4, "d_two")
            softmax_of(nc, gates, 4, "d_s2", keep=keep)
        experts(nc, XT, [(I["L1_ffn_sW1"], I["L1_ffn_sb1"]), (I["L1_ffn_sW2"], I["L1_ffn_sb2"]), (I["L1_ffn_sW3"], I["L1_ffn_sb3"])], 1, ACT.Relu, X, "d_shared")
        experts(nc, XT, [(I["L1_ffn_eW1"], I["L1_ffn_eb1"]), (I["L1_ffn_eW2"], I["L1_ffn_eb2"]), (I["L1_ffn_eW3"], I["L1_ffn_eb3"])], 4, ACT.Relu, X, "d_own", gates=gates)


def layer2_graph(nc, I, X, edge, const):
    with Scope(nc, "e") as k:
        XT = k.sb("XT", [128, 2, N])
        A = k.sb("A", [128, T, D])
        table = nc.dram_tensor("e_table", (N, 136), F32, kind="Internal").ap()
        tile_norm(nc, X, A, "e_norm")
        turn_rows(nc, A, XT, const, "e_turn")
        with Scope(nc, "e1") as j:
            W, f, r = j.sb("W", [128, 2, 136]), j.sb("f", [128, 2, 4]), j.sb("r", [128, 2, 4])
            wf, wr, at = j.sb("wf", [64, D]), j.sb("wr", [64, D]), j.sb("at", [64, 4])
            rows = j.sb("rows", [128, T, 136])
            on_vector(nc, "e_load", lambda dve: None, loads=[(wf[:, :], I["L2_gnn_W_forward"]), (wr[:, :], I["L2_gnn_W_reverse"]), (at[:, :], I["L2_gnn_attnT"]),
                                                         (W[:, :, 0:64], I["L2_gnn_WfT"].rearrange("(k p) n -> p k n", p=128)), (W[:, :, 64:128], I["L2_gnn_WrT"].rearrange("(k p) n -> p k n", p=128))])
            product(nc, [wf[:, :]], [at[:, :]], f, "e_f")
            product(nc, [wr[:, :]], [at[:, :]], r, "e_r")

            def columns(dve):
                dve.tensor_copy(W[:, :, 128:132], f[:, :, :])
                dve.tensor_copy(W[:, :, 132:136], r[:, :, :])
            on_vector(nc, "e_c", columns)
            project(nc, halves(XT), None, 136, put_rows(rows), "e_p", weights_sb=W)
            on_vector(nc, "e_store", lambda dve: None, stores=[(table_rows(table), rows[0:NP, :, :])])
        with Scope(nc, "e2") as j:
            acc, run, top = j.sb("acc", [128, T, 4 * 65]), j.sb("run", [128, T, 4]), j.sb("top", [128, 4])
            res = j.sb("res", [128, T, D])
            fill(nc, [(acc[:, :, :], 0.0), (run[:, :, :], -FAR)])
            edge_pass(nc, edge, table, "mix", 4, 64, 136, None, 0.2, dict(acc=acc, m=run), const, "ee")
            every_max(nc, run, top, const, "e_max")

            def relative(dve):
                dve.tensor_tensor(run[0:NP, :, :], top[0:NP, :].unsqueeze(1).to_broadcast([NP, T, 4]), run[0:NP, :, :], ALU.subtract)
                dve.drain()
                dve.tensor_scalar(run[0:NP, :, :], run[0:NP, :, :], 80.0, None, ALU.min)
            on_vector(nc, "e_rel", relative)
            on_scalar(nc, "e_exp", lambda act: act.activation(run[0:NP, :, :], run[0:NP, :, :], ACT.Exp))
            on_vector(nc, "e_eps", lambda dve: dve.tensor_scalar(run[0:NP, :, :], run[0:NP, :, :], 1e-10, None, ALU.mult))
            finish_heads(nc, acc, 4, 64, res, "e_fin", eps_rows=run)
            add_rows(nc, X, res, "e_add")
        B, C = k.sb("B", [128, T, D]), k.sb("C", [128, T, D])
        with Scope(nc, "e3") as j:
            G, PT, M = j.sb("G", [128, 2, D]), j.sb("PT", [128, 2, D]), j.sb("M", [128, 2, D])
            wq, bq, bq_wide, bq_row = j.sb("wq", [128, 2, D]), j.sb("bq", [128, 2]), j.sb("bq_wide", [128, 2, 128]), j.sb("bq_row", [128, 1, D])
            top, total = j.sb("top", [128, 2]), j.sb("total", [128, 2])
            project(nc, halves(XT), I["L2_mix_wk"], D, put_rows(B), "e_k", bias=I["L2_mix_bk"],
                    loads=[(wq[:, :, :], I["L2_mix_wqT"].rearrange("(k p) n -> p k n", p=128)), (bq[:, :], I["L2_mix_bq"])])
            project(nc, halves(XT), I["L2_mix_wv"], D, put_rows(C), "e_v", bias=I["L2_mix_bv"])
            gram(nc, B, C, G, "e_g")
            on_vector(nc, "e_sc", lambda dve: dve.tensor_scalar(G[:, :, :], G[:, :, :], 64 ** -0.5, None, ALU.mult))
            keep_blocks(nc, [(0, G[:, 0, :], D), (128, G[:, 1, :], D)], 64, "e_b", fill=-FAR)

            def less_top(dve):
                dve.tensor_reduce(top[:, :], G[:, :, :], AX.X, ALU.max)
                dve.memset(PT[:, :, :], 0.0)
                dve.drain()
                dve.tensor_tensor(G[:, :, :], G[:, :, :], top[:, :].unsqueeze(2).to_broadcast([128, 2, D]), ALU.subtract)
                for m in range(2):
                    dve.tensor_copy(bq_wide[:, m, :], bq[:, m:m + 1].to_broadcast([128, 128]))
            on_vector(nc, "e_s1", less_top)
            on_scalar(nc, "e_s2", lambda act: act.activation(G[:, :, :], G[:, :, :], ACT.Exp))

            def shares(dve):
                dve.reduce_sum(total[:, :], G[:, :, :], axis=AX.X)
                dve.drain()
                dve.reciprocal(total[:, :], total[:, :])
                dve.drain()
                dve.tensor_tensor(G[:, :, :], G[:, :, :], total[:, :].unsqueeze(2).to_broadcast([128, 2, D]), ALU.mult)
            on_vector(nc, "e_s3", shares)
            turn_blocks(nc, [(G[:, m, m * 128:(m + 1) * 128], PT[:, m, m * 128:(m + 1) * 128]) for m in range(2)], const, "e_t")
            product(nc, halves(wq), halves(PT), M, "e_m")
            product(nc, [bq_wide[:, m, 0:NP] for m in range(2)], halves(PT), bq_row, "e_bq")
            project(nc, halves(XT), None, D, put_rows(B, add=A), "e_x", weights_sb=M, bias_sb=bq_row[:, 0, :])
            tile_norm(nc, B, C, "e_n", gain=I["L2_mix_norm_g"], shift=I["L2_mix_norm_b"], square=A)
        turn_rows(nc, C, XT, const, "e_turn2")
        experts(nc, XT, [(I["L2_mix_w_fc1"], I["L2_mix_b_fc1"]), (I["L2_mix_w_fc2"], I["L2_mix_b_fc2"])], 1, ACT.Gelu, B, "e_mlp")
        add_rows(nc, X, B, "e_add2")


def turn_blocks(nc, pairs, const, name):
    with Scope(nc, name) as k:
        banks = [k.ps(f"bank{n}", [128, 512]) for n in range(len(pairs))]
        made = k.sem("made")
        with nc.Block() as block:
            @block.tensor
            def _(pe):
                for n, (of, to) in enumerate(pairs):
                    p, c = of.shape
                    pe.transpose(banks[n][0:c, 0:p], of, const["eye"][0:p, 0:p]).then_inc(made, 1)

            @block.vector
            def _(dve):
                for n, (of, to) in enumerate(pairs):
                    p, c = of.shape
                    dve.wait_ge(made, n + 1)
                    dve.tensor_copy(to, banks[n][0:c, 0:p])


def every_max(nc, run, top, const, name):
    with Scope(nc, name) as k:
        mine, turned, wide = k.sb("mine", [128, 4]), k.sb("turned", [4, 1]), k.sb("wide", [4, 128])
        b0, b1 = k.ps("b0", [128, 512]), k.ps("b1", [128, 512])
        first, across, second, back = (k.sem(n) for n in ("first", "across", "second", "back"))
        with nc.Block() as block:
            @block.tensor
            def _(pe):
                pe.wait_ge(first, 1)
                pe.transpose(b0[0:4, 0:NP], mine[0:NP, :], const["eye"][0:NP, 0:NP]).then_inc(across, 1)
                pe.wait_ge(second, 1)
                pe.matmul(b1[0:NP, 0:4], wide[:, 0:NP], const["eye"][0:4, 0:4], start=True, stop=True).then_inc(back, 1)

            @block.vector
            def _(dve):
                dve.tensor_reduce(mine[0:NP, :], run[0:NP, :, :].rearrange("p t h -> p h t"), AX.X, ALU.max).then_inc(first, 1)
                dve.wait_ge(across, 1)
                dve.tensor_reduce(turned[:, :], b0[0:4, 0:NP], AX.X, ALU.max)
                dve.drain()
                dve.tensor_copy(wide[:, :], turned[:, :].to_broadcast([4, 128])).then_inc(second, 1)
                dve.wait_ge(back, 1)
                dve.tensor_copy(top[0:NP, :], b1[0:NP, 0:4])


def layer2_experts(nc, I, X, const, lower):
    with Scope(nc, "f") as k:
        XT, gates = k.sb("XT", [128, 2, N]), k.sb("gates", [128, T, 8])
        with Scope(nc, "f1") as j:
            A, keep, total = j.sb("A", [128, T, D]), j.sb("keep", [128, T, 8]), j.sb("total", [128, T])
            tile_norm(nc, X, A, "f_norm")
            turn_rows(nc, A, XT, const, "f_turn")
            project(nc, halves(XT), I["L2_ffn_Wr"], 8, put_rows(gates), "f_g", bias=I["L2_ffn_br"])
            softmax_of(nc, gates, 8, "f_s")
            choose_two(nc, gates, keep, lower[8], 8, "f_two")

            def shares(dve):
                dve.tensor_tensor(gates[0:NP, :, :], gates[0:NP, :, :], keep[0:NP, :, :], ALU.mult)
                dve.drain()
                normalise(dve, gates, total, 8)
            on_vector(nc, "f_sh", shares)
            tile_norm(nc, A, A, "f_norm2")
            turn_rows(nc, A, XT, const, "f_turn2")
        experts(nc, XT, [(I["L2_ffn_W1"], I["L2_ffn_b1"]), (I["L2_ffn_W2"], I["L2_ffn_b2"])], 8, ACT.Gelu, X, "f_mlp", gates=gates, affine=(I["L2_ffn_ln_g"], I["L2_ffn_ln_b"]))


def layer3_graph(nc, I, X, edge, const):
    with Scope(nc, "g") as k:
        A, B = k.sb("A", [128, T, D]), k.sb("B", [128, T, D])
        table = nc.dram_tensor("g_table", (N, 264), F32, kind="Internal").ap()
        tile_norm(nc, X, A, "g_norm")
        with Scope(nc, "g1") as j:
            s, own, acc, run = j.sb("s", [128, T, 8]), j.sb("own", [128, T, 8]), j.sb("acc", [128, T, 264]), j.sb("run", [128, T, 8])
            with Scope(nc, "g2") as m:
                XT, VS = m.sb("XT", [128, 2, N]), m.sb("VS", [128, T, 264])
                turn_rows(nc, A, XT, const, "g_turn")
                project(nc, halves(XT), I["L3_gnn_Wq"], D, put_rows(B), "g_q", bias=I["L3_gnn_bq"])
                project(nc, halves(XT), I["L3_gnn_Wk"], D, lambda dve, t, bank, bias: key_row(dve, VS, t, bank, bias), "g_k", bias=I["L3_gnn_bk"])

                def scores(dve):
                    dve.tensor_tensor(B[0:NP, :, :], B[0:NP, :, :], VS[0:NP, :, 0:D], ALU.mult)
                    dve.drain()
                    dve.reduce_sum(s[0:NP, :, :], B[0:NP, :, :].rearrange("p t (h e) -> p t h e", h=8), axis=AX.X)
                    dve.drain()
                    dve.tensor_scalar(s[0:NP, :, :], s[0:NP, :, :], 32 ** -0.5, None, ALU.mult)
                    dve.drain()
                    dve.tensor_scalar(own[0:NP, :, :], s[0:NP, :, :], 2.0, None, ALU.mult)
                    dve.tensor_copy(VS[0:NP, :, D:264], s[0:NP, :, :])
                on_vector(nc, "g_s", scores)
                project(nc, halves(XT), I["L3_gnn_Wv"], D, put_rows(VS), "g_v", bias=I["L3_gnn_bv"])
                on_vector(nc, "g_st", lambda dve: start_with_self(dve, acc, run, VS, own[0:NP, :, :], 8, 32, None), stores=[(table_rows(table), VS[0:NP, :, :])])
            edge_pass(nc, edge, table, "add", 8, 32, 264, s, 0.2, dict(acc=acc, m=run), const, "ge")
            finish_heads(nc, acc, 8, 32, B, "g_fin")
        with Scope(nc, "g3") as j:
            XT, C = j.sb("XT", [128, 2, N]), j.sb("C", [128, T, D])
            turn_rows(nc, B, XT, const, "g_turn2")
            project(nc, halves(XT), I["L3_gnn_Wo"], D, put_rows(B, add=A), "g_o", bias=I["L3_gnn_bo"])
            node_norm(nc, B, C, I["L3_gnn_bn1_g"], I["L3_gnn_bn1_b"], const, "g_bn1")
            turn_rows(nc, B, XT, const, "g_turn3")
            experts(nc, XT, [(I["L3_gnn_W1"], I["L3_gnn_b1"]), (I["L3_gnn_W2"], I["L3_gnn_b2"])], 1, ACT.Relu, B, "g_mlp")
            node_norm(nc, B, C, I["L3_gnn_bn2_g"], I["L3_gnn_bn2_b"], const, "g_bn2")
            add_rows(nc, X, B, "g_add", also=A)
        with Scope(nc, "g4") as j:
            XT = j.sb("XT", [128, 2, N])
            rms_norm(nc, A, B, I["L3_mix_g_pre"], "g_rms")
            turn_rows(nc, B, XT, const, "g_turn4")
            q, kv = j.sb("q", [128, T, 128]), j.sb("kv", [128, T, 257])

            def put(dve, t, bank, bias):
                dve.tensor_copy(q[0:NP, t, :], bank[:, 0:128])
                return dve.tensor_copy(kv[0:NP, t, 0:256], bank[:, 128:384])
            project(nc, halves(XT), I["L3_mix_w_qkv"], 384, put, "g_qkv")
            fill(nc, [(kv[:, :, 256:257], 1.0)])
            mem_k, mem_v, mem_kT = j.sb("mem_k", [128, 4]), j.sb("mem_v", [4, 129]), j.sb("mem_kT", [4, 128])
            G, GT, M2, w_out = j.sb("G", [128, 1, 129]), j.sb("GT", [128, 128]), j.sb("M2", [128, 1, D]), j.sb("w_out", [128, D])
            top_q, cols = j.sb("top_q", [128, T * 4]), j.sb("cols", [128, 128])
            top_k, top_wide, top_row, inv = j.sb("top_k", [128, 1]), j.sb("top_wide", [128, 128]), j.sb("top_row", [128, 1, 128]), j.sb("inv", [128, 1])
            turned = j.sb("turned", [128, 128])
            q4 = q[0:NP, :, :].rearrange("p t (h e) -> p (t h) e", h=4)
            heads = [NP, T * 4, 32]

            def tops(dve):
                dve.memset(mem_v[:, 128:129], 1.0)
                dve.tensor_reduce(top_q[0:NP, :], q4, AX.X, ALU.max)
                dve.tensor_reduce(cols[0:NP, :], kv[0:NP, :, 0:128].rearrange("p t d -> p d t"), AX.X, ALU.max)
                dve.drain()
                dve.tensor_tensor(q4, q4, top_q[0:NP, :].unsqueeze(2).to_broadcast(heads), ALU.subtract)
            on_vector(nc, "g_m1", tops, loads=[(mem_k[:, :], I["L3_mem_k"]), (mem_v[:, 0:128], I["L3_mem_vT"]), (w_out[:, :], I["L3_mix_w_out"])])
            turn_blocks(nc, [(cols[0:NP, :], turned[:, 0:NP])], const, "g_m2")

            def key_top(dve):
                dve.memset(turned[:, NP:128], -FAR)
                dve.drain()
                dve.tensor_copy(turned[:, NP:NP + 1], mem_k[:, 0:1])
                dve.tensor_copy(turned[:, NP + 1:128], mem_k[:, 1:3])
                dve.drain()
                dve.tensor_reduce(top_k[:, :], turned[:, :], AX.X, ALU.max)
                dve.drain()
                dve.tensor_tensor(top_k[:, :], top_k[:, :], mem_k[:, 3:4], ALU.max)
                dve.drain()
                dve.tensor_copy(top_wide[:, :], top_k[:, :].to_broadcast([128, 128]))
                dve.tensor_tensor(mem_k[:, :], mem_k[:, :], top_k[:, :].to_broadcast([128, 4]), ALU.subtract)
            on_vector(nc, "g_m3", key_top)
            product(nc, [top_wide[:, :]], [const["eye"][:, :]], top_row, "g_m4")
            on_vector(nc, "g_m5", lambda dve: dve.tensor_tensor(kv[0:NP, :, 0:128], kv[0:NP, :, 0:128], top_row[0:NP, :, :].to_broadcast([NP, T, 128]), ALU.subtract))

            def exps(act):
                act.activation(q4, q4, ACT.Exp)
                act.activation(kv[0:NP, :, 0:128], kv[0:NP, :, 0:128], ACT.Exp)
                act.activation(mem_k[:, :], mem_k[:, :], ACT.Exp)
            on_scalar(nc, "g_m6", exps)

            def query_shares(dve):
                dve.reduce_sum(top_q[0:NP, :], q4, axis=AX.X)
                dve.drain()
                dve.reciprocal(top_q[0:NP, :], top_q[0:NP, :])
                dve.drain()
                dve.tensor_tensor(q4, q4, top_q[0:NP, :].unsqueeze(2).to_broadcast(heads), ALU.mult)
            on_vector(nc, "g_m7", query_shares)
            turn_blocks(nc, [(mem_k[:, :], mem_kT[:, :])], const, "g_m8")
            gram(nc, kv, kv[:, :, 128:257], G, "g_gram", m_cols=128, n_cols=129, extra=(mem_kT[:, :], mem_v[:, :]))

            def context(dve):
                dve.reciprocal(inv[:, :], G[:, 0, 128:129])
                dve.drain()
                dve.tensor_scalar(G[:, 0, 0:128], G[:, 0, 0:128], inv[:, 0:1], 32 ** -0.5, ALU.mult, ALU.mult)
            on_vector(nc, "g_m9", context)
            keep_blocks(nc, [(0, G[:, 0, :], 128)], 32, "g_kb")
            turn_blocks(nc, [(G[:, 0, 0:128], GT[:, :])], const, "g_m10")
            product(nc, [GT[:, :]], [w_out[:, :]], M2, "g_m11")
            turn_rows(nc, q, XT, const, "g_turn5", halves=1)
            project(nc, [XT[:, 0, :]], None, D, put_rows(B), "g_out", weights_sb=M2, bias=I["L3_mix_b_out"])
            rms_norm(nc, B, A, I["L3_mix_g_out"], "g_rms2")
            add_rows(nc, X, A, "g_add2")


def key_row(dve, to, t, bank, bias):
    return dve.tensor_tensor(to[0:NP, t, 0:D], bank, bias, ALU.add)


def layer3_tokens(nc, I, X, const):
    KEEP = max(1, N // 2) - 1
    with Scope(nc, "h") as k:
        XT, gates = k.sb("XT", [128, 2, N]), k.sb("gates", [128, T, 1])
        stored_w = nc.dram_tensor("h_w", (N, 1), F32, kind="Internal").ap()
        with Scope(nc, "h1") as j:
            A = j.sb("A", [128, T, D])
            tile_norm(nc, X, A, "h_norm")
            turn_rows(nc, A, XT, const, "h_turn")
            add_rows(nc, X, A, "h_add")
            w = j.sb("w", [128, 2, 1])
            project(nc, halves(XT), None, 1, put_rows(gates), "h_w", bias=I["L3_ffn_br"], weights_sb=w, loads=[(w[:, :, :].rearrange("p k n -> p (k n)"), I["L3_ffn_wr"])])
            with nc.allow_non_contiguous_dma(reason="one weight per node, 12.5 KB in all"):
                on_vector(nc, "h_st", lambda dve: None, stores=[(table_rows(stored_w), gates[0:NP, :, :])])
        with Scope(nc, "h2") as j:
            every, index, before, same = (j.sb(n, [128, N]) for n in ("every", "index", "before", "same"))
            whole, mine_i = j.sb("whole", [128, N], I32), j.sb("mine_i", [128, T], I32)
            mine, more, ties = j.sb("mine", [128, T]), j.sb("more", [128, T]), j.sb("ties", [128, T])
            counted = j.sem("counted")
            with nc.Block() as block:
                @block.gpsimd
                def _(pool):
                    pool.iota(whole[:, :], pattern=[[1, N]], base=0, channel_multiplier=0)
                    pool.iota(mine_i[:, :], pattern=[[NP, T]], base=0, channel_multiplier=1)

            def rank(dve):
                dve.tensor_copy(index[:, :], whole[:, :])
                dve.tensor_copy(mine[:, :], mine_i[:, :])
                dve.drain()
                for t in range(T):
                    w = gates[0:NP, t, :]
                    dve.tensor_scalar(same[0:NP, :], every[0:NP, :], w, 0.0, ALU.is_gt, ALU.add, accum_out=more[0:NP, t:t + 1])
                    dve.tensor_scalar(before[0:NP, :], index[0:NP, :], mine[0:NP, t:t + 1], None, ALU.is_lt)
                    dve.drain()
                    dve.scalar_tensor_tensor(out=same[0:NP, :], in0=every[0:NP, :], scalar=w, in1=before[0:NP, :], op0=ALU.is_equal, op1=ALU.mult)
                    dve.drain()
                    dve.reduce_sum(ties[0:NP, t:t + 1], same[0:NP, :], axis=AX.X)
                    dve.drain()
                dve.tensor_tensor(more[0:NP, :], more[0:NP, :], ties[0:NP, :], ALU.add)
                dve.drain()
                dve.tensor_scalar(more[0:NP, :], more[0:NP, :], float(KEEP), None, ALU.is_lt)
                dve.drain()
                dve.tensor_tensor(flat(gates[0:NP, :, :]), flat(gates[0:NP, :, :]), more[0:NP, :], ALU.mult)
            on_vector(nc, "h_rank", rank, loads=[(every[0:NP, :], along(stored_w.rearrange("n a -> (n a)"), NP))])
        experts(nc, XT, [(I["L3_ffn_w1"], I["L3_ffn_b1"]), (I["L3_ffn_w2"], I["L3_ffn_b2"])], 1, ACT.Gelu_apprx_tanh, X, "h_mlp", gates=gates)


E_MAIN, COLS_MAIN, J_MAIN = 100000, 840, 784
E_GAT, COLS_GAT, J_GAT = 65536, 576, 512


def program(nc, I, out):
    with Scope(nc, "net") as k:
        const = dict(eye=k.sb("eye", [128, 128]), ones=k.sb("ones", [128, 128]), before=k.sb("before", [128, 128]),
                     ramp=k.sb("ramp", [128, 128]), eye4_bf=k.sb("eye4_bf", [128, 512], BF16))
        lower = {4: k.sb("lower4", [128, 4, 4]), 8: k.sb("lower8", [128, 8, 8])}
        X, inv_deg = k.sb("X", [128, T, D]), k.sb("inv_deg", [128, T])
        main = dict(data=k.sb("main_data", [128, COLS_MAIN + 8, 4]), tile_of=k.sb("main_tile", [128, COLS_MAIN // 2 + 3], I32), cols=COLS_MAIN)
        gat = dict(data=k.sb("gat_data", [128, COLS_GAT + 8, 4]), tile_of=k.sb("gat_tile", [128, COLS_GAT // 2 + 3], I32), cols=COLS_GAT)
        constants(nc, const)
        cut = k.sem("lower_cut")
        with nc.Block() as block:
            @block.gpsimd
            def _(pool):
                for n, E in enumerate((4, 8)):
                    pool.memset(lower[E][:, :, :], 1.0).then_inc(cut, 1)
                    pool.wait_ge(cut, n + 1)
                    pool.affine_select(out=lower[E][:, :, :], in_=lower[E][:, :, :], compare_op=ALU.is_gt, fill=0.0, base=0, pattern=[[1, E], [-1, E]], channel_multiplier=0)
        on_vector(nc, "x_in", lambda dve: None, loads=[(X[0:NP, :, :], table_rows(I["x"]))])
        rows_main = nc.dram_tensor("edges_main", (128 * COLS_MAIN + 128 * J_MAIN, 4), F32, kind="Internal").ap()
        rows_gat = nc.dram_tensor("edges_gat", (128 * COLS_GAT + 128 * J_GAT, 4), F32, kind="Internal").ap()
        group_edges(nc, main, I["src"], I["dst"], I["edge_attr_2"], E_MAIN, J_MAIN, const, rows_main, "em")
        group_edges(nc, gat, I["gat_src"], I["gat_dst"], None, E_GAT, J_GAT, const, rows_gat, "eg")
        stages = [lambda: layer0_graph(nc, I, X, inv_deg, main, const), lambda: layer0_experts(nc, I, X, gat, const, lower),
                  lambda: layer1_graph(nc, I, X, inv_deg, main, const), lambda: layer1_experts(nc, I, X, const, lower),
                  lambda: layer2_graph(nc, I, X, main, const), lambda: layer2_experts(nc, I, X, const, lower),
                  lambda: layer3_graph(nc, I, X, main, const), lambda: layer3_tokens(nc, I, X, const)]
        for stage in stages:
            stage()
        on_vector(nc, "x_out", lambda dve: None, stores=[(table_rows(out), X[0:NP, :, :])])


def layouts(a):
    import numpy as np

    a = dict(a)
    for name in ("L0_gnn_ffn_w1", "L0_gnn_ffn_w2", "L0_gnn_ffn_b1", "L0_gnn_ffn_b2", "L1_mix_W1", "L1_mix_W2", "L1_ffn_sW1", "L1_ffn_sW2", "L1_ffn_sW3",
                 "L1_ffn_sb1", "L1_ffn_sb2", "L1_ffn_sb3", "L2_mix_w_fc1", "L2_mix_w_fc2", "L2_mix_b_fc1", "L2_mix_b_fc2", "L3_gnn_W1", "L3_gnn_W2",
                 "L3_gnn_b1", "L3_gnn_b2", "L3_ffn_w1", "L3_ffn_w2", "L3_ffn_b1", "L3_ffn_b2"):
        a[name] = a[name][None]
    for name in ("wk", "wv", "wo"):
        a[f"L0_mix_{name}T"] = a.pop(f"L0_mix_{name}").T
    a["L0_gnn_Wkv"] = np.concatenate([a.pop("L0_gnn_Wk"), a.pop("L0_gnn_Wv")], axis=1)
    a["L0_ffn_att_src"], a["L0_ffn_att_dst"] = a["L0_ffn_att_src"].reshape(-1), a["L0_ffn_att_dst"].reshape(-1)
    a["gat_src"], a["gat_dst"] = a["L0_ffn_edge_index"][0], a["L0_ffn_edge_index"][1]
    del a["L0_ffn_edge_index"]
    a["L1_gnn_WT"] = a.pop("L1_gnn_W").T
    a["zeros512"], a["zeros256"] = np.zeros((1, 512), np.float32), np.zeros((1, 256), np.float32)
    a["L2_gnn_WfT"], a["L2_gnn_WrT"] = a["L2_gnn_W_forward"].T, a["L2_gnn_W_reverse"].T
    a["L2_gnn_attnT"] = a.pop("L2_gnn_attn_forward")[0].T
    w, b = a.pop("L2_mix_w_qkv"), a.pop("L2_mix_b_qkv")
    a["L2_mix_wqT"], a["L2_mix_wk"], a["L2_mix_wv"] = w[:, 0:256].T, w[:, 256:512], w[:, 512:768]
    a["L2_mix_bq"], a["L2_mix_bk"], a["L2_mix_bv"] = b[0:256], b[256:512], b[512:768]
    mem = a.pop("L3_mix_mem_kv")
    a["L3_ffn_wr"] = a["L3_ffn_wr"].reshape(2, 128).T
    a["L3_mem_k"], a["L3_mem_vT"] = mem[0].reshape(128, 4), mem[1].reshape(128, 4).T
    for name in ("L0_gnn_ffn_b1", "L0_ffn_b1", "zeros512", "L1_ffn_sb1", "L1_ffn_sb2", "L1_ffn_eb1", "L1_ffn_eb2", "L2_mix_b_fc1", "L2_ffn_b1", "L2_ffn_ln_g",
                 "L2_ffn_ln_b", "L3_gnn_b1", "L3_ffn_b1"):
        E, n = a[name].shape
        a[name] = a[name].reshape(E, max(1, n // 128), min(128, n)).transpose(0, 2, 1)
    a["L2_mix_bq"] = a["L2_mix_bq"].reshape(2, 128).T
    return {name: np.ascontiguousarray(v) for name, v in a.items()}


def kernel(**inputs):
    import numpy as _np
    import concourse.bacc as _bacc
    from concourse import mybir as _mybir
    from concourse.bass_utils import run_bass_kernel_spmd as _run

    nc = _bacc.Bacc("TRN2", target_bir_lowering=False, num_devices=1)
    arrays, args = {}, {}
    given = {name: _np.asarray(v) for name, v in inputs.items() if name not in ("L3_mix_t", "L3_ffn_attention_mask")}
    for name, a in layouts(given).items():
        arrays[f"in_{name}_dram"] = a
        args[name] = nc.dram_tensor(f"in_{name}_dram", a.shape, _mybir.dt.from_np(a.dtype), kind="ExternalInput").ap()
    out = nc.dram_tensor("out_0_dram", (N, D), F32, kind="ExternalOutput").ap()
    program(nc, args, out)
    r = _run(nc, [arrays], core_ids=[0])
    return r.results[0]["out_0_dram"]
```
